# Optimizing a Trainium2 kernel written in Bass

```python
import numpy as np
import jax
import jax.numpy as jnp

def _softmax(x, axis=-1):
    return jax.nn.softmax(x, axis=axis)

def _gelu(x):
    return jax.nn.gelu(x, approximate=True)

def _silu(x):
    return jax.nn.silu(x)

def _sigmoid(x):
    return jax.nn.sigmoid(x)

def _layernorm(x, axis=-1, eps=1e-05):
    m = jnp.mean(x, axis=axis, keepdims=True)
    v = jnp.var(x, axis=axis, keepdims=True)
    return (x - m) / jnp.sqrt(v + eps)

def _scatter_add(tgt, idx, src, axis=0):
    return tgt.at[idx].add(src)

def _segment_sum(src, seg, n):
    return jax.ops.segment_sum(src, seg, n)
kernel_name = 'mk_decoder_postln_d2_seqx_r8_53f4fe'

def setup_inputs(seed: int=0):
    np.random.seed(seed)
    _w = jnp.asarray

    def _rec_inputs():
        import jax
        import jax.numpy as jnp
        _rk = jax.random.key(seed)
        x = -0.0002928 + 1 * jax.random.normal(jax.random.fold_in(_rk, 1), (32, 128, 128), jnp.float32)
        _lenS = 128 - jax.random.randint(jax.random.fold_in(_rk, 7), (32,), 0, max(1, 128 // 4) + 1, jnp.int32)
        _lenS2 = 128 - jax.random.randint(jax.random.fold_in(_rk, 8), (32,), 0, max(1, 128 // 4) + 1, jnp.int32)
        _ctx_1024P = jax.random.normal(jax.random.fold_in(_rk, 11), (32, 16, 128), jnp.float32)
        _ctx_1024c = jax.random.dirichlet(jax.random.fold_in(_rk, 511), 0.3 * jnp.ones((16,), jnp.float32), (32, 128))
        _ctx_1024t = jnp.einsum('bsk,bkd->bsd', _ctx_1024c, _ctx_1024P)
        _ctx_1024t = _ctx_1024t * jax.lax.rsqrt(jnp.mean(jnp.square(_ctx_1024t)) + 1e-12) * 0.953939
        ctx_1024 = -1.39393e-06 + 0.999914 * (_ctx_1024t + 0.3 * jax.random.normal(jax.random.fold_in(_rk, 611), (32, 128, 128), jnp.float32))
        fside_1x1xSxS2_0 = 0.000675642 + 1.00031 * jax.random.normal(jax.random.fold_in(_rk, 12), (1, 1, 128, 128), jnp.float32)
        return (x, ctx_1024, fside_1x1xSxS2_0)
    x, ctx_1024, fside_1x1xSxS2_0 = _rec_inputs()

    def _L0_attn_setup():
        import jax, jax.numpy as jnp
        import numpy as np
        import math
        H = 128
        S = 16
        K = 4
        INNER = 2 * H
        BATCH, L = (2, 512)

        def _linrec_combine(c1, c2):
            a1, b1 = c1
            a2, b2 = c2
            return (a1 * a2, a2 * b1 + b2)
        key = jax.random.key(seed)
        ks = jax.random.split(key, 8)
        x = jax.random.normal(ks[0], (BATCH, L, H), dtype=jnp.float32)
        W_in = jax.random.normal(ks[1], (2 * INNER, H), dtype=jnp.float32) * 0.02
        conv_w = jax.random.normal(ks[2], (INNER, 1, K), dtype=jnp.float32) * 0.1
        conv_b = jnp.zeros((INNER,), dtype=jnp.float32)
        W_x = jax.random.normal(ks[3], (2 * S + INNER, INNER), dtype=jnp.float32) * 0.02
        W_dt = jax.random.normal(ks[4], (INNER, INNER), dtype=jnp.float32) * 0.02
        u = jax.random.uniform(ks[5], (INNER,), dtype=jnp.float32)
        b_dt = jnp.exp(u * (math.log(0.1) - math.log(0.001)) + math.log(0.001))
        A_log = jnp.log(jnp.broadcast_to(jnp.arange(1, S + 1, dtype=jnp.float32), (INNER, S)))
        D = jnp.ones((INNER,), dtype=jnp.float32)
        W_out = jax.random.normal(ks[6], (H, INNER), dtype=jnp.float32) * 0.02
        return {'x': x, 'W_in': W_in, 'conv_w': conv_w, 'conv_b': conv_b, 'W_x': W_x, 'W_dt': W_dt, 'b_dt': b_dt, 'A_log': A_log, 'D': D, 'W_out': W_out}
    _L0_attn_all = _L0_attn_setup()
    _L0_attn_in = {k: v for k, v in _L0_attn_all.items() if k in ('W_in', 'conv_w', 'conv_b', 'W_x', 'W_dt', 'b_dt', 'A_log', 'D', 'W_out')}
    del _L0_attn_all

    def _L0_xattn_setup():
        import jax, jax.numpy as jnp
        import numpy as np
        D_MODEL = 128
        N_HEAD = 16
        D_KEY = 64
        D_VALUE = 64

        def _split_heads(x, n_head, d_head):
            B, S, _ = x.shape
            return x.reshape(B, S, n_head, d_head).transpose(0, 2, 1, 3)
        key = jax.random.key(seed)
        ks = jax.random.split(key, 8)
        B, S = (2, 256)
        queries = jax.random.normal(ks[0], (B, S, D_MODEL), dtype=jnp.float32)
        keys = jax.random.normal(ks[1], (B, S, D_MODEL), dtype=jnp.float32)
        values = jax.random.normal(ks[2], (B, S, D_MODEL), dtype=jnp.float32)
        attn_bias = jax.random.normal(ks[3], (1, 1, S, S), dtype=jnp.float32)
        s = 1.0 / np.sqrt(D_MODEL)
        Wq = jax.random.normal(ks[4], (N_HEAD * D_KEY, D_MODEL), dtype=jnp.float32) * s
        Wk = jax.random.normal(ks[5], (N_HEAD * D_KEY, D_MODEL), dtype=jnp.float32) * s
        Wv = jax.random.normal(ks[6], (N_HEAD * D_VALUE, D_MODEL), dtype=jnp.float32) * s
        Wp = jax.random.normal(ks[7], (D_MODEL, N_HEAD * D_VALUE), dtype=jnp.float32) * s
        return {'queries': queries, 'keys': keys, 'values': values, 'attn_bias': attn_bias, 'Wq': Wq, 'Wk': Wk, 'Wv': Wv, 'Wp': Wp}
    _L0_xattn_all = _L0_xattn_setup()
    _L0_xattn_in = {k: v for k, v in _L0_xattn_all.items() if k in ('Wq', 'Wk', 'Wv', 'Wp')}
    del _L0_xattn_all

    def _L0_ffn_setup():
        import math
        import jax, jax.numpy as jnp
        import numpy as np
        B, S, D, F, E = (8, 256, 128, 512, 8)
        CAPACITY_FACTOR = 1.0
        key = jax.random.key(seed)
        k1, k2, k3, k4 = jax.random.split(key, 4)
        x = jax.random.normal(k1, (B, S, D), dtype=jnp.float32)
        Wr = jax.random.normal(k2, (D, E), dtype=jnp.float32) * (1.0 / math.sqrt(D))
        W1 = jax.random.normal(k3, (E, D, F), dtype=jnp.float32) * (1.0 / math.sqrt(D))
        W2 = jax.random.normal(k4, (E, F, D), dtype=jnp.float32) * (1.0 / math.sqrt(F))
        return {'x': x, 'Wr': Wr, 'W1': W1, 'W2': W2}
    _L0_ffn_all = _L0_ffn_setup()
    _L0_ffn_in = {k: v for k, v in _L0_ffn_all.items() if k in ('Wr', 'W1', 'W2')}
    del _L0_ffn_all

    def _L1_attn_setup():
        import math
        import jax, jax.numpy as jnp
        import numpy as np
        SEQ, BATCH, D_MODEL, NHEAD, FEAT = (256, 2, 128, 8, 128)

        def _sinusoid_pe(length, d_model, dtype):
            pos = jnp.arange(length, dtype=dtype)[:, None]
            div = jnp.exp(jnp.arange(0, d_model, 2, dtype=dtype) * (-math.log(10000.0) / d_model))
            ang = pos * div
            return jnp.stack([jnp.sin(ang), jnp.cos(ang)], axis=-1).reshape(length, d_model)

        def _left_shift(x):
            I, J, B, N = x.shape
            zero = jnp.zeros((I, 1, B, N), x.dtype)
            padded = jnp.concatenate([zero, x], axis=1)
            padded = padded.reshape(J + 1, I, B, N)[1:]
            x = padded.reshape(I, J, B, N)
            return jnp.tril(x)
        key = jax.random.key(seed)
        ks = jax.random.split(key, 8)
        s = 0.02
        return {'x': jax.random.normal(ks[0], (SEQ, BATCH, D_MODEL), dtype=jnp.float32), 'gamma': jnp.ones((D_MODEL,), jnp.float32), 'beta': jnp.zeros((D_MODEL,), jnp.float32), 'Wq': jax.random.normal(ks[1], (D_MODEL, NHEAD * FEAT), jnp.float32) * s, 'Wv': jax.random.normal(ks[2], (D_MODEL, NHEAD * FEAT), jnp.float32) * s, 'Wr': jax.random.normal(ks[3], (D_MODEL, NHEAD * FEAT), jnp.float32) * s, 'u_bias': jax.random.normal(ks[4], (NHEAD, FEAT), jnp.float32) * s, 'v_bias': jax.random.normal(ks[5], (NHEAD, FEAT), jnp.float32) * s, 'Wout': jax.random.normal(ks[6], (NHEAD * FEAT, D_MODEL), jnp.float32) * s, 'bout': jnp.zeros((D_MODEL,), jnp.float32)}
    _L1_attn_all = _L1_attn_setup()
    _L1_attn_in = {k: v for k, v in _L1_attn_all.items() if k in ('gamma', 'beta', 'Wq', 'Wv', 'Wr', 'u_bias', 'v_bias', 'Wout', 'bout')}
    del _L1_attn_all

    def _L1_xattn_setup():
        import jax, jax.numpy as jnp
        import numpy as np
        N_HEADS, D_MODEL, DK, DV = (16, 128, 64, 64)
        B, S = (4, 256)
        key = jax.random.key(seed)
        ks = jax.random.split(key, 7)
        scale = 1.0 / np.sqrt(D_MODEL)
        return {'Q': jax.random.normal(ks[0], (B, S, D_MODEL), dtype=jnp.float32), 'K': jax.random.normal(ks[1], (B, S, D_MODEL), dtype=jnp.float32), 'V': jax.random.normal(ks[2], (B, S, D_MODEL), dtype=jnp.float32), 'w_q': jax.random.normal(ks[3], (D_MODEL, N_HEADS * DK), dtype=jnp.float32) * scale, 'w_k': jax.random.normal(ks[4], (D_MODEL, N_HEADS * DK), dtype=jnp.float32) * scale, 'w_v': jax.random.normal(ks[5], (D_MODEL, N_HEADS * DV), dtype=jnp.float32) * scale, 'w_o': jax.random.normal(ks[6], (N_HEADS * DV, D_MODEL), dtype=jnp.float32) * scale}
    _L1_xattn_all = _L1_xattn_setup()
    _L1_xattn_in = {k: v for k, v in _L1_xattn_all.items() if k in ('w_q', 'w_k', 'w_v', 'w_o')}
    del _L1_xattn_all

    def _L1_ffn_setup():
        import jax, jax.numpy as jnp
        import numpy as np
        B, S, H, E = (2, 1024, 128, 8)
        SCALE = 0.5
        key = jax.random.key(seed)
        k1, k2 = jax.random.split(key)
        x = jax.random.normal(k1, (B, S, H), dtype=jnp.float32)
        gate_w = jax.random.normal(k2, (E, H), dtype=jnp.float32) * 0.02
        coeff = SCALE * (1.0 + 0.05 * jnp.arange(E, dtype=jnp.float32))
        expert_w = coeff[:, None, None] * jnp.eye(H, dtype=jnp.float32)
        return {'x': x, 'gate_w': gate_w, 'expert_w': expert_w}
    _L1_ffn_all = _L1_ffn_setup()
    _L1_ffn_in = {k: v for k, v in _L1_ffn_all.items() if k in ('gate_w', 'expert_w')}
    del _L1_ffn_all
    return {'x': x, 'ctx_1024': ctx_1024, 'fside_1x1xSxS2_0': fside_1x1xSxS2_0, 'L0_attn_W_in': _L0_attn_in['W_in'], 'L0_attn_conv_w': _L0_attn_in['conv_w'], 'L0_attn_conv_b': _L0_attn_in['conv_b'], 'L0_attn_W_x': _L0_attn_in['W_x'], 'L0_attn_W_dt': _L0_attn_in['W_dt'], 'L0_attn_b_dt': _L0_attn_in['b_dt'], 'L0_attn_A_log': _L0_attn_in['A_log'], 'L0_attn_D': _L0_attn_in['D'], 'L0_attn_W_out': _L0_attn_in['W_out'], 'L0_xattn_Wq': _L0_xattn_in['Wq'], 'L0_xattn_Wk': _L0_xattn_in['Wk'], 'L0_xattn_Wv': _L0_xattn_in['Wv'], 'L0_xattn_Wp': _L0_xattn_in['Wp'], 'L0_ffn_Wr': _L0_ffn_in['Wr'], 'L0_ffn_W1': _L0_ffn_in['W1'], 'L0_ffn_W2': _L0_ffn_in['W2'], 'L1_attn_gamma': _L1_attn_in['gamma'], 'L1_attn_beta': _L1_attn_in['beta'], 'L1_attn_Wq': _L1_attn_in['Wq'], 'L1_attn_Wv': _L1_attn_in['Wv'], 'L1_attn_Wr': _L1_attn_in['Wr'], 'L1_attn_u_bias': _L1_attn_in['u_bias'], 'L1_attn_v_bias': _L1_attn_in['v_bias'], 'L1_attn_Wout': _L1_attn_in['Wout'], 'L1_attn_bout': _L1_attn_in['bout'], 'L1_xattn_w_q': _L1_xattn_in['w_q'], 'L1_xattn_w_k': _L1_xattn_in['w_k'], 'L1_xattn_w_v': _L1_xattn_in['w_v'], 'L1_xattn_w_o': _L1_xattn_in['w_o'], 'L1_ffn_gate_w': _L1_ffn_in['gate_w'], 'L1_ffn_expert_w': _L1_ffn_in['expert_w']}

def reference(x, ctx_1024, fside_1x1xSxS2_0, L0_attn_W_in, L0_attn_conv_w, L0_attn_conv_b, L0_attn_W_x, L0_attn_W_dt, L0_attn_b_dt, L0_attn_A_log, L0_attn_D, L0_attn_W_out, L0_xattn_Wq, L0_xattn_Wk, L0_xattn_Wv, L0_xattn_Wp, L0_ffn_Wr, L0_ffn_W1, L0_ffn_W2, L1_attn_gamma, L1_attn_beta, L1_attn_Wq, L1_attn_Wv, L1_attn_Wr, L1_attn_u_bias, L1_attn_v_bias, L1_attn_Wout, L1_attn_bout, L1_xattn_w_q, L1_xattn_w_k, L1_xattn_w_v, L1_xattn_w_o, L1_ffn_gate_w, L1_ffn_expert_w):
    import jax
    import jax.numpy as jnp

    def _L0_attn_ref(x, W_in, conv_w, conv_b, W_x, W_dt, b_dt, A_log, D, W_out):
        import jax, jax.numpy as jnp
        import numpy as np
        import math
        H = 128
        S = 16
        K = 4
        INNER = 2 * H
        BATCH, L = (2, 512)

        def _linrec_combine(c1, c2):
            a1, b1 = c1
            a2, b2 = c2
            return (a1 * a2, a2 * b1 + b2)
        xz = jnp.einsum('blh,ih->bli', x, W_in)
        x_proj, z = jnp.split(xz, 2, axis=-1)
        xc = jnp.transpose(x_proj, (0, 2, 1))
        xc = jax.lax.conv_general_dilated(xc, conv_w, window_strides=(1,), padding=[(K - 1, 0)], dimension_numbers=('NCH', 'OIH', 'NCH'), feature_group_count=INNER)
        xc = xc + conv_b[None, :, None]
        x_conv = jax.nn.silu(jnp.transpose(xc, (0, 2, 1)))
        x_ssm = jnp.einsum('bli,oi->blo', x_conv, W_x)
        Bm = x_ssm[..., :S]
        Cm = x_ssm[..., S:2 * S]
        dt_in = x_ssm[..., 2 * S:]
        dt = jax.nn.softplus(jnp.einsum('bli,oi->blo', dt_in, W_dt) + b_dt)
        alpha = jax.nn.sigmoid(dt * 0.1)
        B_gate = jax.nn.sigmoid(jnp.mean(Bm, axis=-1, keepdims=True))
        gated = (1.0 - alpha) * B_gate * x_conv
        alpha_c = jnp.clip(alpha, 0.01, 0.99)
        _, h = jax.lax.associative_scan(_linrec_combine, (alpha_c, gated), axis=1)
        C_gate = jax.nn.sigmoid(jnp.mean(Cm, axis=-1, keepdims=True))
        y = h * C_gate + D * x_conv
        y = y * jax.nn.silu(z)
        out = jnp.einsum('bli,hi->blh', y, W_out)
        return out

    def _L0_xattn_ref(queries, keys, values, attn_bias, Wq, Wk, Wv, Wp):
        import jax, jax.numpy as jnp
        import numpy as np
        D_MODEL = 128
        N_HEAD = 16
        D_KEY = 64
        D_VALUE = 64

        def _split_heads(x, n_head, d_head):
            B, S, _ = x.shape
            return x.reshape(B, S, n_head, d_head).transpose(0, 2, 1, 3)
        q = _split_heads(queries @ Wq.T, N_HEAD, D_KEY)
        k = _split_heads(keys @ Wk.T, N_HEAD, D_KEY)
        v = _split_heads(values @ Wv.T, N_HEAD, D_VALUE)
        scores = jnp.einsum('bhqd,bhkd->bhqk', q, k) * D_MODEL ** (-0.5) + attn_bias
        weights = jax.nn.softmax(scores, axis=-1)
        out = jnp.einsum('bhqk,bhkd->bhqd', weights, v)
        B, H, Sq, Dv = out.shape
        out = out.transpose(0, 2, 1, 3).reshape(B, Sq, H * Dv)
        return out @ Wp.T

    def _L0_ffn_ref(x, Wr, W1, W2):
        import math
        import jax, jax.numpy as jnp
        import numpy as np
        B, S, D, F, E = (8, 256, 128, 512, 8)
        CAPACITY_FACTOR = 1.0
        b, s, d = x.shape
        t = b * s
        cap = max(math.ceil(t * CAPACITY_FACTOR / E), 1)
        xf = x.reshape(t, d)
        probs = jax.nn.softmax(xf.astype(jnp.float32) @ Wr, axis=-1)
        eidx = jnp.argmax(probs, axis=-1)
        p_tok = jnp.take_along_axis(probs, eidx[:, None], axis=1)[:, 0]
        onehot = jax.nn.one_hot(eidx, E, dtype=jnp.int32)
        rank_all = jnp.cumsum(onehot, axis=0) - onehot
        rank = jnp.take_along_axis(rank_all, eidx[:, None], axis=1)[:, 0]
        keep = rank < cap
        slot = jnp.where(keep, rank, cap)
        dispatch = jnp.zeros((E, cap + 1), dtype=jnp.int32).at[eidx, slot].set(jnp.arange(t, dtype=jnp.int32))
        valid = jnp.zeros((E, cap + 1), dtype=bool).at[eidx, slot].set(keep)
        dispatch = dispatch[:, :cap]
        valid = valid[:, :cap]
        xe = xf[dispatch]
        h = jnp.maximum(jnp.einsum('ecd,edf->ecf', xe, W1), 0.0)
        ye = jnp.einsum('ecf,efd->ecd', h, W2)
        pe = p_tok[dispatch]
        ye = ye * (pe * valid.astype(ye.dtype))[:, :, None]
        y = jnp.zeros((t, d), dtype=x.dtype).at[dispatch.reshape(-1)].add(ye.reshape(E * cap, d).astype(x.dtype))
        return y.reshape(b, s, d)

    def _L1_attn_ref(x, gamma, beta, Wq, Wv, Wr, u_bias, v_bias, Wout, bout):
        import math
        import jax, jax.numpy as jnp
        import numpy as np
        SEQ, BATCH, D_MODEL, NHEAD, FEAT = (256, 2, 128, 8, 128)

        def _sinusoid_pe(length, d_model, dtype):
            pos = jnp.arange(length, dtype=dtype)[:, None]
            div = jnp.exp(jnp.arange(0, d_model, 2, dtype=dtype) * (-math.log(10000.0) / d_model))
            ang = pos * div
            return jnp.stack([jnp.sin(ang), jnp.cos(ang)], axis=-1).reshape(length, d_model)

        def _left_shift(x):
            I, J, B, N = x.shape
            zero = jnp.zeros((I, 1, B, N), x.dtype)
            padded = jnp.concatenate([zero, x], axis=1)
            padded = padded.reshape(J + 1, I, B, N)[1:]
            x = padded.reshape(I, J, B, N)
            return jnp.tril(x)
        I, B, D = x.shape
        H, F = u_bias.shape
        sqrt_d = jnp.asarray(math.sqrt(D), x.dtype)
        mu = jnp.mean(x, axis=-1, keepdims=True)
        var = jnp.mean((x - mu) ** 2, axis=-1, keepdims=True)
        h = (x - mu) * jax.lax.rsqrt(var + 1e-05) * gamma + beta
        pe = _sinusoid_pe(I, D, x.dtype)[::-1]
        q = (h @ Wq).reshape(I, B, H, F)
        k = (h @ Wq).reshape(I, B, H, F)
        v = (h @ Wv).reshape(I, B, H, F)
        r = (pe @ Wr).reshape(I, H, F)
        content = jnp.einsum('ibnf,jbnf->ijbn', q + u_bias, k)
        pos = jnp.einsum('ibnf,jnf->ijbn', q + v_bias, r)
        pos = _left_shift(pos)
        attn = jax.nn.softmax((content + pos) / sqrt_d, axis=1)
        o = jnp.einsum('ijbn,jbnf->ibnf', attn, v).reshape(I, B, H * F)
        return o @ Wout + bout

    def _L1_xattn_ref(Q, K, V, w_q, w_k, w_v, w_o):
        import jax, jax.numpy as jnp
        import numpy as np
        N_HEADS, D_MODEL, DK, DV = (16, 128, 64, 64)
        B, S = (4, 256)
        b, s, _ = Q.shape
        q = (Q @ w_q).reshape(b, s, N_HEADS, DK).transpose(0, 2, 1, 3)
        k = (K @ w_k).reshape(b, s, N_HEADS, DK).transpose(0, 2, 1, 3)
        v = (V @ w_v).reshape(b, s, N_HEADS, DV).transpose(0, 2, 1, 3)
        scores = jnp.einsum('bhqd,bhkd->bhqk', q, k) / jnp.sqrt(jnp.float32(DK))
        attn = jax.nn.softmax(scores, axis=-1)
        x = jnp.einsum('bhqk,bhkd->bhqd', attn, v)
        x = x.transpose(0, 2, 1, 3).reshape(b, s, N_HEADS * DV)
        return x @ w_o

    def _L1_ffn_ref(x, gate_w, expert_w):
        import jax, jax.numpy as jnp
        import numpy as np
        B, S, H, E = (2, 1024, 128, 8)
        SCALE = 0.5
        scores = jnp.einsum('bsh,eh->bse', x, gate_w)
        chosen = jnp.argmax(scores, axis=-1)
        onehot = jax.nn.one_hot(chosen, gate_w.shape[0], dtype=x.dtype)
        expert_out = jnp.einsum('bsh,efh->bsef', x, expert_w)
        return x + jnp.einsum('bsef,bse->bsf', expert_out, onehot)
    x = _layernorm(x + _L0_attn_ref(x, L0_attn_W_in, L0_attn_conv_w, L0_attn_conv_b, L0_attn_W_x, L0_attn_W_dt, L0_attn_b_dt, L0_attn_A_log, L0_attn_D, L0_attn_W_out), axis=-1)
    x = _layernorm(x + _L0_xattn_ref(x, ctx_1024, ctx_1024, fside_1x1xSxS2_0, L0_xattn_Wq, L0_xattn_Wk, L0_xattn_Wv, L0_xattn_Wp), axis=-1)
    x = _layernorm(x + _L0_ffn_ref(x, L0_ffn_Wr, L0_ffn_W1, L0_ffn_W2), axis=-1)
    x = _layernorm(x + _L1_attn_ref(x, L1_attn_gamma, L1_attn_beta, L1_attn_Wq, L1_attn_Wv, L1_attn_Wr, L1_attn_u_bias, L1_attn_v_bias, L1_attn_Wout, L1_attn_bout), axis=-1)
    x = _layernorm(x + _L1_xattn_ref(x, ctx_1024, ctx_1024, L1_xattn_w_q, L1_xattn_w_k, L1_xattn_w_v, L1_xattn_w_o), axis=-1)
    x = _layernorm(x + _L1_ffn_ref(x, L1_ffn_gate_w, L1_ffn_expert_w), axis=-1)
    return x

_drawn_inputs = setup_inputs


def setup_inputs(seed=0):
    import zlib

    import numpy as np

    out = dict(_drawn_inputs(seed))
    spreads = {'L0_attn_conv_b': (0.0, 0.8),
     'L0_attn_D': (1.0, 0.6),
     'L1_attn_gamma': (1.0, 0.6),
     'L1_attn_beta': (0.0, 0.8),
     'L1_attn_bout': (0.0, 0.1)}
    factors = {'L0_attn_W_in': 8.0,
     'L0_attn_conv_w': 8.0,
     'L0_attn_W_x': 8.0,
     'L0_attn_W_dt': 27.878,
     'L0_attn_b_dt': 64.0,
     'L0_attn_W_out': 8.0,
     'L1_attn_Wq': 64.0,
     'L1_attn_Wv': 2.885,
     'L1_attn_Wr': 64.0,
     'L1_attn_u_bias': 64.0,
     'L1_attn_v_bias': 64.0,
     'L1_attn_Wout': 2.935,
     'L1_ffn_gate_w': 64.0}
    for name, (base, spread) in spreads.items():
        noise = np.random.default_rng([zlib.crc32(name.encode()), seed]).standard_normal(out[name].shape)
        drawn = base * np.exp(spread * noise) if base else spread * noise
        out[name] = jnp.asarray(drawn.astype(out[name].dtype))
    for name, factor in factors.items():
        out[name] = (out[name] * factor).astype(out[name].dtype)
    return out
```

```python
from contextlib import ExitStack
import math

import numpy as np

import concourse.bass as bass
from concourse import mybir

F32 = mybir.dt.float32
BF16 = mybir.dt.bfloat16
I32 = mybir.dt.int32
U32 = mybir.dt.uint32
ALU = mybir.AluOpType
ACT = mybir.ActivationFunctionType
AX = mybir.AxisListType

P = 128
NB = 32
EPS = 1e-5
BANK = 512


def wait_alone(eng, sem, value):
    eng.wait_ge(sem, value)
    eng.nop(nofuse=True)


def after(eng, sem, value):
    if not isinstance(value, int) or value > 0:
        eng.wait_ge(sem, value)


def skewed(eng, turns, front, back):
    front(0, 0)
    front(1, 1)
    back(0, 0)
    front(2, 0)
    back(1, 1)
    with eng.Fori(1, turns // 2 - 1) as i:
        front(2 * i + 1, 1)
        back(2 * i, 0)
        front(2 * i + 2, 0)
        back(2 * i + 1, 1)
    front(turns - 1, 1)
    back(turns - 2, 0)
    back(turns - 1, 1)


class Chain:

    def __init__(self, eng, sem, turn, per_turn, before=0):
        self.eng, self.sem, self.per_turn = eng, sem, per_turn
        self.base = turn * per_turn + before
        self.n = 0

    def __call__(self, ins, alone=False):
        self.n += 1
        ins.then_inc(self.sem, 1)
        self.eng.wait_ge(self.sem, self.base + self.n)
        if alone:
            self.eng.nop(nofuse=True)

    def end(self):
        assert self.n == self.per_turn, (self.n, self.per_turn)


def make_identity(nc, pool, ident, sem):
    nc.gpsimd.memset(ident[:], 0.0).then_inc(sem, 1)
    pool.wait_ge(sem, 1)
    nc.gpsimd.affine_select(out=ident[:], in_=ident[:], compare_op=ALU.not_equal, fill=1.0, base=0,
                            pattern=[[-1, P]], channel_multiplier=1).then_inc(sem, 1)


def mamba_pass(nc, ps, dram, w, out):
    SEQS = 4
    T = SEQS * P
    TURNS = NB // SEQS
    PAD = 3
    with ExitStack() as ctx:
        def sb(name, shape, dt=F32):
            return ctx.enter_context(nc.sbuf_tensor("m_" + name, shape, dt))

        def sem(name):
            return nc.alloc_semaphore("m_" + name)

        w_in = sb("w_in", [P, 4 * P])
        w_x_dt = sb("w_x_dt", [P, 2, 2 * P])
        w_x_b = sb("w_x_b", [16, 2 * P])
        w_x_c = sb("w_x_c", [16, 2 * P])
        w_dt = sb("w_dt", [P, 2, 2 * P])
        w_out = sb("w_out", [P, 2, P])
        w_comb = sb("w_comb", [P, 2, 2 * P])
        w_gate = sb("w_gate", [P, 2, 2, P])
        per_channel = sb("per_channel", [P, 2, 7])
        conv_w = per_channel[:, :, 0:4]
        conv_b = per_channel[:, :, 4]
        b_dt = per_channel[:, :, 5]
        d_skip = per_channel[:, :, 6]
        sixteenth = sb("sixteenth", [16, P])
        minus_half = sb("minus_half", [P, SEQS])
        xT = sb("xT", [P, T])
        x_tok = sb("x_tok", [P, SEQS, P])
        xpad = sb("xpad", [P, 2, SEQS, PAD + P])
        conv = sb("conv", [P, 2, T])
        sig = sb("sig", [P, 2, T])
        sigz = sb("sigz", [P, 2, T])
        zs = sb("zs", [P, 2, 2, T])
        xc = sb("xc", [P, 2, 2, T])
        gate = sb("gate", [P, 2, T])
        relu = sb("relu", [P, 2, T])
        soft = sb("soft", [P, 2, T])
        sp = sb("sp", [P, 2, T])
        g = sb("g", [P, 2, T])
        alpha = sb("alpha", [P, 2, T])
        alpha_c = sb("alpha_c", [P, 2, T])
        gated = sb("gated", [P, 2, T])
        hid = sb("hid", [P, 2, T])
        hc = sb("hc", [P, 2, T])
        y = sb("y", [P, 2, T])
        res = sb("res", [P, SEQS, P])
        stats = sb("stats", [P, SEQS, 6])
        mv = sb("mv", [P, SEQS, 2])
        ve = sb("ve", [P, SEQS])
        rstd = sb("rstd", [P, SEQS])
        x1 = sb("x1", [P, SEQS, P])

        weights_in = sem("weights_in")
        consts = sem("consts")
        wprod = sem("wprod")
        wcomb_ready = sem("wcomb_ready")
        xT_in = sem("xT_in")
        x_in = sem("x_in")
        inproj_done = sem("inproj_done")
        taps_ready = sem("taps_ready")
        conv_done = sem("conv_done")
        ez_done = sem("ez_done")
        ez_bound = sem("ez_bound")
        sigz_done = sem("sigz_done")
        zs_done = sem("zs_done")
        ec_done = sem("ec_done")
        ec_bound = sem("ec_bound")
        sig_done = sem("sig_done")
        xc_done = sem("xc_done")
        gate_sums = sem("gate_sums")
        gate_exp = sem("gate_exp")
        gate_bound = sem("gate_bound")
        gates = sem("gates")
        dt_done = sem("dt_done")
        absd = sem("absd")
        soft_done = sem("soft_done")
        sp_done = sem("sp_done")
        g_done = sem("g_done")
        alpha_done = sem("alpha_done")
        gated_done = sem("gated_done")
        scan_done = sem("scan_done")
        hc_done = sem("hc_done")
        yskip = sem("yskip")
        y_done = sem("y_done")
        out_done = sem("out_done")
        res_done = sem("res_done")
        var_done = sem("var_done")
        rstd_done = sem("rstd_done")
        x1_done = sem("x1_done")
        stored = sem("stored")
        act_front = sem("act_front")
        act_back = sem("act_back")
        dve_front = sem("dve_front")
        dve_back = sem("dve_back")
        pool_link = sem("pool_link")

        XP, Z, DT, GT = (0, 1), (2, 3), (4, 5), (6, 7)
        OUT = 6
        LARGE = 1e18

        block = ctx.enter_context(nc.Block())
        WEIGHT_DMAS = 7

        @block.sync
        def _(sp_):
            for dst, src in (
                (w_in[:], w["W_inT"]),
                (per_channel[:], w["per_channel"].rearrange("(k p) t -> p k t", k=2)),
                (w_x_dt[:], w["W_x"][32:].rearrange("(k p) i -> p k i", k=2)),
                (w_dt[:], w["W_dtT"].rearrange("(k p) o -> p k o", k=2)),
                (w_x_b[:], w["W_x"][0:16]),
                (w_x_c[:], w["W_x"][16:32]),
                (w_out[:], w["W_outT"].rearrange("(k p) o -> p k o", k=2)),
            ):
                sp_.dma_start(dst, src).then_inc(weights_in, 16)

            with sp_.Fori(0, TURNS) as i:
                sp_.wait_ge(inproj_done, i * 4)
                sp_.dma_start(xT[:], dram["xT"][:, bass.ds(i * T, T)]).then_inc(xT_in, 16)
                sp_.wait_ge(res_done, i)
                sp_.dma_start(x_tok[:], dram["x"][bass.ds(i * SEQS, SEQS)].rearrange("b s d -> s b d")
                              ).then_inc(x_in, 16)

        @block.tensor
        def _(pe):
            pe.wait_ge(weights_in, 16 * WEIGHT_DMAS)
            pe.wait_ge(consts, 1)
            for k in range(2):
                for m in range(2):
                    last = nc.tensor.matmul(ps[k][:, 0:2 * P], w_x_dt[:, m, k * P:(k + 1) * P],
                                            w_dt[:, m, :], start=(m == 0), stop=(m == 1))
                last.then_inc(wprod, 1)
            for q, wx in enumerate((w_x_b, w_x_c)):
                for k in range(2):
                    last = nc.tensor.matmul(ps[2][:, (2 * k + q) * P:(2 * k + q + 1) * P],
                                            wx[:, k * P:(k + 1) * P], sixteenth[:],
                                            start=True, stop=True)
            last.then_inc(wprod, 1)
            pe.wait_ge(wcomb_ready, 3)

            def front(t, par):
                pe.wait_ge(xT_in, t * 16 + 16)
                for q, bank in enumerate(XP + Z):
                    if q in (0, 1):
                        after(pe, taps_ready, t * 2 - 1 + q)
                    else:
                        after(pe, zs_done, t * 2 - 3 + q)
                    nc.tensor.matmul(ps[bank], w_in[:, q * P:(q + 1) * P], xT[:],
                                     start=True, stop=True).then_inc(inproj_done, 1)

            def back(t, par):
                pe.wait_ge(xc_done, t * 2 + 2)
                after(pe, res_done, t)
                after(pe, gate_exp, t * 2)
                for q, bank in enumerate(GT):
                    for k in range(2):
                        last = nc.tensor.matmul(ps[bank], w_gate[:, k, q, :], xc[:, par, k, :],
                                                start=(k == 0), stop=(k == 1))
                    last.then_inc(gate_sums, 1)
                after(pe, sp_done, t * 2)
                for h, bank in enumerate(DT):
                    for k in range(2):
                        last = nc.tensor.matmul(ps[bank], w_comb[:, k, h * P:(h + 1) * P],
                                                xc[:, par, k, :], start=(k == 0), stop=(k == 1))
                    last.then_inc(dt_done, 1)
                pe.wait_ge(gate_exp, t * 2 + 1)
                pe.wait_ge(y_done, t * 2 + 2)
                for b in range(SEQS):
                    for k in range(2):
                        last = nc.tensor.matmul(ps[OUT][:, b * P:(b + 1) * P],
                                                y[:, k, b * P:(b + 1) * P], w_out[:, k, :],
                                                start=(k == 0), stop=(k == 1))
                last.then_inc(out_done, 1)

            skewed(pe, TURNS, front, back)

        @block.scalar
        def _(act):
            nc.scalar.preload_act_table_set("natural_log_exp_and_others")
            for k in range(2):
                act.wait_ge(wprod, k + 1)
                nc.scalar.copy(w_comb[:, k, :], ps[k][:, 0:2 * P]).then_inc(wcomb_ready, 1)
            act.wait_ge(wprod, 3)
            nc.scalar.copy(w_gate[:].rearrange("p k q c -> p (k q c)"), ps[2]).then_inc(wcomb_ready, 1)
            act.wait_ge(consts, 3)

            def front(t, par):
                for h in range(2):
                    act.wait_ge(inproj_done, t * 4 + h + 1)
                    after(act, xc_done, t * 2 - 1 + h)
                    nc.scalar.activation(conv[:, h, :], ps[XP[h]], ACT.Identity,
                                         bias=conv_b[:, h:h + 1], scale=conv_w[:, h, 3:4])
                    nc.scalar.copy(xpad[:, h, :, PAD:],
                                   ps[XP[h]].rearrange("p (b s) -> p b s", b=SEQS)
                                   ).then_inc(taps_ready, 1)
                for h in range(2):
                    act.wait_ge(inproj_done, t * 4 + 3 + h)
                    after(act, zs_done, t * 2 - 1 + h)
                    nc.scalar.activation(sigz[:, h, :], ps[Z[h]], ACT.Exp, scale=-1.0
                                         ).then_inc(ez_done, 1)
                for h in range(2):
                    act.wait_ge(conv_done, t * 2 + h + 1)
                    nc.scalar.activation(sig[:, h, :], conv[:, h, :], ACT.Exp, scale=-1.0
                                         ).then_inc(ec_done, 1)
                link = Chain(act, act_front, t, 4)
                for h in range(2):
                    act.wait_ge(ez_bound, t * 2 + h + 1)
                    link(nc.scalar.activation(sigz[:, h, :], sigz[:, h, :], ACT.Ln, bias=1.0))
                    nc.scalar.activation(sigz[:, h, :], sigz[:, h, :], ACT.Exp, scale=-1.0
                                         ).then_inc(sigz_done, 1)
                for h in range(2):
                    act.wait_ge(ec_bound, t * 2 + h + 1)
                    link(nc.scalar.activation(sig[:, h, :], sig[:, h, :], ACT.Ln, bias=1.0))
                    nc.scalar.activation(sig[:, h, :], sig[:, h, :], ACT.Exp, scale=-1.0
                                         ).then_inc(sig_done, 1)
                link.end()

            def back(t, par):
                link = Chain(act, act_back, t, 6)
                after(act, hc_done, t * 2)
                for q in range(2):
                    act.wait_ge(gate_sums, t * 2 + q + 1)
                    nc.scalar.activation(gate[:, q, :], ps[GT[q]], ACT.Exp, scale=-1.0
                                         ).then_inc(gate_exp, 1)
                after(act, sp_done, t * 2)
                for h in range(2):
                    act.wait_ge(dt_done, t * 2 + h + 1)
                    nc.scalar.activation(soft[:, h, :], ps[DT[h]], ACT.Abs, bias=b_dt[:, h:h + 1]
                                         ).then_inc(absd, 1)
                for h in range(2):
                    act.wait_ge(absd, t * 2 + h + 1)
                    link(nc.scalar.activation(soft[:, h, :], soft[:, h, :], ACT.Exp, scale=-1.0))
                    nc.scalar.activation(soft[:, h, :], soft[:, h, :], ACT.Ln, bias=1.0
                                         ).then_inc(soft_done, 1)
                for q in range(2):
                    act.wait_ge(gate_bound, t * 2 + q + 1)
                    link(nc.scalar.activation(gate[:, q, :], gate[:, q, :], ACT.Ln, bias=1.0))
                    nc.scalar.activation(gate[:, q, :], gate[:, q, :], ACT.Exp, scale=-1.0
                                         ).then_inc(gates, 1)
                after(act, gated_done, t * 2)
                for h in range(2):
                    act.wait_ge(sp_done, t * 2 + h + 1)
                    nc.scalar.activation(g[:, h, :], sp[:, h, :], ACT.Exp, scale=-0.1
                                         ).then_inc(g_done, 1)
                after(act, scan_done, t * 2)
                for h in range(2):
                    act.wait_ge(g_done, t * 2 + h + 1)
                    link(nc.scalar.activation(alpha[:, h, :], g[:, h, :], ACT.Ln, bias=1.0))
                    nc.scalar.activation(alpha[:, h, :], alpha[:, h, :], ACT.Exp, scale=-1.0
                                         ).then_inc(alpha_done, 1)
                link.end()

            skewed(act, TURNS, front, back)

        @block.gpsimd
        def _(pool):
            nc.gpsimd.memset(sixteenth[:], 1.0 / 16).then_inc(consts, 1)
            nc.gpsimd.memset(xpad[:, :, :, 0:PAD], 0.0).then_inc(consts, 1)
            nc.gpsimd.memset(minus_half[:], -0.5).then_inc(consts, 1)
            pool.wait_ge(consts, 3)

            def front(t, par):
                pass

            def back(t, par):
                link = Chain(pool, pool_link, t, 4)
                after(pool, scan_done, t * 2)
                pool.wait_ge(gates, t * 2 + 1)
                for h in range(2):
                    link(nc.gpsimd.tensor_tensor(gated[:, h, :], xc[:, par, h, :], gate[:, 0, :],
                                                 ALU.mult))
                for h in range(2):
                    pool.wait_ge(alpha_done, t * 2 + h + 1)
                    link(nc.gpsimd.tensor_tensor(g[:, h, :], g[:, h, :], alpha[:, h, :], ALU.mult))
                    nc.gpsimd.tensor_tensor(gated[:, h, :], gated[:, h, :], g[:, h, :], ALU.mult
                                            ).then_inc(gated_done, 1)
                pool.wait_ge(gates, t * 2 + 2)
                for h in range(2):
                    pool.wait_ge(scan_done, t * 2 + h + 1)
                    nc.gpsimd.tensor_tensor(hc[:, h, :], hid[:, h, :], gate[:, 1, :], ALU.mult
                                            ).then_inc(hc_done, 1)
                after(pool, out_done, t)
                for h in range(2):
                    pool.wait_ge(yskip, t * 2 + h + 1)
                    nc.gpsimd.tensor_tensor(y[:, h, :], hc[:, h, :], zs[:, par, h, :], ALU.mult
                                            ).then_inc(y_done, 1)
                pool.wait_ge(var_done, t + 1)
                nc.gpsimd.tensor_tensor(rstd[:], ve[:], minus_half[:], ALU.pow).then_inc(rstd_done, 1)
                wait_alone(pool, x1_done, t + 1)
                pool.dma_start(out[bass.ds(t * SEQS, SEQS)].rearrange("b s d -> s b d"), x1[:]
                               ).then_inc(stored, 16)
                link.end()

            skewed(pool, TURNS, front, back)
            pool.wait_ge(stored, 16 * TURNS)

        @block.vector
        def _(dve):
            dve.wait_ge(weights_in, 16 * WEIGHT_DMAS)

            def front(t, par):
                link = Chain(dve, dve_front, t, 4)
                views = [conv[:, h, :].rearrange("p (b s) -> p b s", b=SEQS) for h in range(2)]
                for tap in (2, 1, 0):
                    for h in range(2):
                        if tap == 2:
                            dve.wait_ge(taps_ready, t * 2 + h + 1)
                        ins = nc.vector.scalar_tensor_tensor(
                            out=views[h], in0=xpad[:, h, :, tap:tap + P],
                            scalar=conv_w[:, h, tap:tap + 1], in1=views[h],
                            op0=ALU.mult, op1=ALU.add)
                        if tap:
                            link(ins)
                        else:
                            ins.then_inc(conv_done, 1)
                for v, made, bound in ((sigz, ez_done, ez_bound), (sig, ec_done, ec_bound)):
                    for h in range(2):
                        dve.wait_ge(made, t * 2 + h + 1)
                        nc.vector.tensor_scalar(v[:, h, :], v[:, h, :], LARGE, None, ALU.min
                                                ).then_inc(bound, 1)
                after(dve, y_done, t * 2 - 2)
                for h in range(2):
                    dve.wait_ge(sigz_done, t * 2 + h + 1)
                    nc.vector.tensor_tensor(zs[:, par, h, :], ps[Z[h]], sigz[:, h, :], ALU.mult
                                            ).then_inc(zs_done, 1)
                after(dve, gated_done, t * 2 - 2)
                after(dve, dt_done, t * 2 - 2)
                for h in range(2):
                    dve.wait_ge(sig_done, t * 2 + h + 1)
                    nc.vector.tensor_tensor(xc[:, par, h, :], conv[:, h, :], sig[:, h, :], ALU.mult
                                            ).then_inc(xc_done, 1)
                link.end()

            def back(t, par):
                link = Chain(dve, dve_back, t, 8)
                for q in range(2):
                    dve.wait_ge(gate_exp, t * 2 + q + 1)
                    nc.vector.tensor_scalar(gate[:, q, :], gate[:, q, :], LARGE, None, ALU.min
                                            ).then_inc(gate_bound, 1)
                for h in range(2):
                    dve.wait_ge(absd, t * 2 + h + 1)
                    link(nc.vector.tensor_scalar(relu[:, h, :], ps[DT[h]], b_dt[:, h:h + 1], 0.0,
                                                 ALU.add, ALU.max))
                for h in range(2):
                    dve.wait_ge(soft_done, t * 2 + h + 1)
                    nc.vector.tensor_tensor(sp[:, h, :], relu[:, h, :], soft[:, h, :], ALU.add
                                            ).then_inc(sp_done, 1)
                for h in range(2):
                    dve.wait_ge(alpha_done, t * 2 + h + 1)
                    link(nc.vector.tensor_scalar(alpha_c[:, h, :], alpha[:, h, :], 0.01, 0.99,
                                                 ALU.max, ALU.min))
                    link(nc.vector.memset(alpha_c[:, h, 0:T:P], 0.0))
                after(dve, hc_done, t * 2)
                for h in range(2):
                    dve.wait_ge(gated_done, t * 2 + h + 1)
                    nc.vector.tensor_tensor_scan(hid[:, h, :], alpha_c[:, h, :], gated[:, h, :], 0.0,
                                                 ALU.mult, ALU.add).then_inc(scan_done, 1)
                for h in range(2):
                    dve.wait_ge(hc_done, t * 2 + h + 1)
                    nc.vector.scalar_tensor_tensor(out=hc[:, h, :], in0=xc[:, par, h, :],
                                                   scalar=d_skip[:, h:h + 1], in1=hc[:, h, :],
                                                   op0=ALU.mult, op1=ALU.add).then_inc(yskip, 1)
                dve.wait_ge(out_done, t + 1)
                dve.wait_ge(x_in, t * 16 + 16)
                nc.vector.tensor_tensor(res[:], ps[OUT].rearrange("p (b d) -> p b d", b=SEQS),
                                        x_tok[:], ALU.add).then_inc(res_done, 1)
                dve.wait_ge(res_done, t + 1)
                for b in range(SEQS):
                    ins = nc.vector.bn_stats(stats[:, b, :], res[:, b, :])
                link(ins, alone=True)
                for b in range(SEQS):
                    ins = nc.vector.bn_aggr(mv[:, b, :], stats[:, b, :])
                link(ins)
                nc.vector.tensor_scalar(ve[:], mv[:, :, 1], EPS, None, ALU.add).then_inc(var_done, 1)
                dve.wait_ge(rstd_done, t + 1)
                after(dve, stored, t * 16)
                for b in range(SEQS):
                    ins = nc.vector.tensor_scalar(x1[:, b, :], res[:, b, :], mv[:, b, 0:1],
                                                  rstd[:, b:b + 1], ALU.subtract, ALU.mult)
                ins.then_inc(x1_done, 1)
                link.end()

            skewed(dve, TURNS, front, back)


HEADS, DH = 16, 64
GROUP = 4
GROUPS = HEADS // GROUP


def cross_attention_pass(nc, ps, name, x_dram, ctxT_dram, w, scale, bias_dram, ident, x_out):
    with ExitStack() as ctx:
        def sb(nm, shape, dt=F32):
            return ctx.enter_context(nc.sbuf_tensor(f"{name}_{nm}", shape, dt))

        def sem(nm):
            return nc.alloc_semaphore(f"{name}_{nm}")

        wq = sb("wq", [P, HEADS * DH])
        wk = sb("wk", [P, HEADS * DH])
        wv = sb("wv", [P, HEADS * DH])
        wo = sb("wo", [P, HEADS // 2, P])
        bias = sb("bias", [P, P]) if bias_dram is not None else None
        minus_half = sb("minus_half", [P, 1])
        xa = sb("xa", [P, P])
        xr = sb("xr", [P, P])
        ctxT = sb("ctxT", [P, P])
        xT = sb("xT", [P, P])
        qT = sb("qT", [P, 2, 8, P])
        kT = sb("kT", [P, 2, 8, P])
        v = sb("v", [P, 2, HEADS * DH])
        ss = sb("ss", [P, 2, GROUP, P]) if bias_dram is not None else None
        nmax = sb("nmax", [P, 2, GROUP])
        prob = sb("prob", [P, 2, GROUP, P])
        rsum = sb("rsum", [P, 2, GROUP])
        rinv = sb("rinv", [P, 2, GROUP])
        pT = sb("pT", [P, 2, GROUP, P])
        oT = sb("oT", [P, 8, P])
        res = sb("res", [P, P])
        stats = sb("stats", [P, 6])
        mv = sb("mv", [P, 2])
        ve = sb("ve", [P, 1])
        rstd = sb("rstd", [P, 1])

        weights_in = sem("weights_in")
        consts = sem("consts")
        xa_in = sem("xa_in")
        xr_in = sem("xr_in")
        ctx_in = sem("ctx_in")
        fill_done = sem("fill_done")
        act_copied = sem("act_copied")
        v_copied = sem("v_copied")
        s_done = sem("s_done")
        biased = sem("biased")
        nmax_done = sem("nmax_done")
        exp_done = sem("exp_done")
        rinv_done = sem("rinv_done")
        norm_done = sem("norm_done")
        t_done = sem("t_done")
        pt_copied = sem("pt_copied")
        pv_done = sem("pv_done")
        ot_copied = sem("ot_copied")
        op_done = sem("op_done")
        res_done = sem("res_done")
        var_done = sem("var_done")
        rstd_done = sem("rstd_done")
        x_done = sem("x_done")
        ln_link = sem("ln_link")

        SC, PT, OT, FILL, OP = (0, 1), (2, 3), 4, (5, 6), 7
        LAST = NB - 1
        n_weights = 4 + (bias is not None)

        def turns(eng, begin, turn, end=None):
            begin()
            turn(0, 0, True)
            turn(1, 1, True)
            with eng.Fori(1, NB // 2 - 1) as i:
                turn(2 * i, 0, True)
                turn(2 * i + 1, 1, True)
            turn(NB - 2, 0, True)
            turn(NB - 1, 1, False)
            if end is not None:
                end()

        block = ctx.enter_context(nc.Block())

        @block.sync
        def _(sp):
            for dst, src in (
                (wk[:], w["k"]), (wv[:], w["v"]), (wq[:], w["q"]),
                (wo[:], w["o"].rearrange("(j p) o -> p j o", p=P)),
            ):
                sp.dma_start(dst, src).then_inc(weights_in, 16)
            if bias is not None:
                sp.dma_start(bias[:], bias_dram).then_inc(weights_in, 16)

            def load_next(t):
                after(sp, fill_done, 7 * t - 6)
                sp.dma_start(xa[:], x_dram[t]).then_inc(xa_in, 16)
                after(sp, fill_done, 7 * t - 2)
                sp.dma_start(ctxT[:], ctxT_dram[:, bass.ds(t * P, P)]).then_inc(ctx_in, 16)

            def load_residual(t):
                sp.wait_ge(res_done, t)
                sp.dma_start(xr[:], x_dram[t]).then_inc(xr_in, 16)

            load_next(0)
            load_next(1)
            load_residual(0)
            with sp.Fori(1, LAST) as i:
                load_next(i + 1)
                load_residual(i)
            load_residual(LAST)

        def bank_of(par, f):
            return FILL[(par + f) % 2]

        @block.tensor
        def _(pe):
            def fill(t, par, f):
                out = ps[bank_of(par, f)]
                if f == 0:
                    after(pe, act_copied, 5 * t - 1)
                    pe.wait_ge(xa_in, 16 * t + 16)
                    nc.tensor.transpose(out[:, 0:P], xa[:], ident[:]).then_inc(fill_done, 1)
                elif f in (1, 2):
                    after(pe, act_copied, 5 * t + f - 1)
                    if f == 1:
                        pe.wait_ge(ctx_in, 16 * t + 16)
                    for j in range(4):
                        pair = 4 * (f - 1) + j
                        last = nc.tensor.matmul(out[:, j * P:(j + 1) * P],
                                                wk[:, pair * P:(pair + 1) * P], ctxT[:],
                                                start=True, stop=True)
                    last.then_inc(fill_done, 1)
                elif f in (3, 4):
                    pe.wait_ge(act_copied, 5 * t + f - 1)
                    nc.tensor.matmul(out[:], ctxT[:], wv[:, (f - 3) * BANK:(f - 2) * BANK],
                                     start=True, stop=True).then_inc(fill_done, 1)
                else:
                    pe.wait_ge(v_copied, 2 * t + f - 4)
                    if f == 5:
                        pe.wait_ge(act_copied, 5 * t + 1)
                    for j in range(4):
                        pair = 4 * (f - 5) + j
                        last = nc.tensor.matmul(out[:, j * P:(j + 1) * P],
                                                wq[:, pair * P:(pair + 1) * P], xT[:],
                                                start=True, stop=True)
                    last.then_inc(fill_done, 1)

            def scores(t, par, g):
                after(pe, exp_done if bias is None else biased, 4 * t + g - 1)
                pe.wait_ge(act_copied, 5 * t + 5)
                for j in range(GROUP):
                    pair = GROUP * (g // 2) + j
                    r = DH * (g % 2)
                    last = nc.tensor.matmul(ps[SC[g % 2]][:, j * P:(j + 1) * P],
                                            qT[r:r + DH, par, pair, :], kT[r:r + DH, par, pair, :],
                                            start=True, stop=True)
                last.then_inc(s_done, 1)

            def transposes(t, g):
                pe.wait_ge(norm_done, 4 * t + g + 1)
                after(pe, pt_copied, 4 * t + g - 1)
                for j in range(GROUP):
                    last = nc.tensor.transpose(ps[PT[g % 2]][:, j * P:(j + 1) * P],
                                               prob[:, g % 2, j, :], ident[:])
                last.then_inc(t_done, 1)

            def values(t, par, g):
                pe.wait_ge(pt_copied, 4 * t + g + 1)
                if g == 0:
                    after(pe, ot_copied, 2 * t)
                    pe.wait_ge(v_copied, 2 * t + 2)
                if g == 2:
                    pe.wait_ge(ot_copied, 2 * t + 1)
                for j in range(GROUP):
                    h = 2 * (GROUP * (g // 2) + j) + g % 2
                    r = DH * (g % 2)
                    last = nc.tensor.matmul(ps[OT][r:r + DH, j * P:(j + 1) * P],
                                            v[:, par, h * DH:(h + 1) * DH], pT[:, g % 2, j, :],
                                            start=True, stop=True)
                last.then_inc(pv_done, 1)

            def out_projection(t):
                pe.wait_ge(ot_copied, 2 * t + 2)
                after(pe, res_done, t)
                for j in range(8):
                    last = nc.tensor.matmul(ps[OP][:, 0:P], oT[:, j, :], wo[:, j, :],
                                            start=(j == 0), stop=(j == 7))
                last.then_inc(op_done, 1)

            def begin():
                pe.wait_ge(weights_in, 16 * n_weights)
                for f in range(7):
                    fill(0, 0, f)
                scores(0, 0, 0)
                scores(0, 0, 1)

            def turn(t, par, more):
                for g, fills in enumerate(((0, 1), (2, 3), (4, 5), (6,))):
                    if more:
                        for f in fills:
                            fill(t + 1, 1 - par, f)
                    transposes(t, g)
                    values(t, par, g)
                    if g < 2:
                        scores(t, par, g + 2)
                if more:
                    scores(t + 1, 1 - par, 0)
                    scores(t + 1, 1 - par, 1)
                out_projection(t)

            turns(pe, begin, turn)

        @block.scalar
        def _(act):
            def copy(t, par, f):
                act.wait_ge(fill_done, 7 * t + f + 1)
                src = ps[bank_of(par, f)]
                if f == 0:
                    after(act, fill_done, 7 * t)
                    ins = nc.scalar.copy(xT[:], src[:, 0:P])
                elif f in (1, 2):
                    after(act, s_done, 4 * t - 4)
                    ins = nc.scalar.copy(kT[:, par, 4 * (f - 1):4 * f, :].rearrange("p j t -> p (j t)"),
                                         src[:])
                else:
                    after(act, s_done, 4 * t - 4)
                    ins = nc.scalar.mul(qT[:, par, 4 * (f - 5):4 * (f - 4), :]
                                        .rearrange("p j t -> p (j t)"), src[:], scale)
                ins.then_inc(act_copied, 1)

            def exps(t, g):
                act.wait_ge(nmax_done, 4 * t + g + 1)
                after(act, t_done, 4 * t + g - 1)
                after(act, rinv_done, 4 * t + g - 1)
                for j in range(GROUP):
                    src = ps[SC[g % 2]][:, j * P:(j + 1) * P] if bias is None else ss[:, g % 2, j, :]
                    last = nc.scalar.activation(prob[:, g % 2, j, :], src, ACT.Exp,
                                                bias=nmax[:, g % 2, j:j + 1],
                                                accum_out=rsum[:, g % 2, j:j + 1])
                last.then_inc(exp_done, 1)

            def copy_values(t, half):
                act.wait_ge(pv_done, 4 * t + 2 * half + 2)
                after(act, op_done, t)
                nc.scalar.copy(oT[:, 4 * half:4 * half + 4, :].rearrange("p j t -> p (j t)"),
                               ps[OT]).then_inc(ot_copied, 1)

            def begin():
                for f in (0, 1, 2, 5, 6):
                    copy(0, 0, f)
                exps(0, 0)
                exps(0, 1)

            def turn(t, par, more):
                if more:
                    copy(t + 1, 1 - par, 0)
                    copy(t + 1, 1 - par, 1)
                exps(t, 2)
                if more:
                    copy(t + 1, 1 - par, 2)
                exps(t, 3)
                copy_values(t, 0)
                if more:
                    copy(t + 1, 1 - par, 5)
                    copy(t + 1, 1 - par, 6)
                copy_values(t, 1)
                if more:
                    exps(t + 1, 0)
                    exps(t + 1, 1)

            turns(act, begin, turn)

        @block.gpsimd
        def _(pool):
            nc.gpsimd.memset(minus_half[:], -0.5).then_inc(consts, 1)

            def normalise(t, g):
                pool.wait_ge(rinv_done, 4 * t + g + 1)
                nc.gpsimd.tensor_tensor(prob[:, g % 2], prob[:, g % 2],
                                        rinv[:, g % 2, :].unsqueeze(2).to_broadcast([P, GROUP, P]),
                                        ALU.mult).then_inc(norm_done, 1)

            def begin():
                pool.wait_ge(consts, 1)
                normalise(0, 0)
                normalise(0, 1)

            def turn(t, par, more):
                normalise(t, 2)
                normalise(t, 3)
                if more:
                    normalise(t + 1, 0)
                    normalise(t + 1, 1)
                pool.wait_ge(var_done, t + 1)
                nc.gpsimd.tensor_tensor(rstd[:], ve[:], minus_half[:], ALU.pow).then_inc(rstd_done, 1)

            turns(pool, begin, turn)

        @block.vector
        def _(dve):
            def copy_v(t, par, n):
                dve.wait_ge(fill_done, 7 * t + 4 + n)
                after(dve, pv_done, 4 * t - 4)
                nc.vector.tensor_copy(v[:, par, n * BANK:(n + 1) * BANK], ps[bank_of(par, 3 + n)]
                                      ).then_inc(v_copied, 1)

            def maxima(t, g):
                dve.wait_ge(s_done, 4 * t + g + 1)
                src = ps[SC[g % 2]].rearrange("p (j k) -> p j k", j=GROUP)
                after(dve, exp_done, 4 * t + g - 1)
                if bias is not None:
                    nc.vector.tensor_tensor(ss[:, g % 2], src,
                                            bias[:].unsqueeze(1).to_broadcast([P, GROUP, P]), ALU.add
                                            ).then_inc(biased, 1)
                    dve.wait_ge(biased, 4 * t + g + 1)
                    src = ss[:, g % 2]
                nc.vector.tensor_reduce(nmax[:, g % 2, :], src, AX.X, ALU.max, negate=True
                                        ).then_inc(nmax_done, 1)

            def inverse(t, g):
                dve.wait_ge(exp_done, 4 * t + g + 1)
                after(dve, norm_done, 4 * t + g - 1)
                nc.vector.reciprocal(rinv[:, g % 2, :], rsum[:, g % 2, :]).then_inc(rinv_done, 1)

            def copy_pt(t, g):
                dve.wait_ge(t_done, 4 * t + g + 1)
                after(dve, pv_done, 4 * t + g - 1)
                nc.vector.tensor_copy(pT[:, g % 2].rearrange("p j t -> p (j t)"), ps[PT[g % 2]]
                                      ).then_inc(pt_copied, 1)

            def norm_layer(t):
                link = Chain(dve, ln_link, t, 2)
                dve.wait_ge(op_done, t + 1)
                dve.wait_ge(xr_in, 16 * t + 16)
                nc.vector.tensor_tensor(res[:], ps[OP][:, 0:P], xr[:], ALU.add).then_inc(res_done, 1)
                dve.wait_ge(res_done, t + 1)
                link(nc.vector.bn_stats(stats[:], res[:]), alone=True)
                link(nc.vector.bn_aggr(mv[:], stats[:]))
                nc.vector.tensor_scalar(ve[:], mv[:, 1:2], EPS, None, ALU.add).then_inc(var_done, 1)
                dve.wait_ge(rstd_done, t + 1)
                nc.vector.tensor_scalar(x_out(t), res[:], mv[:, 0:1], rstd[:, 0:1],
                                        ALU.subtract, ALU.mult).then_inc(x_done, 1)
                link.end()

            def begin():
                dve.wait_ge(weights_in, 16 * n_weights)
                copy_v(0, 0, 0)
                copy_v(0, 0, 1)
                maxima(0, 0)
                maxima(0, 1)
                inverse(0, 0)
                inverse(0, 1)

            def turn(t, par, more):
                copy_pt(t, 0)
                maxima(t, 2)
                if more:
                    copy_v(t + 1, 1 - par, 0)
                copy_pt(t, 1)
                maxima(t, 3)
                inverse(t, 2)
                if more:
                    copy_v(t + 1, 1 - par, 1)
                copy_pt(t, 2)
                inverse(t, 3)
                copy_pt(t, 3)
                if more:
                    maxima(t + 1, 0)
                    maxima(t + 1, 1)
                    inverse(t + 1, 0)
                    inverse(t + 1, 1)
                norm_layer(t)

            def end():
                dve.wait_ge(x_done, NB)

            turns(dve, begin, turn, end)


E, F, CAP = 8, 512, NB * P // 8
TOKENS = NB * P


def routing_pass(nc, ps, wr_dram, ident, x_res, p_tok, slot, xe_dram, ye_dram):
    QUAD = 4
    with ExitStack() as ctx:
        def sb(nm, shape, dt=F32):
            return ctx.enter_context(nc.sbuf_tensor("r_" + nm, shape, dt))

        def sem(nm):
            return nc.alloc_semaphore("r_" + nm)

        wr = sb("wr", [P, E])
        zeros = sb("zeros", [P, BANK])
        stage = sb("stage", [P, BANK])
        xT = sb("xT", [P, BANK])
        logits = sb("logits", [P, NB, E])
        nmax = sb("nmax", [P, NB])
        diff = sb("diff", [P, NB, E])
        ex = sb("ex", [P, NB, E])
        esum = sb("esum", [P, NB])
        order = sb("order", [P, E])
        val = sb("val", [P, NB, E])
        vmax = sb("vmax", [P, NB])
        onehot = sb("onehot", [P, NB, E])
        onehot_h = sb("onehot_h", [P, NB, E], BF16)
        before = sb("before", [P, P], BF16)
        ones_h = sb("ones_h", [P, P], BF16)
        ones = sb("ones", [P, NB])
        upto = sb("upto", [P, NB, E])
        rank = sb("rank", [P, NB, E])
        picked = sb("picked", [P, NB, E])
        base = sb("base", [P, E])
        rank_tok = sb("rank_tok", [P, NB])
        base_tok = sb("base_tok", [P, NB])
        keep = sb("keep", [P, NB])
        slot_f = sb("slot_f", [P, NB])

        wr_in = sem("wr_in")
        consts = sem("consts")
        cleared = sem("cleared")
        staged = sem("staged")
        t_done = sem("t_done")
        t_copied = sem("t_copied")
        l_done = sem("l_done")
        l_copied = sem("l_copied")
        diff_done = sem("diff_done")
        ex_done = sem("ex_done")
        onehot_done = sem("onehot_done")
        ranks_done = sem("ranks_done")
        slot_done = sem("slot_done")
        scattered = sem("scattered")
        dve_link = sem("dve_link")
        n_consts = 8
        block = ctx.enter_context(nc.Block())

        @block.sync
        def _(sp):
            sp.dma_start(wr[:], wr_dram).then_inc(wr_in, 16)
            sp.wait_ge(consts, 1)
            for n in range(8):
                sp.dma_start(xe_dram[n * CAP:(n + 1) * CAP].rearrange("(p r) d -> p (r d)", p=P),
                             zeros[:]).then_inc(cleared, 16)
            sp.dma_start(ye_dram[TOKENS:TOKENS + 1], zeros[0:1, 0:P]).then_inc(cleared, 16)

        @block.gpsimd
        def _(pool):
            nc.gpsimd.memset(zeros[:], 0.0).then_inc(consts, 1)
            nc.gpsimd.memset(ones_h[:], 1.0).then_inc(consts, 1)
            nc.gpsimd.memset(ones[:], 1.0).then_inc(consts, 1)
            nc.gpsimd.memset(before[:], 1.0).then_inc(consts, 1)
            for e in range(E):
                nc.gpsimd.memset(order[:, e:e + 1], float(E - e))
                last = nc.gpsimd.memset(base[:, e:e + 1], float(CAP * e))
            last.then_inc(consts, 1)
            pool.wait_ge(consts, 5)
            nc.gpsimd.affine_select(out=before[:], in_=before[:], compare_op=ALU.is_gt, fill=0.0,
                                    base=0, pattern=[[1, P]], channel_multiplier=-1
                                    ).then_inc(consts, 3)
            pool.wait_ge(slot_done, 1)
            pool.wait_ge(cleared, 16 * 9)
            for b in range(NB):
                nc.gpsimd.indirect_dma_start(
                    out=xe_dram[:, :], out_offset=bass.IndirectOffsetOnAxis(ap=slot[:, b:b + 1], axis=0),
                    in_=x_res[:, b * P:(b + 1) * P], in_offset=None,
                    bounds_check=TOKENS - 1, oob_is_err=False).then_inc(scattered, 16)
            pool.wait_ge(scattered, 16 * NB)

        @block.scalar
        def _(act):
            with act.Fori(0, NB // QUAD) as i:
                act.wait_ge(t_done, i)
                act.nop(nofuse=True)
                nc.scalar.copy(stage[:], x_res[:, bass.ds(i * BANK, BANK)]).then_inc(staged, 1)
                act.wait_ge(t_done, i + 1)
                nc.scalar.copy(xT[:], ps[0]).then_inc(t_copied, 1)
            act.wait_ge(diff_done, 1)
            nc.scalar.activation(ex[:], diff[:], ACT.Exp).then_inc(ex_done, 1)

        @block.tensor
        def _(pe):
            pe.wait_ge(wr_in, 16)
            with pe.Fori(0, NB // QUAD) as i:
                pe.wait_ge(staged, i + 1)
                pe.wait_ge(t_copied, i)
                for j in range(QUAD):
                    last = nc.tensor.transpose(ps[0][:, j * P:(j + 1) * P], stage[:, j * P:(j + 1) * P],
                                               ident[:])
                last.then_inc(t_done, 1)
                pe.wait_ge(t_copied, i + 1)
                pe.wait_ge(l_copied, i)
                for j in range(QUAD):
                    last = nc.tensor.matmul(ps[1][:, j * E:(j + 1) * E], xT[:, j * P:(j + 1) * P], wr[:],
                                            start=True, stop=True)
                last.then_inc(l_done, 1)
            pe.wait_ge(onehot_done, 1)
            pe.wait_ge(consts, n_consts)
            oh = onehot_h[:].rearrange("p t e -> p (t e)")
            nc.tensor.matmul(ps[2][:, 0:NB * E], before[:], oh, start=True, stop=True)
            nc.tensor.matmul(ps[3][:, 0:NB * E], ones_h[:], oh, start=True, stop=True
                             ).then_inc(ranks_done, 1)

        @block.vector
        def _(dve):
            with dve.Fori(0, NB // QUAD) as i:
                wait_alone(dve, l_done, i + 1)
                nc.vector.tensor_copy(
                    logits[:].rearrange("p t e -> p (t e)")[:, bass.ds(i * QUAD * E, QUAD * E)],
                    ps[1][:, 0:QUAD * E]).then_inc(l_copied, 1)
            dve.wait_ge(l_copied, NB // QUAD)
            dve.wait_ge(consts, n_consts)
            link = Chain(dve, dve_link, 0, 18)

            def wide(v):
                return v.unsqueeze(2).to_broadcast([P, NB, E])

            def per_expert(v):
                return v.unsqueeze(1).to_broadcast([P, NB, E])

            link(nc.vector.tensor_reduce(nmax[:], logits[:], AX.X, ALU.max, negate=True))
            nc.vector.tensor_tensor(diff[:], logits[:], wide(nmax[:]), ALU.add).then_inc(diff_done, 1)
            dve.wait_ge(diff_done, 1)
            link(nc.vector.scalar_tensor_tensor(out=val[:], in0=diff[:], scalar=0.0,
                                                in1=per_expert(order[:]), op0=ALU.is_equal, op1=ALU.mult))
            link(nc.vector.tensor_reduce(vmax[:], val[:], AX.X, ALU.max))
            link(nc.vector.tensor_tensor(onehot[:], val[:], wide(vmax[:]), ALU.is_equal))
            nc.vector.tensor_copy(onehot_h[:], onehot[:]).then_inc(onehot_done, 1)
            dve.wait_ge(ex_done, 1)
            link(nc.vector.tensor_reduce(esum[:], ex[:], AX.X, ALU.add))
            link(nc.vector.reciprocal(p_tok[:], esum[:]))
            dve.wait_ge(ranks_done, 1)
            within = ps[2][:, 0:NB * E].rearrange("p (t e) -> p t e", e=E)
            total = ps[3][:, 0:NB * E].rearrange("p (t e) -> p t e", e=E)
            for e in range(E):
                ins = nc.vector.tensor_tensor_scan(upto[:, :, e], ones[:], total[:, :, e], 0.0,
                                                   ALU.mult, ALU.add)
            link(ins)
            link(nc.vector.tensor_tensor(rank[:], upto[:], total, ALU.subtract))
            link(nc.vector.tensor_tensor(rank[:], rank[:], within, ALU.add))
            link(nc.vector.tensor_tensor(picked[:], rank[:], onehot[:], ALU.mult))
            link(nc.vector.tensor_reduce(rank_tok[:], picked[:], AX.X, ALU.add))
            link(nc.vector.tensor_tensor(val[:], onehot[:], per_expert(base[:]), ALU.mult))
            link(nc.vector.tensor_reduce(base_tok[:], val[:], AX.X, ALU.add))
            link(nc.vector.tensor_scalar(keep[:], rank_tok[:], float(CAP), None, ALU.is_lt))
            link(nc.vector.tensor_tensor(slot_f[:], base_tok[:], rank_tok[:], ALU.add))
            link(nc.vector.scalar_tensor_tensor(out=slot_f[:], in0=slot_f[:], scalar=float(-TOKENS),
                                                in1=keep[:], op0=ALU.add, op1=ALU.mult))
            link(nc.vector.tensor_scalar(slot_f[:], slot_f[:], float(TOKENS), None, ALU.add))
            nc.vector.tensor_copy(slot[:], slot_f[:]).then_inc(slot_done, 1)
            dve.wait_ge(slot_done, 1)
            assert link.n <= 18


def experts_pass(nc, ps, w1_dram, w2_dram, ident, xe_dram, ye_dram):
    S = CAP // P
    C = F // P
    with ExitStack() as ctx:
        def sb(nm, shape, dt=F32):
            return ctx.enter_context(nc.sbuf_tensor("f_" + nm, shape, dt))

        def sem(nm):
            return nc.alloc_semaphore("f_" + nm)

        xe = sb("xe", [P, 2, S, P])
        w1 = sb("w1", [P, 2, F])
        w2 = sb("w2", [P, 2, C, P])
        xeT = sb("xeT", [P, 2, CAP])
        hT = sb("hT", [P, C, CAP])
        ye = sb("ye", [P, S, P])
        xe_in = [sem("xe_in0"), sem("xe_in1")]
        w_in = [sem("w_in0"), sem("w_in1")]
        t_done = sem("t_done")
        t_copied = sem("t_copied")
        h_done = sem("h_done")
        h_act = sem("h_act")
        h_dve = sem("h_dve")
        y_done = sem("y_done")
        y_copied = sem("y_copied")
        stored = sem("stored")
        TB, HB, YB = (0, 1), (2, 3, 4, 5), (6, 7)
        block = ctx.enter_context(nc.Block())

        @block.sync
        def _(sp):
            def front(t, par):
                after(sp, t_done, t - 1)
                sp.dma_start(xe[:, par], xe_dram[bass.ds(t * CAP, CAP)].rearrange("(s p) d -> p s d", p=P)
                             ).then_inc(xe_in[par], 16)
                after(sp, y_done, t - 1)
                sp.dma_start(w1[:, par, :], w1_dram[t]).then_inc(w_in[par], 16)
                sp.dma_start(w2[:, par], w2_dram[t].rearrange("(c f) d -> f c d", f=P)
                             ).then_inc(w_in[par], 16)

            def back(t, par):
                sp.wait_ge(y_copied, t + 1)
                sp.dma_start(ye_dram[bass.ds(t * CAP, CAP)].rearrange("(s p) d -> p s d", p=P), ye[:]
                             ).then_inc(stored, 16)

            skewed(sp, E, front, back)
            sp.wait_ge(stored, 16 * E)

        @block.tensor
        def _(pe):
            def front(t, par):
                pe.wait_ge(xe_in[par], 8 * (t - par) + 16)
                after(pe, t_copied, t - 1)
                for s in range(S):
                    last = nc.tensor.transpose(ps[TB[par]][:, s * P:(s + 1) * P], xe[:, par, s, :], ident[:])
                last.then_inc(t_done, 1)

            def back(t, par):
                pe.wait_ge(t_copied, t + 1)
                pe.wait_ge(w_in[par], 16 * (t - par) + 32)
                for c in range(C):
                    after(pe, h_act if c % 2 == 0 else h_dve, (C // 2) * (t - 1) + c // 2 + 1)
                    nc.tensor.matmul(ps[HB[c]], w1[:, par, c * P:(c + 1) * P], xeT[:, par, :],
                                     start=True, stop=True).then_inc(h_done, 1)
                pe.wait_ge(h_act, (C // 2) * (t + 1))
                pe.wait_ge(h_dve, (C // 2) * (t + 1))
                after(pe, y_copied, t - 1)
                for s in range(S):
                    for c in range(C):
                        last = nc.tensor.matmul(ps[YB[par]][:, s * P:(s + 1) * P],
                                                hT[:, c, s * P:(s + 1) * P], w2[:, par, c, :],
                                                start=(c == 0), stop=(c == C - 1))
                last.then_inc(y_done, 1)

            skewed(pe, E, front, back)

        @block.scalar
        def _(act):
            def front(t, par):
                act.wait_ge(t_done, t + 1)
                after(act, h_done, C * (t - 1))
                nc.scalar.copy(xeT[:, par, :], ps[TB[par]]).then_inc(t_copied, 1)

            def back(t, par):
                after(act, y_done, t)
                for c in range(0, C, 2):
                    act.wait_ge(h_done, C * t + c + 1)
                    nc.scalar.activation(hT[:, c, :], ps[HB[c]], ACT.Relu).then_inc(h_act, 1)

            skewed(act, E, front, back)

        @block.vector
        def _(dve):
            def back(t, par):
                after(dve, y_done, t)
                for c in range(1, C, 2):
                    dve.wait_ge(h_done, C * t + c + 1)
                    nc.vector.tensor_scalar(hT[:, c, :], ps[HB[c]], 0.0, None, ALU.max
                                            ).then_inc(h_dve, 1)
                dve.wait_ge(y_done, t + 1)
                after(dve, stored, 16 * t)
                nc.vector.tensor_copy(ye[:].rearrange("p s d -> p (s d)"), ps[YB[par]]
                                      ).then_inc(y_copied, 1)

            skewed(dve, E, lambda t, par: None, back)


RH = 8
SEQ = NB


def relative_setup(nc, ps, peT_dram, wr_dram, r_pad):
    with ExitStack() as ctx:
        peT = ctx.enter_context(nc.sbuf_tensor("rs_peT", [P, SEQ], F32))
        wr = ctx.enter_context(nc.sbuf_tensor("rs_wr", [P, RH * P], F32))
        loaded = nc.alloc_semaphore("rs_loaded")
        cleared = nc.alloc_semaphore("rs_cleared")
        made = nc.alloc_semaphore("rs_made")
        copied = nc.alloc_semaphore("rs_copied")
        block = ctx.enter_context(nc.Block())

        @block.sync
        def _(sp):
            sp.dma_start(peT[:], peT_dram).then_inc(loaded, 16)
            sp.dma_start(wr[:], wr_dram).then_inc(loaded, 16)

        @block.tensor
        def _(pe):
            pe.wait_ge(loaded, 32)
            for h in range(RH):
                last = nc.tensor.matmul(ps[0][:, h * SEQ:(h + 1) * SEQ], wr[:, h * P:(h + 1) * P], peT[:],
                                        start=True, stop=True)
            last.then_inc(made, 1)

        @block.vector
        def _(dve):
            nc.vector.memset(r_pad[:], 0.0).then_inc(cleared, 1)
            dve.wait_ge(cleared, 1)
            dve.wait_ge(made, 1)
            nc.vector.tensor_copy(r_pad[:, :, 0:SEQ],
                                  ps[0][:, 0:RH * SEQ].rearrange("p (h n) -> p h n", h=RH)
                                  ).then_inc(copied, 1)
            dve.wait_ge(copied, 1)


def relative_project_pass(nc, ps, w, ident, r_pad, x_res, p_tok, slot, ye_dram, hT, qT, x3_dram, pos_dram):
    with ExitStack() as ctx:
        def sb(nm, shape, dt=F32):
            return ctx.enter_context(nc.sbuf_tensor("rp_" + nm, shape, dt))

        def sem(nm):
            return nc.alloc_semaphore("rp_" + nm)

        wq = sb("wq", [P, RH * P])
        chan = sb("chan", [P, 2 + RH])
        minus_half = sb("minus_half", [P, 1])
        yg = sb("yg", [P, NB * P])
        res = sb("res", [P, P])
        stats = sb("stats", [P, 6])
        mv = sb("mv", [P, 2])
        ve = sb("ve", [P, 1])
        rstd = sb("rstd", [P, 1])
        x3 = sb("x3", [P, 2, P])
        stats2 = sb("stats2", [P, 6])
        mv2 = sb("mv2", [P, 2])
        ve2 = sb("ve2", [P, 1])
        rstd2 = sb("rstd2", [P, 1])
        hn = sb("hn", [P, P])
        hs = sb("hs", [P, 2, P])
        qv = sb("qv", [P, RH, P])
        pos = sb("pos", [P, 2, RH * SEQ])

        weights_in = sem("weights_in")
        consts = sem("consts")
        gathered = sem("gathered")
        var_done = sem("var_done")
        rstd_done = sem("rstd_done")
        x3_done = sem("x3_done")
        hn_done = sem("hn_done")
        link_sem = sem("link")
        t_done = sem("t_done")
        hs_done = sem("hs_done")
        h_kept = sem("h_kept")
        q_done = sem("q_done")
        q_kept = sem("q_kept")
        qv_done = sem("qv_done")
        pos_done = sem("pos_done")
        pos_copied = sem("pos_copied")
        x3_stored = [sem("x3_stored0"), sem("x3_stored1")]
        pos_stored = [sem("pos_stored0"), sem("pos_stored1")]
        TB, QB, PB = 0, ((1, 2), (3, 4)), (5, 6)
        block = ctx.enter_context(nc.Block())

        @block.sync
        def _(sp):
            sp.dma_start(wq[:], w["r_q"]).then_inc(weights_in, 16)
            sp.dma_start(chan[:], w["r_chan"]).then_inc(weights_in, 16)

            def front(t, par):
                sp.wait_ge(x3_done, t + 1)
                sp.dma_start(x3_dram[t], x3[:, par, :]).then_inc(x3_stored[par], 16)

            def back(t, par):
                sp.wait_ge(pos_copied, t + 1)
                sp.dma_start(pos_dram[t], pos[:, par, :]).then_inc(pos_stored[par], 16)

            skewed(sp, NB, front, back)
            for par in range(2):
                sp.wait_ge(x3_stored[par], 16 * NB // 2)
                sp.wait_ge(pos_stored[par], 16 * NB // 2)

        @block.gpsimd
        def _(pool):
            nc.gpsimd.memset(minus_half[:], -0.5).then_inc(consts, 1)
            for b in range(NB):
                nc.gpsimd.indirect_dma_start(
                    out=yg[:, b * P:(b + 1) * P], out_offset=None, in_=ye_dram[:, :],
                    in_offset=bass.IndirectOffsetOnAxis(ap=slot[:, b:b + 1], axis=0),
                    bounds_check=TOKENS, oob_is_err=False).then_inc(gathered, 16)
            pool.wait_ge(consts, 1)

            def front(t, par):
                pool.wait_ge(var_done, 2 * t + 1)
                nc.gpsimd.tensor_tensor(rstd[:], ve[:], minus_half[:], ALU.pow).then_inc(rstd_done, 1)
                pool.wait_ge(var_done, 2 * t + 2)
                nc.gpsimd.tensor_tensor(rstd2[:], ve2[:], minus_half[:], ALU.pow).then_inc(rstd_done, 1)

            skewed(pool, NB, front, lambda t, par: None)

        @block.vector
        def _(dve):
            dve.wait_ge(weights_in, 32)
            dve.wait_ge(gathered, 16 * NB)

            def front(t, par):
                link = Chain(dve, link_sem, t, 5)
                after(dve, hn_done, t)
                if not isinstance(t, int):
                    dve.nop(nofuse=True)
                link(nc.vector.scalar_tensor_tensor(
                    out=res[:], in0=yg[:, bass.ds(t * P, P)], scalar=p_tok[:, bass.ds(t, 1)],
                    in1=x_res[:, bass.ds(t * P, P)], op0=ALU.mult, op1=ALU.add))
                link(nc.vector.bn_stats(stats[:], res[:]), alone=True)
                link(nc.vector.bn_aggr(mv[:], stats[:]))
                nc.vector.tensor_scalar(ve[:], mv[:, 1:2], EPS, None, ALU.add).then_inc(var_done, 1)
                dve.wait_ge(rstd_done, 2 * t + 1)
                after(dve, x3_stored[par], 8 * (t - par))
                nc.vector.tensor_scalar(x3[:, par, :], res[:], mv[:, 0:1], rstd[:, 0:1],
                                        ALU.subtract, ALU.mult).then_inc(x3_done, 1)
                dve.wait_ge(x3_done, t + 1)
                link(nc.vector.bn_stats(stats2[:], x3[:, par, :]), alone=True)
                link(nc.vector.bn_aggr(mv2[:], stats2[:]))
                nc.vector.tensor_scalar(ve2[:], mv2[:, 1:2], EPS, None, ALU.add).then_inc(var_done, 1)
                dve.wait_ge(rstd_done, 2 * t + 2)
                after(dve, t_done, t)
                nc.vector.tensor_scalar(hn[:], x3[:, par, :], mv2[:, 0:1], rstd2[:, 0:1],
                                        ALU.subtract, ALU.mult).then_inc(hn_done, 1)
                link.end()

            def back(t, par):
                after(dve, pos_done, t)
                for n in range(2):
                    dve.wait_ge(q_kept, 2 * t + n + 1)
                    nc.vector.tensor_tensor(
                        qv[:, 4 * n:4 * n + 4, :], ps[QB[par][n]].rearrange("p (h t) -> p h t", h=4),
                        chan[:, 2 + 4 * n:6 + 4 * n].unsqueeze(2).to_broadcast([P, 4, P]), ALU.add
                    ).then_inc(qv_done, 1)
                after(dve, pos_stored[par], 8 * (t - par))
                dve.wait_ge(pos_done, t + 1)
                nc.vector.tensor_copy(pos[:, par, :], ps[PB[par]][:, 0:RH * SEQ]).then_inc(pos_copied, 1)

            skewed(dve, NB, front, back)

        @block.tensor
        def _(pe):
            pe.wait_ge(weights_in, 32)

            def front(t, par):
                pe.wait_ge(hn_done, t + 1)
                after(pe, hs_done, t)
                after(pe, h_kept, t)
                nc.tensor.transpose(ps[TB][:, 0:P], hn[:], ident[:]).then_inc(t_done, 1)

            def back(t, par):
                pe.wait_ge(hs_done, t + 1)
                after(pe, qv_done, 2 * t - 2)
                for n in range(2):
                    for j in range(4):
                        h = 4 * n + j
                        last = nc.tensor.matmul(ps[QB[par][n]][:, j * P:(j + 1) * P],
                                                wq[:, h * P:(h + 1) * P], hs[:, par, :],
                                                start=True, stop=True)
                    last.then_inc(q_done, 1)
                after(pe, pos_copied, t - 1)
                for n in range(2):
                    wait_alone(pe, qv_done, 2 * t + n + 1)
                    for h in range(4 * n, 4 * n + 4):
                        last = nc.tensor.matmul(ps[PB[par]][:, h * SEQ:(h + 1) * SEQ], qv[:, h, :],
                                                r_pad[:, h, bass.ds(SEQ - 1 - t, SEQ)],
                                                start=True, stop=True)
                last.then_inc(pos_done, 1)

            skewed(pe, NB, front, back)

        @block.scalar
        def _(act):
            act.wait_ge(weights_in, 32)

            def front(t, par):
                act.wait_ge(t_done, t + 1)
                after(act, q_done, 2 * t - 2)
                nc.scalar.activation(hs[:, par, :], ps[TB][:, 0:P], ACT.Identity,
                                     scale=chan[:, 0:1], bias=chan[:, 1:2]).then_inc(hs_done, 1)
                act.wait_ge(hs_done, t + 1)
                act.nop(nofuse=True)
                nc.scalar.copy(hT[:, bass.ds(t * P, P)], hs[:, par, :]).then_inc(h_kept, 1)

            def back(t, par):
                for n in range(2):
                    wait_alone(act, q_done, 2 * t + n + 1)
                    nc.scalar.copy(qT[:, 4 * n:4 * n + 4, bass.ds(t * P, P)],
                                   ps[QB[par][n]].rearrange("p (h t) -> p h t", h=4)).then_inc(q_kept, 1)

            skewed(act, NB, front, back)
            act.wait_ge(q_kept, 2 * NB)


def relative_attention_pass(nc, ps2, ps, w, hT, qT, x3_dram, pos_dram, x4_dram):
    POS = 4
    TURNS = P // POS
    with ExitStack() as ctx:
        def sb(nm, shape, dt=F32):
            return ctx.enter_context(nc.sbuf_tensor("ra_" + nm, shape, dt))

        def sem(nm):
            return nc.alloc_semaphore("ra_" + nm)

        wv = sb("wv", [P, RH * P])
        wo = sb("wo", [P, RH, P])
        u_bias = sb("u_bias", [P, RH])
        b_out = sb("b_out", [P, P])
        minus_half = sb("minus_half", [P, 1])
        hst = sb("hst", [P, P])
        kst = sb("kst", [P, RH, P])
        qu = sb("qu", [P, RH, P])
        v = sb("v", [P, 2, RH * P])
        pos = sb("pos", [P, 2, RH * SEQ])
        s = sb("s", [P, RH, SEQ])
        nmax = sb("nmax", [P, RH])
        rsum = sb("rsum", [P, RH])
        rinv = sb("rinv", [P, RH])
        pTb = sb("pTb", [P, 2, RH, P])
        oT = sb("oT", [P, RH, P])
        xr = sb("xr", [P, 2, P])
        res = sb("res", [P, P])
        stats = sb("stats", [P, 6])
        mv = sb("mv", [P, 2])
        ve = sb("ve", [P, 1])
        rstd = sb("rstd", [P, 1])
        x4 = sb("x4", [P, 2, P])

        weights_in = sem("weights_in")
        consts = sem("consts")
        pos_in = [sem("pos_in0"), sem("pos_in1")]
        xr_in = [sem("xr_in0"), sem("xr_in1")]
        h_staged = sem("h_staged")
        k_staged = sem("k_staged")
        qu_done = sem("qu_done")
        v_done = sem("v_done")
        v_copied = sem("v_copied")
        c_done = sem("c_done")
        s_done = sem("s_done")
        sub_done = sem("sub_done")
        exp_done = sem("exp_done")
        pt_done = sem("pt_done")
        pv_done = sem("pv_done")
        o_copied = sem("o_copied")
        op_done = sem("op_done")
        bout_done = sem("bout_done")
        res_done = sem("res_done")
        var_done = sem("var_done")
        rstd_done = sem("rstd_done")
        x4_done = sem("x4_done")
        stored = [sem("stored0"), sem("stored1")]
        front_link = sem("front_link")
        back_link = sem("back_link")
        VB, OB, PB = (0, 1), (4, 5), (6, 7)
        content = ps2
        SCALE = float(P) ** -0.5
        block = ctx.enter_context(nc.Block())

        @block.sync
        def _(sp):
            for dst, src in ((wv[:], w["r_v"]), (wo[:], w["r_out"].rearrange("(h f) d -> f h d", f=P)),
                             (u_bias[:], w["r_uT"]), (b_out[:], w["r_bout"].to_broadcast([P, P]))):
                sp.dma_start(dst, src).then_inc(weights_in, 16)

            def front(t, par):
                after(sp, s_done, t - 1)
                after(sp, res_done, t - 1)
                for p in range(POS):
                    rows = slice(p * SEQ, (p + 1) * SEQ)
                    sp.dma_start(pos[rows, par, :], pos_dram[:, bass.ds(t * POS + p, 1), :]
                                 .rearrange("i o c -> (i o) c")).then_inc(pos_in[par], 16)
                    sp.dma_start(xr[rows, par, :], x3_dram[:, bass.ds(t * POS + p, 1), :]
                                 .rearrange("i o c -> (i o) c")).then_inc(xr_in[par], 16)

            def back(t, par):
                sp.wait_ge(x4_done, t + 1)
                for p in range(POS):
                    rows = slice(p * SEQ, (p + 1) * SEQ)
                    sp.dma_start(x4_dram[:, bass.ds(t * POS + p, 1), :].rearrange("i o c -> (i o) c"),
                                 x4[rows, par, :]).then_inc(stored[par], 16)

            skewed(sp, TURNS, front, back)
            for par in range(2):
                sp.wait_ge(stored[par], 16 * POS * TURNS // 2)

        @block.gpsimd
        def _(pool):
            nc.gpsimd.memset(minus_half[:], -0.5).then_inc(consts, 1)
            nc.gpsimd.memset(pTb[:], 0.0).then_inc(consts, 1)
            pool.wait_ge(weights_in, 64)
            pool.wait_ge(consts, 2)

            def tile_of(src, t):
                return src.rearrange("f (i p) -> f p i", p=P)[:, bass.ds(t * POS, POS), :]

            def front(t, par):
                after(pool, v_done, 2 * t)
                if not isinstance(t, int):
                    pool.nop(nofuse=True)
                nc.gpsimd.tensor_copy(hst[:].rearrange("f (p i) -> f p i", p=POS), tile_of(hT[:], t)
                                      ).then_inc(h_staged, 1)
                after(pool, c_done, 2 * t)
                if not isinstance(t, int):
                    pool.nop(nofuse=True)
                for h in range(RH):
                    last = nc.gpsimd.tensor_copy(kst[:, h, :].rearrange("f (p i) -> f p i", p=POS),
                                                 tile_of(qT[:, h, :], t))
                last.then_inc(k_staged, 1)
                pool.wait_ge(k_staged, t + 1)
                nc.gpsimd.tensor_tensor(qu[:], kst[:], u_bias[:].unsqueeze(2).to_broadcast([P, RH, P]),
                                        ALU.add).then_inc(qu_done, 1)

            def back(t, par):
                pool.wait_ge(xr_in[par], 32 * (t - par) + 64)
                nc.gpsimd.tensor_tensor(xr[:, par, :], xr[:, par, :], b_out[:], ALU.add
                                        ).then_inc(bout_done, 1)
                pool.wait_ge(var_done, t + 1)
                nc.gpsimd.tensor_tensor(rstd[:], ve[:], minus_half[:], ALU.pow).then_inc(rstd_done, 1)

            skewed(pool, TURNS, front, back)

        @block.tensor
        def _(pe):
            pe.wait_ge(weights_in, 64)

            def front(t, par):
                pe.wait_ge(h_staged, t + 1)
                for n in range(2):
                    after(pe, v_copied, 2 * t - 1 + n)
                    nc.tensor.matmul(ps[VB[n]], hst[:], wv[:, n * BANK:(n + 1) * BANK],
                                     start=True, stop=True).then_inc(v_done, 1)
                pe.wait_ge(qu_done, t + 1)
                after(pe, s_done, t)
                for n in range(2):
                    for h in range(4 * n, 4 * n + 4):
                        last = nc.tensor.matmul(content[:, h * P:(h + 1) * P], qu[:, h, :], kst[:, h, :],
                                                start=True, stop=True)
                    last.then_inc(c_done, 1)

            def back(t, par):
                pe.wait_ge(pt_done, t + 1)
                pe.wait_ge(v_copied, 2 * t + 2)
                for n in range(2):
                    after(pe, o_copied, 2 * t - 1 + n)
                    for j in range(4):
                        h = 4 * n + j
                        last = nc.tensor.matmul(ps[OB[n]][:, j * P:(j + 1) * P],
                                                v[:, par, h * P:(h + 1) * P], pTb[:, par, h, :],
                                                start=True, stop=True)
                    last.then_inc(pv_done, 1)
                after(pe, res_done, t - 1)
                pe.wait_ge(o_copied, 2 * t + 2)
                for h in range(RH):
                    last = nc.tensor.matmul(ps[PB[par]][:, 0:P], oT[:, h, :], wo[:, h, :],
                                            start=(h == 0), stop=(h == RH - 1))
                last.then_inc(op_done, 1)

            skewed(pe, TURNS, front, back)

        @block.scalar
        def _(act):
            def front(t, par):
                after(act, pv_done, 2 * t - 2)
                for n in range(2):
                    act.wait_ge(v_done, 2 * t + n + 1)
                    nc.scalar.copy(v[:, par, n * BANK:(n + 1) * BANK], ps[VB[n]]).then_inc(v_copied, 1)
                act.wait_ge(sub_done, t + 1)
                nc.scalar.activation(s[:], s[:], ACT.Exp, scale=SCALE).then_inc(exp_done, 1)

            def back(t, par):
                after(act, op_done, t)
                for n in range(2):
                    act.wait_ge(pv_done, 2 * t + n + 1)
                    nc.scalar.copy(oT[:, 4 * n:4 * n + 4, :].rearrange("p h t -> p (h t)"), ps[OB[n]]
                                   ).then_inc(o_copied, 1)

            skewed(act, TURNS, front, back)

        @block.vector
        def _(dve):
            dve.wait_ge(weights_in, 64)
            dve.wait_ge(consts, 2)

            def front(t, par):
                link = Chain(dve, front_link, t, 4)
                after(dve, pt_done, t)
                dve.wait_ge(pos_in[par], 32 * (t - par) + 64)
                dve.wait_ge(c_done, 2 * t + 2)
                blocks = content.rearrange("r (h c) -> r h c", h=RH)
                for p in range(POS):
                    rows = slice(p * SEQ, (p + 1) * SEQ)
                    last = nc.vector.tensor_tensor(
                        s[rows], blocks[rows, :, rows],
                        pos[rows, par, :].rearrange("r (h j) -> r h j", h=RH), ALU.add)
                last.then_inc(s_done, 1)
                dve.wait_ge(s_done, t + 1)
                link(nc.vector.tensor_reduce(nmax[:], s[:], AX.X, ALU.max, negate=True))
                nc.vector.tensor_tensor(s[:], s[:], nmax[:].unsqueeze(2).to_broadcast([P, RH, SEQ]),
                                        ALU.add).then_inc(sub_done, 1)
                dve.wait_ge(exp_done, t + 1)
                link(nc.vector.tensor_reduce(rsum[:], s[:], AX.X, ALU.add))
                link(nc.vector.reciprocal(rinv[:], rsum[:]))
                link(nc.vector.tensor_tensor(s[:], s[:], rinv[:].unsqueeze(2).to_broadcast([P, RH, SEQ]),
                                             ALU.mult))
                after(dve, pv_done, 2 * t - 2)
                for p in range(POS):
                    rows = slice(p * SEQ, (p + 1) * SEQ)
                    last = nc.vector.transpose(pTb[rows, par, :, rows], s[rows])
                last.then_inc(pt_done, 1)
                link.end()

            def back(t, par):
                link = Chain(dve, back_link, t, 2)
                dve.wait_ge(op_done, t + 1)
                dve.wait_ge(bout_done, t + 1)
                after(dve, x4_done, t)
                nc.vector.tensor_tensor(res[:], ps[PB[par]][:, 0:P], xr[:, par, :], ALU.add
                                        ).then_inc(res_done, 1)
                dve.wait_ge(res_done, t + 1)
                link(nc.vector.bn_stats(stats[:], res[:]), alone=True)
                link(nc.vector.bn_aggr(mv[:], stats[:]))
                nc.vector.tensor_scalar(ve[:], mv[:, 1:2], EPS, None, ALU.add).then_inc(var_done, 1)
                dve.wait_ge(rstd_done, t + 1)
                after(dve, stored[par], 32 * (t - par))
                nc.vector.tensor_scalar(x4[:, par, :], res[:], mv[:, 0:1], rstd[:, 0:1],
                                        ALU.subtract, ALU.mult).then_inc(x4_done, 1)
                link.end()

            skewed(dve, TURNS, front, back)


def routed_linear_pass(nc, ps2s, ps, gate_dram, wexp_dram, ident, x_res, out):
    N = E * P
    with ExitStack() as ctx:
        def sb(nm, shape, dt=F32):
            return ctx.enter_context(nc.sbuf_tensor("l_" + nm, shape, dt))

        def sem(nm):
            return nc.alloc_semaphore("l_" + nm)

        wexp = sb("wexp", [P, N])
        gate = sb("gate", [P, E])
        order = sb("order", [P, E])
        minus_half = sb("minus_half", [P, 1])
        stage = sb("stage", [P, 2, P])
        xT = sb("xT", [P, 2, P])
        smax = sb("smax", [P, 8])
        val = sb("val", [P, E])
        vmax = sb("vmax", [P, 1])
        onehot = sb("onehot", [P, E])
        acc = sb("acc", [P, 2, P])
        stats = sb("stats", [P, 6])
        mv = sb("mv", [P, 2])
        ve = sb("ve", [P, 1])
        rstd = sb("rstd", [P, 1])
        y = sb("y", [P, 2, P])

        weights_in = sem("weights_in")
        consts = sem("consts")
        staged = sem("staged")
        t_done = sem("t_done")
        t_copied = sem("t_copied")
        g_done = sem("g_done")
        e_done = sem("e_done")
        doubled = sem("doubled")
        mixed = sem("mixed")
        var_done = sem("var_done")
        rstd_done = sem("rstd_done")
        y_done = sem("y_done")
        link_sem = sem("link")
        stored = [sem("stored0"), sem("stored1")]
        TB, GB = 0, (1, 6)
        block = ctx.enter_context(nc.Block())

        @block.sync
        def _(sp):
            sp.dma_start(wexp[:], wexp_dram).then_inc(weights_in, 16)
            sp.dma_start(gate[:], gate_dram).then_inc(weights_in, 16)

            def back(t, par):
                sp.wait_ge(y_done, t + 1)
                sp.dma_start(out[t], y[:, par, :]).then_inc(stored[par], 16)

            skewed(sp, NB, lambda t, par: None, back)
            for par in range(2):
                sp.wait_ge(stored[par], 16 * NB // 2)

        @block.gpsimd
        def _(pool):
            nc.gpsimd.memset(minus_half[:], -0.5)
            for e in range(E):
                last = nc.gpsimd.memset(order[:, e:e + 1], float(E - e))
            last.then_inc(consts, 1)
            pool.wait_ge(consts, 1)

            def back(t, par):
                pool.wait_ge(var_done, t + 1)
                nc.gpsimd.tensor_tensor(rstd[:], ve[:], minus_half[:], ALU.pow).then_inc(rstd_done, 1)

            skewed(pool, NB, lambda t, par: None, back)

        @block.scalar
        def _(act):
            def front(t, par):
                after(act, t_done, t - 1)
                after(act, doubled, t - 1)
                if not isinstance(t, int):
                    act.nop(nofuse=True)
                nc.scalar.copy(stage[:, par, :], x_res[:, bass.ds(t * P, P)]).then_inc(staged, 1)
                act.wait_ge(t_done, t + 1)
                after(act, e_done, t - 1)
                nc.scalar.copy(xT[:, par, :], ps[TB][:, 0:P]).then_inc(t_copied, 1)

            def back(t, par):
                after(act, mixed, t - 1)
                after(act, y_done, t - 1)
                act.wait_ge(staged, t + 1)
                nc.scalar.mul(acc[:, par, :], stage[:, par, :], 2.0).then_inc(doubled, 1)

            skewed(act, NB, front, back)

        @block.tensor
        def _(pe):
            pe.wait_ge(weights_in, 32)

            def front(t, par):
                pe.wait_ge(staged, t + 1)
                after(pe, t_copied, t)
                nc.tensor.transpose(ps[TB][:, 0:P], stage[:, par, :], ident[:]).then_inc(t_done, 1)

            def back(t, par):
                pe.wait_ge(t_copied, t + 1)
                after(pe, mixed, t - 1)
                nc.tensor.matmul(ps[GB[par]][:, 0:E], xT[:, par, :], gate[:],
                                 start=True, stop=True).then_inc(g_done, 1)
                for n in range(2):
                    last = nc.tensor.matmul(ps2s[par][:, n * BANK:(n + 1) * BANK], xT[:, par, :],
                                            wexp[:, n * BANK:(n + 1) * BANK], start=True, stop=True)
                last.then_inc(e_done, 1)

            skewed(pe, NB, front, back)

        @block.vector
        def _(dve):
            dve.wait_ge(weights_in, 32)
            dve.wait_ge(consts, 1)

            def back(t, par):
                link = Chain(dve, link_sem, t, 13)
                dve.wait_ge(e_done, t + 1)
                after(dve, y_done, t)
                scores = ps[GB[par]][:, 0:E]
                link(nc.vector.tensor_reduce(smax[:, 0:1], scores, AX.X, ALU.max))
                link(nc.vector.scalar_tensor_tensor(out=val[:], in0=scores, scalar=smax[:, 0:1],
                                                    in1=order[:], op0=ALU.is_equal, op1=ALU.mult))
                link(nc.vector.tensor_reduce(vmax[:], val[:], AX.X, ALU.max))
                link(nc.vector.tensor_scalar(onehot[:], val[:], vmax[:, 0:1], None, ALU.is_equal))
                dve.wait_ge(doubled, t + 1)
                for e in range(E):
                    ins = nc.vector.scalar_tensor_tensor(
                        out=acc[:, par, :], in0=ps2s[par][:, e * P:(e + 1) * P],
                        scalar=onehot[:, e:e + 1], in1=acc[:, par, :], op0=ALU.mult, op1=ALU.add)
                    if e < E - 1:
                        link(ins)
                ins.then_inc(mixed, 1)
                dve.wait_ge(mixed, t + 1)
                link(nc.vector.bn_stats(stats[:], acc[:, par, :]), alone=True)
                link(nc.vector.bn_aggr(mv[:], stats[:]))
                nc.vector.tensor_scalar(ve[:], mv[:, 1:2], EPS, None, ALU.add).then_inc(var_done, 1)
                dve.wait_ge(rstd_done, t + 1)
                after(dve, stored[par], 8 * (t - par))
                nc.vector.tensor_scalar(y[:, par, :], acc[:, par, :], mv[:, 0:1], rstd[:, 0:1],
                                        ALU.subtract, ALU.mult).then_inc(y_done, 1)
                link.end()

            skewed(dve, NB, lambda t, par: None, back)


def build(nc, a, out):
    def scratch(name, shape):
        return nc.dram_tensor(name, shape, F32, kind="Internal").ap()

    x1_dram = scratch("x1_scratch", (NB, P, P))
    x3_dram = scratch("x3_scratch", (NB, P, P))
    x4_dram = scratch("x4_scratch", (NB, P, P))
    xe_dram = scratch("xe_scratch", (TOKENS, P))
    ye_dram = scratch("ye_scratch", (TOKENS + 1, P))
    pos_dram = scratch("pos_scratch", (NB, P, RH * SEQ))
    with ExitStack() as ctx:
        banks = ctx.enter_context(nc.psum_tensor("banks", [P, 8 * BANK], F32))
        ps = [banks[:, i * BANK:(i + 1) * BANK] for i in range(8)]
        ident = ctx.enter_context(nc.sbuf_tensor("ident", [P, P], F32))
        x_res = ctx.enter_context(nc.sbuf_tensor("x_res", [P, NB * P], F32))
        p_tok = ctx.enter_context(nc.sbuf_tensor("p_tok", [P, NB], F32))
        slot = ctx.enter_context(nc.sbuf_tensor("slot", [P, NB], U32))
        ident_made = ctx.enter_context(nc.semaphore("ident_made"))
        with nc.Block() as block:
            @block.gpsimd
            def _(pool):
                make_identity(nc, pool, ident, ident_made)
                pool.wait_ge(ident_made, 2)

        def keep_x(t):
            return x_res[:, bass.ds(t * P, P)]

        with nc.cleanup_on_exit():
            mamba_pass(nc, ps, {"x": a["x"], "xT": a["xT"]}, a, x1_dram)
            cross_attention_pass(nc, ps, "xa0", x1_dram, a["ctxT"], {n: a["x0_" + n] for n in "qkvo"},
                                 P ** -0.5, a["bias"], ident, keep_x)
        with nc.cleanup_on_exit():
            routing_pass(nc, ps, a["wr"], ident, x_res, p_tok, slot, xe_dram, ye_dram)
            experts_pass(nc, ps, a["w1"], a["w2"], ident, xe_dram, ye_dram)
            with nc.sbuf_tensor("r_pad", [P, RH, 2 * SEQ], F32) as r_pad, \
                    nc.sbuf_tensor("qT", [P, RH, TOKENS], F32) as qT, \
                    nc.sbuf_tensor("hT", [P, TOKENS], F32) as hT:
                relative_setup(nc, ps, a["r_peT"], a["r_wr"], r_pad)
                relative_project_pass(nc, ps, a, ident, r_pad, x_res, p_tok, slot, ye_dram, hT, qT,
                                      x3_dram, pos_dram)
                relative_attention_pass(nc, banks[:, 2 * BANK:4 * BANK], ps, a, hT, qT, x3_dram,
                                        pos_dram, x4_dram)
        with nc.cleanup_on_exit():
            cross_attention_pass(nc, ps, "xa1", x4_dram, a["ctxT"], {n: a["x1_" + n] for n in "qkvo"},
                                 DH ** -0.5, None, ident, keep_x)
            routed_linear_pass(nc, [banks[:, i * BANK:(i + 2) * BANK] for i in (2, 4)], ps,
                               a["gateT"], a["wexpT"], ident, x_res, out)


def distance_table():
    pos = np.arange(SEQ, dtype=np.float32)[:, None]
    div = np.exp(np.arange(0, P, 2, dtype=np.float32) * np.float32(-math.log(10000.0) / P))
    ang = pos * div
    return np.stack([np.sin(ang), np.cos(ang)], axis=-1).reshape(SEQ, P)[::-1].T


def layout(inp):
    a = {k: np.asarray(v) for k, v in inp.items()}
    return {
        "x": a["x"], "xT": a["x"].reshape(TOKENS, P).T, "ctxT": a["ctx_1024"].reshape(TOKENS, P).T,
        "bias": a["fside_1x1xSxS2_0"].reshape(P, P),
        "W_inT": a["L0_attn_W_in"].T, "W_x": a["L0_attn_W_x"], "W_dtT": a["L0_attn_W_dt"].T,
        "W_outT": a["L0_attn_W_out"].T,
        "per_channel": np.concatenate(
            [a["L0_attn_conv_w"].reshape(2 * P, 4), a["L0_attn_conv_b"][:, None],
             a["L0_attn_b_dt"][:, None], a["L0_attn_D"][:, None]], axis=1),
        "x0_q": a["L0_xattn_Wq"].T, "x0_k": a["L0_xattn_Wk"].T, "x0_v": a["L0_xattn_Wv"].T,
        "x0_o": a["L0_xattn_Wp"].T,
        "wr": a["L0_ffn_Wr"], "w1": a["L0_ffn_W1"], "w2": a["L0_ffn_W2"],
        "r_q": a["L1_attn_Wq"], "r_v": a["L1_attn_Wv"], "r_wr": a["L1_attn_Wr"],
        "r_peT": distance_table(), "r_uT": a["L1_attn_u_bias"].T,
        "r_chan": np.concatenate([a["L1_attn_gamma"][:, None], a["L1_attn_beta"][:, None],
                                  a["L1_attn_v_bias"].T], axis=1),
        "r_bout": a["L1_attn_bout"].reshape(1, P), "r_out": a["L1_attn_Wout"],
        "x1_q": a["L1_xattn_w_q"], "x1_k": a["L1_xattn_w_k"], "x1_v": a["L1_xattn_w_v"],
        "x1_o": a["L1_xattn_w_o"],
        "gateT": a["L1_ffn_gate_w"].T,
        "wexpT": a["L1_ffn_expert_w"].transpose(2, 0, 1).reshape(P, E * P),
    }


def kernel(**inputs):
    import concourse.bacc as _bacc
    from concourse.bass_utils import run_bass_kernel_spmd as _run

    nc = _bacc.Bacc("TRN2", target_bir_lowering=False, num_devices=1)
    arrays, args = {}, {}

    def give(name, a):
        a = np.ascontiguousarray(a)
        arrays["in_" + name] = a
        args[name] = nc.dram_tensor("in_" + name, a.shape, mybir.dt.from_np(a.dtype),
                                    kind="ExternalInput").ap()

    for name, a in layout(inputs).items():
        give(name, a)
    out = nc.dram_tensor("out_0_dram", (NB, P, P), F32, kind="ExternalOutput").ap()
    build(nc, args, out)
    r = _run(nc, [arrays], core_ids=[0])
    return r.results[0]["out_0_dram"]
```

```python
from contextlib import ExitStack
import math

import numpy as np

import concourse.bass as bass
from concourse import mybir

F32 = mybir.dt.float32
BF16 = mybir.dt.bfloat16
I32 = mybir.dt.int32
U32 = mybir.dt.uint32
ALU = mybir.AluOpType
ACT = mybir.ActivationFunctionType
AX = mybir.AxisListType

P = 128
NB = 32
EPS = 1e-5
BANK = 512


def wait_alone(eng, sem, value):
    eng.wait_ge(sem, value)
    eng.nop(nofuse=True)


def after(eng, sem, value):
    if not isinstance(value, int) or value > 0:
        eng.wait_ge(sem, value)


def skewed(eng, turns, front, back):
    front(0, 0)
    front(1, 1)
    back(0, 0)
    front(2, 0)
    back(1, 1)
    with eng.Fori(1, turns // 2 - 1) as i:
        front(2 * i + 1, 1)
        back(2 * i, 0)
        front(2 * i + 2, 0)
        back(2 * i + 1, 1)
    front(turns - 1, 1)
    back(turns - 2, 0)
    back(turns - 1, 1)


def pipelined(eng, turns, steps):
    deepest = max(lag for lag, _ in steps)
    head = 2 * ((deepest + 3) // 2)

    def cycle(k, c):
        for lag, do in steps:
            if not isinstance(k, int) or 0 <= k - lag < turns:
                do(k - lag, (c - lag) % 2)

    for k in range(head):
        cycle(k, k)
    with eng.Fori(head // 2, turns // 2) as i:
        cycle(2 * i, 0)
        cycle(2 * i + 1, 1)
    for k in range(turns, turns + deepest):
        cycle(k, k)


def of(do, part):
    return lambda t, par: do(t, par, part)


class Chain:

    def __init__(self, eng, sem, turn, per_turn, before=0):
        self.eng, self.sem, self.per_turn = eng, sem, per_turn
        self.base = turn * per_turn + before
        self.n = 0

    def __call__(self, ins, alone=False):
        self.n += 1
        ins.then_inc(self.sem, 1)
        self.eng.wait_ge(self.sem, self.base + self.n)
        if alone:
            self.eng.nop(nofuse=True)

    def end(self):
        assert self.n == self.per_turn, (self.n, self.per_turn)


def make_identity(nc, pool, ident, sem):
    nc.gpsimd.memset(ident[:], 0.0).then_inc(sem, 1)
    pool.wait_ge(sem, 1)
    nc.gpsimd.affine_select(out=ident[:], in_=ident[:], compare_op=ALU.not_equal, fill=1.0, base=0,
                            pattern=[[-1, P]], channel_multiplier=1).then_inc(sem, 1)


def mamba_pass(nc, ps, dram, w, out):
    SEQS = 4
    T = SEQS * P
    TURNS = NB // SEQS
    PAD = 3
    with ExitStack() as ctx:
        def sb(name, shape, dt=F32):
            return ctx.enter_context(nc.sbuf_tensor("m_" + name, shape, dt))

        def sem(name):
            return nc.alloc_semaphore("m_" + name)

        w_in = sb("w_in", [P, 4 * P])
        w_x_dt = sb("w_x_dt", [P, 2, 2 * P])
        w_x_b = sb("w_x_b", [16, 2 * P])
        w_x_c = sb("w_x_c", [16, 2 * P])
        w_dt = sb("w_dt", [P, 2, 2 * P])
        w_out = sb("w_out", [P, 2, P])
        w_comb = sb("w_comb", [P, 2, 2 * P])
        w_gate = sb("w_gate", [P, 2, 2, P])
        per_channel = sb("per_channel", [P, 2, 7])
        conv_w = per_channel[:, :, 0:4]
        conv_b = per_channel[:, :, 4]
        b_dt = per_channel[:, :, 5]
        d_skip = per_channel[:, :, 6]
        sixteenth = sb("sixteenth", [16, P])
        minus_half = sb("minus_half", [P, SEQS])
        xT = sb("xT", [P, T])
        x_tok = sb("x_tok", [P, SEQS, P])
        xpad = sb("xpad", [P, 2, SEQS, PAD + P])
        conv = sb("conv", [P, 2, T])
        sig = sb("sig", [P, 2, T])
        sigz = sb("sigz", [P, 2, T])
        zs = sb("zs", [P, 2, 2, T])
        xc = sb("xc", [P, 2, 2, T])
        gate = sb("gate", [P, 2, 2, T])
        relu = sb("relu", [P, 2, T])
        soft = sb("soft", [P, 2, T])
        sp = sb("sp", [P, 2, T])
        g = sb("g", [P, 2, T])
        alpha = sb("alpha", [P, 2, T])
        alpha_c = sb("alpha_c", [P, 2, T])
        gated = sb("gated", [P, 2, T])
        hid = sb("hid", [P, 2, T])
        hc = sb("hc", [P, 2, T])
        y = sb("y", [P, 2, T])
        res = sb("res", [P, SEQS, P])
        stats = sb("stats", [P, SEQS, 6])
        mv = sb("mv", [P, SEQS, 2])
        ve = sb("ve", [P, SEQS])
        rstd = sb("rstd", [P, SEQS])
        x1 = sb("x1", [P, SEQS, P])

        weights_in = sem("weights_in")
        consts = sem("consts")
        wprod = sem("wprod")
        wcomb_ready = sem("wcomb_ready")
        xT_in = sem("xT_in")
        x_in = sem("x_in")
        inproj_done = sem("inproj_done")
        taps_ready = sem("taps_ready")
        conv_done = sem("conv_done")
        ez_done = sem("ez_done")
        ez_bound = sem("ez_bound")
        sigz_done = sem("sigz_done")
        zs_done = sem("zs_done")
        ec_done = sem("ec_done")
        ec_bound = sem("ec_bound")
        sig_done = sem("sig_done")
        xc_done = sem("xc_done")
        gate_sums = sem("gate_sums")
        gate_exp = sem("gate_exp")
        gate_bound = sem("gate_bound")
        gates = sem("gates")
        dt_done = sem("dt_done")
        absd = sem("absd")
        soft_done = sem("soft_done")
        sp_done = sem("sp_done")
        g_done = sem("g_done")
        alpha_done = sem("alpha_done")
        gated_done = sem("gated_done")
        scan_done = sem("scan_done")
        hc_done = sem("hc_done")
        yskip = sem("yskip")
        y_done = sem("y_done")
        out_done = sem("out_done")
        res_done = sem("res_done")
        var_done = sem("var_done")
        rstd_done = sem("rstd_done")
        x1_done = sem("x1_done")
        stored = sem("stored")
        relu_done = sem("relu_done")
        clipped = sem("clipped")
        sigz_link = sem("sigz_link")
        sig_link = sem("sig_link")
        soft_link = sem("soft_link")
        gate_link = sem("gate_link")
        alpha_link = sem("alpha_link")
        tap_link = sem("tap_link")
        clip_link = sem("clip_link")
        norm_link = sem("norm_link")
        g_link = sem("g_link")
        gated_link = sem("gated_link")

        XP, Z, DT, GT = (0, 1), (2, 3), (4, 5), (6, 7)
        OUT = 6
        LARGE = 1e18

        block = ctx.enter_context(nc.Block())
        WEIGHT_DMAS = 7

        @block.sync
        def _(sp_):
            for dst, src in (
                (w_in[:], w["W_inT"]),
                (per_channel[:], w["per_channel"].rearrange("(k p) t -> p k t", k=2)),
                (w_x_dt[:], w["W_x"][32:].rearrange("(k p) i -> p k i", k=2)),
                (w_dt[:], w["W_dtT"].rearrange("(k p) o -> p k o", k=2)),
                (w_x_b[:], w["W_x"][0:16]),
                (w_x_c[:], w["W_x"][16:32]),
                (w_out[:], w["W_outT"].rearrange("(k p) o -> p k o", k=2)),
            ):
                sp_.dma_start(dst, src).then_inc(weights_in, 16)

            def load_channels(t, par):
                after(sp_, inproj_done, 4 * t)
                sp_.dma_start(xT[:], dram["xT"][:, bass.ds(t * T, T)]).then_inc(xT_in, 16)

            def load_tokens(t, par):
                after(sp_, res_done, t)
                sp_.dma_start(x_tok[:], dram["x"][bass.ds(t * SEQS, SEQS)].rearrange("b s d -> s b d")
                              ).then_inc(x_in, 16)

            def store(t, par):
                sp_.wait_ge(x1_done, t + 1)
                sp_.dma_start(out[bass.ds(t * SEQS, SEQS)].rearrange("b s d -> s b d"), x1[:]
                              ).then_inc(stored, 16)

            pipelined(sp_, TURNS, ((0, load_channels), (3, store), (2, load_tokens)))
            sp_.wait_ge(stored, 16 * TURNS)

        @block.tensor
        def _(pe):
            pe.wait_ge(weights_in, 16 * WEIGHT_DMAS)
            pe.wait_ge(consts, 1)
            for k in range(2):
                for m in range(2):
                    last = nc.tensor.matmul(ps[k][:, 0:2 * P], w_x_dt[:, m, k * P:(k + 1) * P],
                                            w_dt[:, m, :], start=(m == 0), stop=(m == 1))
                last.then_inc(wprod, 1)
            for q, wx in enumerate((w_x_b, w_x_c)):
                for k in range(2):
                    last = nc.tensor.matmul(ps[2][:, (2 * k + q) * P:(2 * k + q + 1) * P],
                                            wx[:, k * P:(k + 1) * P], sixteenth[:],
                                            start=True, stop=True)
            last.then_inc(wprod, 1)
            pe.wait_ge(wcomb_ready, 3)

            def project(t, par, half):
                pe.wait_ge(xT_in, t * 16 + 16)
                for q in (2 * half, 2 * half + 1):
                    if half == 0:
                        after(pe, taps_ready, t * 2 - 1 + q)
                    else:
                        after(pe, zs_done, t * 2 - 3 + q)
                    nc.tensor.matmul(ps[(XP + Z)[q]], w_in[:, q * P:(q + 1) * P], xT[:],
                                     start=True, stop=True).then_inc(inproj_done, 1)

            def step_sums(t, par):
                pe.wait_ge(xc_done, t * 2 + 2)
                after(pe, sp_done, t * 2)
                for h, bank in enumerate(DT):
                    for k in range(2):
                        last = nc.tensor.matmul(ps[bank], w_comb[:, k, h * P:(h + 1) * P],
                                                xc[:, par, k, :], start=(k == 0), stop=(k == 1))
                    last.then_inc(dt_done, 1)

            def gate_sum(t, par):
                after(pe, res_done, t - 1)
                after(pe, gate_exp, t * 2)
                for q, bank in enumerate(GT):
                    for k in range(2):
                        last = nc.tensor.matmul(ps[bank], w_gate[:, k, q, :], xc[:, par, k, :],
                                                start=(k == 0), stop=(k == 1))
                    last.then_inc(gate_sums, 1)

            def project_out(t, par):
                last_turn = isinstance(t, int) and t == TURNS - 1
                pe.wait_ge(gate_exp, 2 * TURNS if last_turn else t * 2 + 3)
                pe.wait_ge(y_done, t * 2 + 2)
                for b in range(SEQS):
                    for k in range(2):
                        last = nc.tensor.matmul(ps[OUT][:, b * P:(b + 1) * P],
                                                y[:, k, b * P:(b + 1) * P], w_out[:, k, :],
                                                start=(k == 0), stop=(k == 1))
                last.then_inc(out_done, 1)

            pipelined(pe, TURNS, ((0, of(project, 0)), (1, step_sums), (0, of(project, 1)),
                                  (1, gate_sum), (2, project_out)))

        @block.scalar
        def _(act):
            nc.scalar.preload_act_table_set("natural_log_exp_and_others")
            for k in range(2):
                act.wait_ge(wprod, k + 1)
                nc.scalar.copy(w_comb[:, k, :], ps[k][:, 0:2 * P]).then_inc(wcomb_ready, 1)
            act.wait_ge(wprod, 3)
            nc.scalar.copy(w_gate[:].rearrange("p k q c -> p (k q c)"), ps[2]).then_inc(wcomb_ready, 1)
            act.wait_ge(consts, 3)

            def last_tap(t, par):
                for h in range(2):
                    act.wait_ge(inproj_done, t * 4 + h + 1)
                    after(act, xc_done, t * 2 - 1 + h)
                    nc.scalar.activation(conv[:, h, :], ps[XP[h]], ACT.Identity,
                                         bias=conv_b[:, h:h + 1], scale=conv_w[:, h, 3:4])
                    nc.scalar.copy(xpad[:, h, :, PAD:],
                                   ps[XP[h]].rearrange("p (b s) -> p b s", b=SEQS)
                                   ).then_inc(taps_ready, 1)

            def first_exps(t, par):
                for h in range(2):
                    act.wait_ge(inproj_done, t * 4 + 3 + h)
                    after(act, zs_done, t * 2 - 1 + h)
                    nc.scalar.activation(sigz[:, h, :], ps[Z[h]], ACT.Exp, scale=-1.0
                                         ).then_inc(ez_done, 1)
                for h in range(2):
                    act.wait_ge(conv_done, t * 2 + h + 1)
                    nc.scalar.activation(sig[:, h, :], conv[:, h, :], ACT.Exp, scale=-1.0
                                         ).then_inc(ec_done, 1)

            def sigmoids(t, par):
                for v, bound, link_sem, done in ((sigz, ez_bound, sigz_link, sigz_done),
                                                 (sig, ec_bound, sig_link, sig_done)):
                    link = Chain(act, link_sem, t, 2)
                    for h in range(2):
                        act.wait_ge(bound, t * 2 + h + 1)
                        link(nc.scalar.activation(v[:, h, :], v[:, h, :], ACT.Ln, bias=1.0))
                        nc.scalar.activation(v[:, h, :], v[:, h, :], ACT.Exp, scale=-1.0
                                             ).then_inc(done, 1)
                    link.end()

            def softness(t, par):
                link = Chain(act, soft_link, t, 2)
                after(act, sp_done, t * 2)
                for h in range(2):
                    act.wait_ge(dt_done, t * 2 + h + 1)
                    nc.scalar.activation(soft[:, h, :], ps[DT[h]], ACT.Abs, bias=b_dt[:, h:h + 1]
                                         ).then_inc(absd, 1)
                for h in range(2):
                    act.wait_ge(absd, t * 2 + h + 1)
                    link(nc.scalar.activation(soft[:, h, :], soft[:, h, :], ACT.Exp, scale=-1.0))
                    nc.scalar.activation(soft[:, h, :], soft[:, h, :], ACT.Ln, bias=1.0
                                         ).then_inc(soft_done, 1)
                link.end()

            def gate_exps(t, par):
                after(act, hc_done, t * 2 - 2)
                for q in range(2):
                    act.wait_ge(gate_sums, t * 2 + q + 1)
                    nc.scalar.activation(gate[:, par, q, :], ps[GT[q]], ACT.Exp, scale=-1.0
                                         ).then_inc(gate_exp, 1)

            def gate_ends(t, par):
                link = Chain(act, gate_link, t, 2)
                for q in range(2):
                    act.wait_ge(gate_bound, t * 2 + q + 1)
                    link(nc.scalar.activation(gate[:, par, q, :], gate[:, par, q, :], ACT.Ln, bias=1.0))
                    nc.scalar.activation(gate[:, par, q, :], gate[:, par, q, :], ACT.Exp, scale=-1.0
                                         ).then_inc(gates, 1)
                link.end()

            def alphas(t, par):
                link = Chain(act, alpha_link, t, 2)
                after(act, gated_done, t * 2)
                for h in range(2):
                    act.wait_ge(sp_done, t * 2 + h + 1)
                    nc.scalar.activation(g[:, h, :], sp[:, h, :], ACT.Exp, scale=-0.1
                                         ).then_inc(g_done, 1)
                after(act, clipped, t * 2)
                for h in range(2):
                    act.wait_ge(g_done, t * 2 + h + 1)
                    link(nc.scalar.activation(alpha[:, h, :], g[:, h, :], ACT.Ln, bias=1.0))
                    nc.scalar.activation(alpha[:, h, :], alpha[:, h, :], ACT.Exp, scale=-1.0
                                         ).then_inc(alpha_done, 1)
                link.end()

            pipelined(act, TURNS, ((0, last_tap), (1, softness), (0, first_exps), (1, alphas),
                                   (1, gate_exps), (0, sigmoids), (1, gate_ends)))

        @block.gpsimd
        def _(pool):
            nc.gpsimd.memset(sixteenth[:], 1.0 / 16).then_inc(consts, 1)
            nc.gpsimd.memset(xpad[:, :, :, 0:PAD], 0.0).then_inc(consts, 1)
            nc.gpsimd.memset(minus_half[:], -0.5).then_inc(consts, 1)
            pool.wait_ge(consts, 3)

            def gate_values(t, par):
                for h in range(2):
                    pool.wait_ge(scan_done, t * 2 + h + 1)
                    nc.gpsimd.tensor_tensor(hc[:, h, :], hid[:, h, :], gate[:, par, 1, :], ALU.mult
                                            ).then_inc(hc_done, 1)

            def gate_output(t, par):
                after(pool, out_done, t)
                for h in range(2):
                    pool.wait_ge(yskip, t * 2 + h + 1)
                    nc.gpsimd.tensor_tensor(y[:, h, :], hc[:, h, :], zs[:, par, h, :], ALU.mult
                                            ).then_inc(y_done, 1)

            def one_minus_alpha(t, par):
                link = Chain(pool, g_link, t, 2)
                for h in range(2):
                    pool.wait_ge(alpha_done, t * 2 + h + 1)
                    link(nc.gpsimd.tensor_tensor(g[:, h, :], g[:, h, :], alpha[:, h, :], ALU.mult))
                link.end()

            def gate_inputs(t, par):
                link = Chain(pool, gated_link, t, 2)
                after(pool, scan_done, t * 2)
                pool.wait_ge(gates, t * 2 + 2)
                for h in range(2):
                    link(nc.gpsimd.tensor_tensor(gated[:, h, :], xc[:, par, h, :], gate[:, par, 0, :],
                                                 ALU.mult))
                    nc.gpsimd.tensor_tensor(gated[:, h, :], gated[:, h, :], g[:, h, :], ALU.mult
                                            ).then_inc(gated_done, 1)
                link.end()

            def power(t, par):
                pool.wait_ge(var_done, t + 1)
                nc.gpsimd.tensor_tensor(rstd[:], ve[:], minus_half[:], ALU.pow).then_inc(rstd_done, 1)

            pipelined(pool, TURNS, ((2, gate_values), (2, gate_output), (1, one_minus_alpha),
                                    (1, gate_inputs), (2, power)))

        @block.vector
        def _(dve):
            dve.wait_ge(weights_in, 16 * WEIGHT_DMAS)

            def tap(t, h, k, ins_link):
                view = conv[:, h, :].rearrange("p (b s) -> p b s", b=SEQS)
                ins = nc.vector.scalar_tensor_tensor(
                    out=view, in0=xpad[:, h, :, k:k + P], scalar=conv_w[:, h, k:k + 1], in1=view,
                    op0=ALU.mult, op1=ALU.add)
                if ins_link is None:
                    ins.then_inc(conv_done, 1)
                else:
                    ins_link(ins)

            def middle_taps(t, par):
                link = Chain(dve, tap_link, t, 4)
                for k in (2, 1):
                    for h in range(2):
                        dve.wait_ge(taps_ready, t * 2 + h + 1)
                        tap(t, h, k, link)
                link.end()

            def first_tap(t, par):
                for h in range(2):
                    tap(t, h, 0, None)

            def bounds(t, par):
                for v, made, bound in ((sigz, ez_done, ez_bound), (sig, ec_done, ec_bound)):
                    for h in range(2):
                        dve.wait_ge(made, t * 2 + h + 1)
                        nc.vector.tensor_scalar(v[:, h, :], v[:, h, :], LARGE, None, ALU.min
                                                ).then_inc(bound, 1)

            def silus(t, par):
                after(dve, y_done, t * 2 - 2)
                for h in range(2):
                    dve.wait_ge(sigz_done, t * 2 + h + 1)
                    nc.vector.tensor_tensor(zs[:, par, h, :], ps[Z[h]], sigz[:, h, :], ALU.mult
                                            ).then_inc(zs_done, 1)
                after(dve, gated_done, t * 2 - 2)
                after(dve, gate_sums, t * 2 - 2)
                after(dve, yskip, t * 2 - 2)
                for h in range(2):
                    dve.wait_ge(sig_done, t * 2 + h + 1)
                    nc.vector.tensor_tensor(xc[:, par, h, :], conv[:, h, :], sig[:, h, :], ALU.mult
                                            ).then_inc(xc_done, 1)

            def relus(t, par):
                after(dve, sp_done, t * 2)
                for h in range(2):
                    dve.wait_ge(absd, t * 2 + h + 1)
                    nc.vector.tensor_scalar(relu[:, h, :], ps[DT[h]], b_dt[:, h:h + 1], 0.0,
                                            ALU.add, ALU.max).then_inc(relu_done, 1)

            def softplus(t, par):
                for h in range(2):
                    dve.wait_ge(relu_done, t * 2 + h + 1)
                    dve.wait_ge(soft_done, t * 2 + h + 1)
                    nc.vector.tensor_tensor(sp[:, h, :], relu[:, h, :], soft[:, h, :], ALU.add
                                            ).then_inc(sp_done, 1)

            def gate_bounds(t, par):
                for q in range(2):
                    dve.wait_ge(gate_exp, t * 2 + q + 1)
                    nc.vector.tensor_scalar(gate[:, par, q, :], gate[:, par, q, :], LARGE, None, ALU.min
                                            ).then_inc(gate_bound, 1)

            def clip(t, par):
                link = Chain(dve, clip_link, t, 2)
                after(dve, scan_done, t * 2)
                for h in range(2):
                    dve.wait_ge(alpha_done, t * 2 + h + 1)
                    link(nc.vector.tensor_scalar(alpha_c[:, h, :], alpha[:, h, :], 0.01, 0.99,
                                                 ALU.max, ALU.min))
                    nc.vector.memset(alpha_c[:, h, 0:T:P], 0.0).then_inc(clipped, 1)
                link.end()

            def scan(t, par):
                after(dve, hc_done, t * 2)
                dve.wait_ge(clipped, t * 2 + 2)
                for h in range(2):
                    dve.wait_ge(gated_done, t * 2 + h + 1)
                    nc.vector.tensor_tensor_scan(hid[:, h, :], alpha_c[:, h, :], gated[:, h, :], 0.0,
                                                 ALU.mult, ALU.add).then_inc(scan_done, 1)

            def skip(t, par):
                for h in range(2):
                    dve.wait_ge(hc_done, t * 2 + h + 1)
                    nc.vector.scalar_tensor_tensor(out=hc[:, h, :], in0=xc[:, par, h, :],
                                                   scalar=d_skip[:, h:h + 1], in1=hc[:, h, :],
                                                   op0=ALU.mult, op1=ALU.add).then_inc(yskip, 1)

            def residual(t, par):
                link = Chain(dve, norm_link, t, 2)
                after(dve, x1_done, t)
                dve.wait_ge(out_done, t + 1)
                dve.wait_ge(x_in, t * 16 + 16)
                nc.vector.tensor_tensor(res[:], ps[OUT].rearrange("p (b d) -> p b d", b=SEQS),
                                        x_tok[:], ALU.add).then_inc(res_done, 1)
                dve.wait_ge(res_done, t + 1)
                for b in range(SEQS):
                    ins = nc.vector.bn_stats(stats[:, b, :], res[:, b, :])
                link(ins, alone=True)
                for b in range(SEQS):
                    ins = nc.vector.bn_aggr(mv[:, b, :], stats[:, b, :])
                link(ins)
                nc.vector.tensor_scalar(ve[:], mv[:, :, 1], EPS, None, ALU.add).then_inc(var_done, 1)
                link.end()

            def norm(t, par):
                dve.wait_ge(rstd_done, t + 1)
                after(dve, stored, t * 16)
                for b in range(SEQS):
                    ins = nc.vector.tensor_scalar(x1[:, b, :], res[:, b, :], mv[:, b, 0:1],
                                                  rstd[:, b:b + 1], ALU.subtract, ALU.mult)
                ins.then_inc(x1_done, 1)

            pipelined(dve, TURNS, ((0, middle_taps), (1, relus), (0, first_tap), (1, softplus),
                                   (3, norm), (2, scan), (0, bounds), (1, clip), (2, skip),
                                   (1, gate_bounds), (0, silus), (2, residual)))


HEADS, DH = 16, 64
GROUP = 4
GROUPS = HEADS // GROUP


def cross_attention_pass(nc, ps, name, x_dram, ctxT_dram, w, scale, bias_dram, ident, x_out):
    with ExitStack() as ctx:
        def sb(nm, shape, dt=F32):
            return ctx.enter_context(nc.sbuf_tensor(f"{name}_{nm}", shape, dt))

        def sem(nm):
            return nc.alloc_semaphore(f"{name}_{nm}")

        wq = sb("wq", [P, HEADS * DH])
        wk = sb("wk", [P, HEADS * DH])
        wv = sb("wv", [P, HEADS * DH])
        wo = sb("wo", [P, HEADS // 2, P])
        bias = sb("bias", [P, P]) if bias_dram is not None else None
        minus_half = sb("minus_half", [P, 1])
        xa = sb("xa", [P, 2, P])
        xr = sb("xr", [P, P])
        ctxT = sb("ctxT", [P, 2, P])
        xT = sb("xT", [P, P])
        qT = sb("qT", [P, 2, 8, P])
        kT = sb("kT", [P, 2, 8, P])
        v = sb("v", [P, 2, HEADS * DH])
        ss = sb("ss", [P, GROUPS, GROUP, P]) if bias_dram is not None else None
        nmax = sb("nmax", [P, GROUPS, GROUP])
        prob = sb("prob", [P, GROUPS, GROUP, P])
        rsum = sb("rsum", [P, GROUPS, GROUP])
        rinv = sb("rinv", [P, GROUPS, GROUP])
        pT = sb("pT", [P, 2, GROUP, P])
        oT = sb("oT", [P, 8, P])
        res = sb("res", [P, P])
        stats = sb("stats", [P, 6])
        mv = sb("mv", [P, 2])
        ve = sb("ve", [P, 1])
        rstd = sb("rstd", [P, 1])

        weights_in = sem("weights_in")
        consts = sem("consts")
        xa_in = [sem("xa_in0"), sem("xa_in1")]
        xr_in = sem("xr_in")
        ctx_in = [sem("ctx_in0"), sem("ctx_in1")]
        fill_done = sem("fill_done")
        act_copied = sem("act_copied")
        v_copied = sem("v_copied")
        s_done = sem("s_done")
        biased = sem("biased")
        nmax_done = sem("nmax_done")
        exp_done = sem("exp_done")
        rinv_done = sem("rinv_done")
        norm_done = sem("norm_done")
        t_done = sem("t_done")
        pt_copied = sem("pt_copied")
        pv_done = sem("pv_done")
        ot_copied = sem("ot_copied")
        op_done = sem("op_done")
        res_done = sem("res_done")
        var_done = sem("var_done")
        rstd_done = sem("rstd_done")
        x_done = sem("x_done")
        ln_link = sem("ln_link")

        SC, PT, OT, FILL, OP = (0, 1), (2, 3), 4, (5, 6), 7
        n_weights = 4 + (bias is not None)

        block = ctx.enter_context(nc.Block())

        @block.sync
        def _(sp):
            for dst, src in (
                (wk[:], w["k"]), (wv[:], w["v"]), (wq[:], w["q"]),
                (wo[:], w["o"].rearrange("(j p) o -> p j o", p=P)),
            ):
                sp.dma_start(dst, src).then_inc(weights_in, 16)
            if bias is not None:
                sp.dma_start(bias[:], bias_dram).then_inc(weights_in, 16)

            def load_next(t, par):
                after(sp, fill_done, 7 * t - 13)
                sp.dma_start(xa[:, par, :], x_dram[t]).then_inc(xa_in[par], 16)
                after(sp, fill_done, 7 * t - 7)
                sp.dma_start(ctxT[:, par, :], ctxT_dram[:, bass.ds(t * P, P)]).then_inc(ctx_in[par], 16)

            def load_residual(t, par):
                after(sp, res_done, t)
                sp.dma_start(xr[:], x_dram[t]).then_inc(xr_in, 16)

            pipelined(sp, NB, ((0, load_next), (2, load_residual)))

        def bank_of(par, f):
            return FILL[(par + f) % 2]

        @block.tensor
        def _(pe):
            def fill(t, par, f):
                out = ps[bank_of(par, f)]
                if f == 0:
                    after(pe, v_copied, 2 * t - 1)
                    pe.wait_ge(xa_in[par], 8 * (t - par) + 16)
                    nc.tensor.transpose(out[:, 0:P], xa[:, par, :], ident[:]).then_inc(fill_done, 1)
                elif f in (1, 2, 3, 4):
                    if f == 1:
                        after(pe, v_copied, 2 * t)
                        pe.wait_ge(ctx_in[par], 8 * (t - par) + 16)
                    else:
                        pe.wait_ge(act_copied, 5 * t + f - 1)
                    half = (f - 1) % 2
                    weight, tokens = (wk, ctxT[:, par, :]) if f < 3 else (wq, xT[:])
                    for j in range(4):
                        pair = 4 * half + j
                        last = nc.tensor.matmul(out[:, j * P:(j + 1) * P],
                                                weight[:, pair * P:(pair + 1) * P], tokens,
                                                start=True, stop=True)
                    last.then_inc(fill_done, 1)
                else:
                    pe.wait_ge(act_copied, 5 * t + f - 1)
                    nc.tensor.matmul(out[:], ctxT[:, par, :], wv[:, (f - 5) * BANK:(f - 4) * BANK],
                                     start=True, stop=True).then_inc(fill_done, 1)

            def scores(t, par, g):
                after(pe, exp_done if bias is None else biased, 4 * t + g - 1)
                pe.wait_ge(act_copied, 5 * t + 5)
                for j in range(GROUP):
                    pair = GROUP * (g // 2) + j
                    r = DH * (g % 2)
                    last = nc.tensor.matmul(ps[SC[g % 2]][:, j * P:(j + 1) * P],
                                            qT[r:r + DH, par, pair, :], kT[r:r + DH, par, pair, :],
                                            start=True, stop=True)
                last.then_inc(s_done, 1)

            def transposes(t, par, g):
                pe.wait_ge(norm_done, 4 * t + g + 1)
                after(pe, pt_copied, 4 * t + g - 1)
                for j in range(GROUP):
                    last = nc.tensor.transpose(ps[PT[g % 2]][:, j * P:(j + 1) * P],
                                               prob[:, g, j, :], ident[:])
                last.then_inc(t_done, 1)

            def values(t, par, g):
                pe.wait_ge(pt_copied, 4 * t + g + 1)
                if g == 0:
                    after(pe, ot_copied, 2 * t)
                    pe.wait_ge(v_copied, 2 * t + 2)
                if g == 2:
                    pe.wait_ge(ot_copied, 2 * t + 1)
                for j in range(GROUP):
                    h = 2 * (GROUP * (g // 2) + j) + g % 2
                    r = DH * (g % 2)
                    last = nc.tensor.matmul(ps[OT][r:r + DH, j * P:(j + 1) * P],
                                            v[:, par, h * DH:(h + 1) * DH], pT[:, g % 2, j, :],
                                            start=True, stop=True)
                last.then_inc(pv_done, 1)

            def out_projection(t, par):
                pe.wait_ge(ot_copied, 2 * t + 2)
                after(pe, res_done, t)
                for j in range(8):
                    last = nc.tensor.matmul(ps[OP][:, 0:P], oT[:, j, :], wo[:, j, :],
                                            start=(j == 0), stop=(j == 7))
                last.then_inc(op_done, 1)

            pe.wait_ge(weights_in, 16 * n_weights)
            pipelined(pe, NB, (
                (2, of(scores, 2)), (3, of(values, 3)), (1, of(fill, 4)), (1, of(fill, 5)),
                (2, of(transposes, 0)),
                (2, of(scores, 3)), (3, out_projection), (2, of(values, 0)), (1, of(fill, 6)),
                (2, of(transposes, 1)),
                (1, of(scores, 0)), (2, of(values, 1)), (0, of(fill, 0)), (0, of(fill, 1)),
                (2, of(transposes, 2)),
                (1, of(scores, 1)), (2, of(values, 2)), (0, of(fill, 2)), (0, of(fill, 3)),
                (2, of(transposes, 3))))

        @block.scalar
        def _(act):
            def copy(t, par, f):
                act.wait_ge(fill_done, 7 * t + f + 1)
                src = ps[bank_of(par, f)]
                if f == 0:
                    after(act, fill_done, 7 * t - 2)
                    ins = nc.scalar.copy(xT[:], src[:, 0:P])
                elif f in (1, 2):
                    after(act, s_done, 4 * t - 4)
                    ins = nc.scalar.copy(kT[:, par, 4 * (f - 1):4 * f, :].rearrange("p j t -> p (j t)"),
                                         src[:])
                else:
                    after(act, s_done, 4 * t - 4)
                    ins = nc.scalar.mul(qT[:, par, 4 * (f - 3):4 * (f - 2), :]
                                        .rearrange("p j t -> p (j t)"), src[:], scale)
                ins.then_inc(act_copied, 1)

            def exps(t, par, g):
                act.wait_ge(nmax_done, 4 * t + g + 1)
                after(act, t_done, 4 * t + g - 3)
                after(act, rinv_done, 4 * t + g - 3)
                for j in range(GROUP):
                    src = ps[SC[g % 2]][:, j * P:(j + 1) * P] if bias is None else ss[:, g, j, :]
                    last = nc.scalar.activation(prob[:, g, j, :], src, ACT.Exp,
                                                bias=nmax[:, g, j:j + 1],
                                                accum_out=rsum[:, g, j:j + 1])
                last.then_inc(exp_done, 1)

            def copy_values(t, par, half):
                act.wait_ge(pv_done, 4 * t + 2 * half + 2)
                after(act, op_done, t)
                nc.scalar.copy(oT[:, 4 * half:4 * half + 4, :].rearrange("p j t -> p (j t)"),
                               ps[OT]).then_inc(ot_copied, 1)

            pipelined(act, NB, (
                (3, of(copy_values, 1)), (1, of(copy, 4)), (2, of(exps, 2)),
                (2, of(exps, 3)),
                (2, of(copy_values, 0)), (0, of(copy, 0)), (1, of(exps, 0)), (0, of(copy, 1)),
                (0, of(copy, 2)), (1, of(exps, 1)), (0, of(copy, 3))))

        @block.gpsimd
        def _(pool):
            nc.gpsimd.memset(minus_half[:], -0.5).then_inc(consts, 1)

            def normalise(t, par, g):
                pool.wait_ge(rinv_done, 4 * t + g + 1)
                nc.gpsimd.tensor_tensor(prob[:, g], prob[:, g],
                                        rinv[:, g, :].unsqueeze(2).to_broadcast([P, GROUP, P]),
                                        ALU.mult).then_inc(norm_done, 1)

            def power(t, par):
                pool.wait_ge(var_done, t + 1)
                nc.gpsimd.tensor_tensor(rstd[:], ve[:], minus_half[:], ALU.pow).then_inc(rstd_done, 1)

            pool.wait_ge(consts, 1)
            pipelined(pool, NB, (
                (2, of(normalise, 1)), (2, of(normalise, 2)), (2, of(normalise, 3)), (3, power),
                (1, of(normalise, 0))))

        @block.vector
        def _(dve):
            def copy_v(t, par, n):
                dve.wait_ge(fill_done, 7 * t + 6 + n)
                after(dve, pv_done, 4 * t - 4)
                nc.vector.tensor_copy(v[:, par, n * BANK:(n + 1) * BANK], ps[bank_of(par, 5 + n)]
                                      ).then_inc(v_copied, 1)

            def maxima(t, par, g):
                dve.wait_ge(s_done, 4 * t + g + 1)
                src = ps[SC[g % 2]].rearrange("p (j k) -> p j k", j=GROUP)
                after(dve, exp_done, 4 * t + g - 3)
                if bias is not None:
                    nc.vector.tensor_tensor(ss[:, g], src,
                                            bias[:].unsqueeze(1).to_broadcast([P, GROUP, P]), ALU.add
                                            ).then_inc(biased, 1)
                    dve.wait_ge(biased, 4 * t + g + 1)
                    src = ss[:, g]
                nc.vector.tensor_reduce(nmax[:, g, :], src, AX.X, ALU.max, negate=True
                                        ).then_inc(nmax_done, 1)

            def inverse(t, par, g):
                dve.wait_ge(exp_done, 4 * t + g + 1)
                after(dve, norm_done, 4 * t + g - 3)
                nc.vector.reciprocal(rinv[:, g, :], rsum[:, g, :]).then_inc(rinv_done, 1)

            def copy_pt(t, par, g):
                dve.wait_ge(t_done, 4 * t + g + 1)
                after(dve, pv_done, 4 * t + g - 1)
                nc.vector.tensor_copy(pT[:, g % 2].rearrange("p j t -> p (j t)"), ps[PT[g % 2]]
                                      ).then_inc(pt_copied, 1)

            def residual(t, par):
                link = Chain(dve, ln_link, t, 2)
                after(dve, x_done, t)
                dve.wait_ge(op_done, t + 1)
                dve.wait_ge(xr_in, 16 * t + 16)
                nc.vector.tensor_tensor(res[:], ps[OP][:, 0:P], xr[:], ALU.add).then_inc(res_done, 1)
                dve.wait_ge(res_done, t + 1)
                link(nc.vector.bn_stats(stats[:], res[:]), alone=True)
                link(nc.vector.bn_aggr(mv[:], stats[:]))
                nc.vector.tensor_scalar(ve[:], mv[:, 1:2], EPS, None, ALU.add).then_inc(var_done, 1)
                link.end()

            def norm(t, par):
                dve.wait_ge(rstd_done, t + 1)
                nc.vector.tensor_scalar(x_out(t), res[:], mv[:, 0:1], rstd[:, 0:1],
                                        ALU.subtract, ALU.mult).then_inc(x_done, 1)

            dve.wait_ge(weights_in, 16 * n_weights)
            pipelined(dve, NB, (
                (3, of(copy_pt, 3)), (2, of(maxima, 2)), (2, of(inverse, 1)), (1, of(copy_v, 0)),
                (2, of(copy_pt, 0)), (2, of(maxima, 3)), (2, of(inverse, 2)), (1, of(copy_v, 1)),
                (2, of(copy_pt, 1)), (1, of(maxima, 0)), (2, of(inverse, 3)), (3, residual),
                (2, of(copy_pt, 2)), (1, of(maxima, 1)), (1, of(inverse, 0)), (3, norm)))
            dve.wait_ge(x_done, NB)




E, F, CAP = 8, 512, NB * P // 8
TOKENS = NB * P


def routing_pass(nc, ps, wr_dram, ident, x_res, p_tok, slot, xe_dram, ye_dram):
    QUAD = 4
    with ExitStack() as ctx:
        def sb(nm, shape, dt=F32):
            return ctx.enter_context(nc.sbuf_tensor("r_" + nm, shape, dt))

        def sem(nm):
            return nc.alloc_semaphore("r_" + nm)

        wr = sb("wr", [P, E])
        zeros = sb("zeros", [P, BANK])
        stage = sb("stage", [P, BANK])
        xT = sb("xT", [P, BANK])
        logits = sb("logits", [P, NB, E])
        nmax = sb("nmax", [P, NB])
        diff = sb("diff", [P, NB, E])
        ex = sb("ex", [P, NB, E])
        esum = sb("esum", [P, NB])
        order = sb("order", [P, E])
        val = sb("val", [P, NB, E])
        vmax = sb("vmax", [P, NB])
        onehot = sb("onehot", [P, NB, E])
        onehot_h = sb("onehot_h", [P, NB, E], BF16)
        before = sb("before", [P, P], BF16)
        ones_h = sb("ones_h", [P, P], BF16)
        ones = sb("ones", [P, NB])
        upto = sb("upto", [P, NB, E])
        rank = sb("rank", [P, NB, E])
        picked = sb("picked", [P, NB, E])
        base = sb("base", [P, E])
        rank_tok = sb("rank_tok", [P, NB])
        base_tok = sb("base_tok", [P, NB])
        keep = sb("keep", [P, NB])
        slot_f = sb("slot_f", [P, NB])

        wr_in = sem("wr_in")
        consts = sem("consts")
        cleared = sem("cleared")
        staged = sem("staged")
        t_done = sem("t_done")
        t_copied = sem("t_copied")
        l_done = sem("l_done")
        l_copied = sem("l_copied")
        diff_done = sem("diff_done")
        ex_done = sem("ex_done")
        onehot_done = sem("onehot_done")
        ranks_done = sem("ranks_done")
        slot_done = sem("slot_done")
        scattered = sem("scattered")
        dve_link = sem("dve_link")
        n_consts = 8
        block = ctx.enter_context(nc.Block())

        @block.sync
        def _(sp):
            sp.dma_start(wr[:], wr_dram).then_inc(wr_in, 16)
            sp.wait_ge(consts, 1)
            for n in range(8):
                sp.dma_start(xe_dram[n * CAP:(n + 1) * CAP].rearrange("(p r) d -> p (r d)", p=P),
                             zeros[:]).then_inc(cleared, 16)
            sp.dma_start(ye_dram[TOKENS:TOKENS + 1], zeros[0:1, 0:P]).then_inc(cleared, 16)

        @block.gpsimd
        def _(pool):
            nc.gpsimd.memset(zeros[:], 0.0).then_inc(consts, 1)
            nc.gpsimd.memset(ones_h[:], 1.0).then_inc(consts, 1)
            nc.gpsimd.memset(ones[:], 1.0).then_inc(consts, 1)
            nc.gpsimd.memset(before[:], 1.0).then_inc(consts, 1)
            for e in range(E):
                nc.gpsimd.memset(order[:, e:e + 1], float(E - e))
                last = nc.gpsimd.memset(base[:, e:e + 1], float(CAP * e))
            last.then_inc(consts, 1)
            pool.wait_ge(consts, 5)
            nc.gpsimd.affine_select(out=before[:], in_=before[:], compare_op=ALU.is_gt, fill=0.0,
                                    base=0, pattern=[[1, P]], channel_multiplier=-1
                                    ).then_inc(consts, 3)
            pool.wait_ge(slot_done, 1)
            pool.wait_ge(cleared, 16 * 9)
            for b in range(NB):
                nc.gpsimd.indirect_dma_start(
                    out=xe_dram[:, :], out_offset=bass.IndirectOffsetOnAxis(ap=slot[:, b:b + 1], axis=0),
                    in_=x_res[:, b * P:(b + 1) * P], in_offset=None,
                    bounds_check=TOKENS - 1, oob_is_err=False).then_inc(scattered, 16)
            pool.wait_ge(scattered, 16 * NB)

        @block.scalar
        def _(act):
            with act.Fori(0, NB // QUAD) as i:
                act.wait_ge(t_done, i)
                act.nop(nofuse=True)
                nc.scalar.copy(stage[:], x_res[:, bass.ds(i * BANK, BANK)]).then_inc(staged, 1)
                act.wait_ge(t_done, i + 1)
                nc.scalar.copy(xT[:], ps[0]).then_inc(t_copied, 1)
            act.wait_ge(diff_done, 1)
            nc.scalar.activation(ex[:], diff[:], ACT.Exp).then_inc(ex_done, 1)

        @block.tensor
        def _(pe):
            pe.wait_ge(wr_in, 16)
            with pe.Fori(0, NB // QUAD) as i:
                pe.wait_ge(staged, i + 1)
                pe.wait_ge(t_copied, i)
                for j in range(QUAD):
                    last = nc.tensor.transpose(ps[0][:, j * P:(j + 1) * P], stage[:, j * P:(j + 1) * P],
                                               ident[:])
                last.then_inc(t_done, 1)
                pe.wait_ge(t_copied, i + 1)
                pe.wait_ge(l_copied, i)
                for j in range(QUAD):
                    last = nc.tensor.matmul(ps[1][:, j * E:(j + 1) * E], xT[:, j * P:(j + 1) * P], wr[:],
                                            start=True, stop=True)
                last.then_inc(l_done, 1)
            pe.wait_ge(onehot_done, 1)
            pe.wait_ge(consts, n_consts)
            oh = onehot_h[:].rearrange("p t e -> p (t e)")
            nc.tensor.matmul(ps[2][:, 0:NB * E], before[:], oh, start=True, stop=True)
            nc.tensor.matmul(ps[3][:, 0:NB * E], ones_h[:], oh, start=True, stop=True
                             ).then_inc(ranks_done, 1)

        @block.vector
        def _(dve):
            with dve.Fori(0, NB // QUAD) as i:
                wait_alone(dve, l_done, i + 1)
                nc.vector.tensor_copy(
                    logits[:].rearrange("p t e -> p (t e)")[:, bass.ds(i * QUAD * E, QUAD * E)],
                    ps[1][:, 0:QUAD * E]).then_inc(l_copied, 1)
            dve.wait_ge(l_copied, NB // QUAD)
            dve.wait_ge(consts, n_consts)
            link = Chain(dve, dve_link, 0, 18)

            def wide(v):
                return v.unsqueeze(2).to_broadcast([P, NB, E])

            def per_expert(v):
                return v.unsqueeze(1).to_broadcast([P, NB, E])

            link(nc.vector.tensor_reduce(nmax[:], logits[:], AX.X, ALU.max, negate=True))
            nc.vector.tensor_tensor(diff[:], logits[:], wide(nmax[:]), ALU.add).then_inc(diff_done, 1)
            dve.wait_ge(diff_done, 1)
            link(nc.vector.scalar_tensor_tensor(out=val[:], in0=diff[:], scalar=0.0,
                                                in1=per_expert(order[:]), op0=ALU.is_equal, op1=ALU.mult))
            link(nc.vector.tensor_reduce(vmax[:], val[:], AX.X, ALU.max))
            link(nc.vector.tensor_tensor(onehot[:], val[:], wide(vmax[:]), ALU.is_equal))
            nc.vector.tensor_copy(onehot_h[:], onehot[:]).then_inc(onehot_done, 1)
            dve.wait_ge(ex_done, 1)
            link(nc.vector.tensor_reduce(esum[:], ex[:], AX.X, ALU.add))
            link(nc.vector.reciprocal(p_tok[:], esum[:]))
            dve.wait_ge(ranks_done, 1)
            within = ps[2][:, 0:NB * E].rearrange("p (t e) -> p t e", e=E)
            total = ps[3][:, 0:NB * E].rearrange("p (t e) -> p t e", e=E)
            for e in range(E):
                ins = nc.vector.tensor_tensor_scan(upto[:, :, e], ones[:], total[:, :, e], 0.0,
                                                   ALU.mult, ALU.add)
            link(ins)
            link(nc.vector.tensor_tensor(rank[:], upto[:], total, ALU.subtract))
            link(nc.vector.tensor_tensor(rank[:], rank[:], within, ALU.add))
            link(nc.vector.tensor_tensor(picked[:], rank[:], onehot[:], ALU.mult))
            link(nc.vector.tensor_reduce(rank_tok[:], picked[:], AX.X, ALU.add))
            link(nc.vector.tensor_tensor(val[:], onehot[:], per_expert(base[:]), ALU.mult))
            link(nc.vector.tensor_reduce(base_tok[:], val[:], AX.X, ALU.add))
            link(nc.vector.tensor_scalar(keep[:], rank_tok[:], float(CAP), None, ALU.is_lt))
            link(nc.vector.tensor_tensor(slot_f[:], base_tok[:], rank_tok[:], ALU.add))
            link(nc.vector.scalar_tensor_tensor(out=slot_f[:], in0=slot_f[:], scalar=float(-TOKENS),
                                                in1=keep[:], op0=ALU.add, op1=ALU.mult))
            link(nc.vector.tensor_scalar(slot_f[:], slot_f[:], float(TOKENS), None, ALU.add))
            nc.vector.tensor_copy(slot[:], slot_f[:]).then_inc(slot_done, 1)
            dve.wait_ge(slot_done, 1)
            assert link.n <= 18


def experts_pass(nc, ps, w1_dram, w2_dram, ident, xe_dram, ye_dram):
    S = CAP // P
    C = F // P
    with ExitStack() as ctx:
        def sb(nm, shape, dt=F32):
            return ctx.enter_context(nc.sbuf_tensor("f_" + nm, shape, dt))

        def sem(nm):
            return nc.alloc_semaphore("f_" + nm)

        xe = sb("xe", [P, 2, S, P])
        w1 = sb("w1", [P, 2, F])
        w2 = sb("w2", [P, 2, C, P])
        xeT = sb("xeT", [P, 2, CAP])
        hT = sb("hT", [P, C, CAP])
        ye = sb("ye", [P, S, P])
        xe_in = [sem("xe_in0"), sem("xe_in1")]
        w_in = [sem("w_in0"), sem("w_in1")]
        t_done = sem("t_done")
        t_copied = sem("t_copied")
        h_done = sem("h_done")
        h_act = sem("h_act")
        h_dve = sem("h_dve")
        y_done = sem("y_done")
        y_copied = sem("y_copied")
        stored = sem("stored")
        TB, HB, YB = (0, 1), (2, 3, 4, 5), (6, 7)
        block = ctx.enter_context(nc.Block())

        @block.sync
        def _(sp):
            def front(t, par):
                after(sp, t_done, t - 1)
                sp.dma_start(xe[:, par], xe_dram[bass.ds(t * CAP, CAP)].rearrange("(s p) d -> p s d", p=P)
                             ).then_inc(xe_in[par], 16)
                after(sp, y_done, t - 1)
                sp.dma_start(w1[:, par, :], w1_dram[t]).then_inc(w_in[par], 16)
                sp.dma_start(w2[:, par], w2_dram[t].rearrange("(c f) d -> f c d", f=P)
                             ).then_inc(w_in[par], 16)

            def back(t, par):
                sp.wait_ge(y_copied, t + 1)
                sp.dma_start(ye_dram[bass.ds(t * CAP, CAP)].rearrange("(s p) d -> p s d", p=P), ye[:]
                             ).then_inc(stored, 16)

            skewed(sp, E, front, back)
            sp.wait_ge(stored, 16 * E)

        @block.tensor
        def _(pe):
            def front(t, par):
                pe.wait_ge(xe_in[par], 8 * (t - par) + 16)
                after(pe, t_copied, t - 1)
                for s in range(S):
                    last = nc.tensor.transpose(ps[TB[par]][:, s * P:(s + 1) * P], xe[:, par, s, :], ident[:])
                last.then_inc(t_done, 1)

            def back(t, par):
                pe.wait_ge(t_copied, t + 1)
                pe.wait_ge(w_in[par], 16 * (t - par) + 32)
                for c in range(C):
                    after(pe, h_act if c % 2 == 0 else h_dve, (C // 2) * (t - 1) + c // 2 + 1)
                    nc.tensor.matmul(ps[HB[c]], w1[:, par, c * P:(c + 1) * P], xeT[:, par, :],
                                     start=True, stop=True).then_inc(h_done, 1)
                pe.wait_ge(h_act, (C // 2) * (t + 1))
                pe.wait_ge(h_dve, (C // 2) * (t + 1))
                after(pe, y_copied, t - 1)
                for s in range(S):
                    for c in range(C):
                        last = nc.tensor.matmul(ps[YB[par]][:, s * P:(s + 1) * P],
                                                hT[:, c, s * P:(s + 1) * P], w2[:, par, c, :],
                                                start=(c == 0), stop=(c == C - 1))
                last.then_inc(y_done, 1)

            skewed(pe, E, front, back)

        @block.scalar
        def _(act):
            def front(t, par):
                act.wait_ge(t_done, t + 1)
                after(act, h_done, C * (t - 1))
                nc.scalar.copy(xeT[:, par, :], ps[TB[par]]).then_inc(t_copied, 1)

            def back(t, par):
                after(act, y_done, t)
                for c in range(0, C, 2):
                    act.wait_ge(h_done, C * t + c + 1)
                    nc.scalar.activation(hT[:, c, :], ps[HB[c]], ACT.Relu).then_inc(h_act, 1)

            skewed(act, E, front, back)

        @block.vector
        def _(dve):
            def back(t, par):
                after(dve, y_done, t)
                for c in range(1, C, 2):
                    dve.wait_ge(h_done, C * t + c + 1)
                    nc.vector.tensor_scalar(hT[:, c, :], ps[HB[c]], 0.0, None, ALU.max
                                            ).then_inc(h_dve, 1)
                dve.wait_ge(y_done, t + 1)
                after(dve, stored, 16 * t)
                nc.vector.tensor_copy(ye[:].rearrange("p s d -> p (s d)"), ps[YB[par]]
                                      ).then_inc(y_copied, 1)

            skewed(dve, E, lambda t, par: None, back)


RH = 8
SEQ = NB


def relative_setup(nc, ps, peT_dram, wr_dram, r_pad):
    with ExitStack() as ctx:
        peT = ctx.enter_context(nc.sbuf_tensor("rs_peT", [P, SEQ], F32))
        wr = ctx.enter_context(nc.sbuf_tensor("rs_wr", [P, RH * P], F32))
        loaded = nc.alloc_semaphore("rs_loaded")
        cleared = nc.alloc_semaphore("rs_cleared")
        made = nc.alloc_semaphore("rs_made")
        copied = nc.alloc_semaphore("rs_copied")
        block = ctx.enter_context(nc.Block())

        @block.sync
        def _(sp):
            sp.dma_start(peT[:], peT_dram).then_inc(loaded, 16)
            sp.dma_start(wr[:], wr_dram).then_inc(loaded, 16)

        @block.tensor
        def _(pe):
            pe.wait_ge(loaded, 32)
            for h in range(RH):
                last = nc.tensor.matmul(ps[0][:, h * SEQ:(h + 1) * SEQ], wr[:, h * P:(h + 1) * P], peT[:],
                                        start=True, stop=True)
            last.then_inc(made, 1)

        @block.vector
        def _(dve):
            nc.vector.memset(r_pad[:], 0.0).then_inc(cleared, 1)
            dve.wait_ge(cleared, 1)
            dve.wait_ge(made, 1)
            nc.vector.tensor_copy(r_pad[:, :, 0:SEQ],
                                  ps[0][:, 0:RH * SEQ].rearrange("p (h n) -> p h n", h=RH)
                                  ).then_inc(copied, 1)
            dve.wait_ge(copied, 1)


def relative_project_pass(nc, ps, w, ident, r_pad, x_res, p_tok, slot, ye_dram, qT, x3_dram, pos_dram):
    G = 4
    TURNS = NB // G
    with ExitStack() as ctx:
        def sb(nm, shape, dt=F32):
            return ctx.enter_context(nc.sbuf_tensor("rp_" + nm, shape, dt))

        def sem(nm):
            return nc.alloc_semaphore("rp_" + nm)

        wq = sb("wq", [P, RH * P])
        chan = sb("chan", [P, 2 + RH])
        minus_half = sb("minus_half", [P, G])
        yg = sb("yg", [P, NB * P])
        res = sb("res", [P, G, P])
        stats = sb("stats", [P, G, 6])
        mv = sb("mv", [P, G, 2])
        ve = sb("ve", [P, G])
        rstd = sb("rstd", [P, G])
        x3 = sb("x3", [P, 2, G, P])
        stats2 = sb("stats2", [P, G, 6])
        mv2 = sb("mv2", [P, G, 2])
        ve2 = sb("ve2", [P, G])
        rstd2 = sb("rstd2", [P, G])
        hn = sb("hn", [P, G, P])
        qv = sb("qv", [P, 4, G * P])
        pos = sb("pos", [P, 2, G, RH * SEQ])

        weights_in = sem("weights_in")
        consts = sem("consts")
        gathered = sem("gathered")
        res_link = sem("res_link")
        norm_link = sem("norm_link")
        var_done = sem("var_done")
        rstd_done = sem("rstd_done")
        x3_done = sem("x3_done")
        hn_done = sem("hn_done")
        t_done = sem("t_done")
        h_kept = sem("h_kept")
        q_done = sem("q_done")
        q_kept = sem("q_kept")
        qv_done = sem("qv_done")
        pos_done = sem("pos_done")
        pos_copied = sem("pos_copied")
        x3_stored = [sem("x3_stored0"), sem("x3_stored1")]
        pos_stored = [sem("pos_stored0"), sem("pos_stored1")]
        TB, QB, PB = 0, (1, 2, 3, 4), (5, 6)
        block = ctx.enter_context(nc.Block())

        def by_token(dram, t):
            return dram[bass.ds(G * t, G)].rearrange("i p c -> p i c")

        @block.sync
        def _(sp):
            sp.dma_start(wq[:], w["r_q"]).then_inc(weights_in, 16)
            sp.dma_start(chan[:], w["r_chan"]).then_inc(weights_in, 16)

            def store_x3(t, par):
                sp.wait_ge(x3_done, t + 1)
                sp.dma_start(by_token(x3_dram, t), x3[:, par]).then_inc(x3_stored[par], 16)

            def store_pos(t, par):
                sp.wait_ge(pos_copied, 2 * t + 2)
                sp.dma_start(by_token(pos_dram, t), pos[:, par]).then_inc(pos_stored[par], 16)

            pipelined(sp, TURNS, ((0, store_x3), (1, store_pos)))
            for par in range(2):
                sp.wait_ge(x3_stored[par], 16 * TURNS // 2)
                sp.wait_ge(pos_stored[par], 16 * TURNS // 2)

        @block.gpsimd
        def _(pool):
            nc.gpsimd.memset(minus_half[:], -0.5).then_inc(consts, 1)
            for b in range(NB):
                nc.gpsimd.indirect_dma_start(
                    out=yg[:, b * P:(b + 1) * P], out_offset=None, in_=ye_dram[:, :],
                    in_offset=bass.IndirectOffsetOnAxis(ap=slot[:, b:b + 1], axis=0),
                    bounds_check=TOKENS, oob_is_err=False).then_inc(gathered, 16)
            pool.wait_ge(consts, 1)

            def rstds(t, par):
                pool.wait_ge(var_done, 2 * t + 1)
                nc.gpsimd.tensor_tensor(rstd[:], ve[:], minus_half[:], ALU.pow).then_inc(rstd_done, 1)
                pool.wait_ge(var_done, 2 * t + 2)
                nc.gpsimd.tensor_tensor(rstd2[:], ve2[:], minus_half[:], ALU.pow).then_inc(rstd_done, 1)

            pipelined(pool, TURNS, ((0, rstds),))

        @block.vector
        def _(dve):
            dve.wait_ge(weights_in, 32)
            dve.wait_ge(gathered, 16 * NB)

            def residual(t, par):
                link = Chain(dve, res_link, t, 3)
                after(dve, hn_done, t)
                if not isinstance(t, int):
                    dve.nop(nofuse=True)
                for j in range(G):
                    last = nc.vector.scalar_tensor_tensor(
                        out=res[:, j, :], in0=yg[:, bass.ds((G * t + j) * P, P)],
                        scalar=p_tok[:, bass.ds(G * t + j, 1)],
                        in1=x_res[:, bass.ds((G * t + j) * P, P)], op0=ALU.mult, op1=ALU.add)
                link(last)
                for j in range(G):
                    last = nc.vector.bn_stats(stats[:, j, :], res[:, j, :])
                link(last, alone=True)
                for j in range(G):
                    last = nc.vector.bn_aggr(mv[:, j, :], stats[:, j, :])
                link(last)
                nc.vector.tensor_scalar(ve[:], mv[:, :, 1], EPS, None, ALU.add).then_inc(var_done, 1)
                link.end()

            def residual_norm(t, par):
                link = Chain(dve, norm_link, t, 2)
                after(dve, x3_stored[par], 8 * (t - par))
                dve.wait_ge(rstd_done, 2 * t + 1)
                for j in range(G):
                    last = nc.vector.tensor_scalar(x3[:, par, j, :], res[:, j, :], mv[:, j, 0:1],
                                                   rstd[:, j:j + 1], ALU.subtract, ALU.mult)
                last.then_inc(x3_done, 1)
                dve.wait_ge(x3_done, t + 1)
                for j in range(G):
                    last = nc.vector.bn_stats(stats2[:, j, :], x3[:, par, j, :])
                link(last, alone=True)
                for j in range(G):
                    last = nc.vector.bn_aggr(mv2[:, j, :], stats2[:, j, :])
                link(last)
                nc.vector.tensor_scalar(ve2[:], mv2[:, :, 1], EPS, None, ALU.add).then_inc(var_done, 1)
                link.end()

            def second_norm(t, par):
                after(dve, t_done, t)
                dve.wait_ge(rstd_done, 2 * t + 2)
                for j in range(G):
                    last = nc.vector.tensor_scalar(hn[:, j, :], x3[:, par, j, :], mv2[:, j, 0:1],
                                                   rstd2[:, j:j + 1], ALU.subtract, ALU.mult)
                last.then_inc(hn_done, 1)

            def add_v(first, end):
                def heads(t, par):
                    for h in range(first, end):
                        after(dve, pos_done, RH * t + h - 3)
                        dve.wait_ge(q_kept, RH * t + h + 1)
                        nc.vector.tensor_scalar(qv[:, h % 4, :], ps[QB[h % 4]], chan[:, 2 + h:3 + h],
                                                None, ALU.add).then_inc(qv_done, 1)
                return heads

            pipelined(dve, TURNS, ((1, add_v(0, 2)), (0, residual), (1, add_v(2, 4)),
                                   (0, residual_norm), (1, add_v(4, 6)), (0, second_norm),
                                   (1, add_v(6, 8))))

        @block.tensor
        def _(pe):
            pe.wait_ge(weights_in, 32)

            def transposes(t, par):
                after(pe, h_kept, t)
                pe.wait_ge(hn_done, t + 1)
                for j in range(G):
                    last = nc.tensor.transpose(ps[TB][:, j * P:(j + 1) * P], hn[:, j, :], ident[:])
                last.then_inc(t_done, 1)

            def queries(t, h):
                after(pe, qv_done, RH * t + h - 3)
                if h == 0:
                    wait_alone(pe, h_kept, t + 1)
                nc.tensor.matmul(ps[QB[h % 4]], wq[:, h * P:(h + 1) * P],
                                 x_res[:, bass.ds(t * G * P, G * P)], start=True, stop=True
                                 ).then_inc(q_done, 1)

            def positions(t, h):
                wait_alone(pe, qv_done, RH * t + h + 1)
                for j in range(G):
                    bank = ps[PB[j // 2]][:, (j % 2) * RH * SEQ:(j % 2 + 1) * RH * SEQ]
                    last = nc.tensor.matmul(bank[:, h * SEQ:(h + 1) * SEQ],
                                            qv[:, h % 4, j * P:(j + 1) * P],
                                            r_pad[:, h, bass.ds(SEQ - 1 - G * t - j, SEQ)],
                                            start=True, stop=True)
                last.then_inc(pos_done, 1)

            def all_but_last(t, par):
                queries(t, 0)
                for h in range(1, RH):
                    queries(t, h)
                    if h == 1:
                        after(pe, pos_copied, 2 * t)
                    positions(t, h - 1)

            pipelined(pe, TURNS, ((1, all_but_last), (0, transposes),
                                  (1, lambda t, par: positions(t, RH - 1))))

        @block.scalar
        def _(act):
            act.wait_ge(weights_in, 32)

            def keep_h(t, par):
                wait_alone(act, t_done, t + 1)
                nc.scalar.activation(x_res[:, bass.ds(t * G * P, G * P)], ps[TB], ACT.Identity,
                                     scale=chan[:, 0:1], bias=chan[:, 1:2]).then_inc(h_kept, 1)

            def keep_q(t, par):
                for h in range(RH):
                    wait_alone(act, q_done, RH * t + h + 1)
                    by_position = qT[:, h, :].rearrange("f (p i) -> f i p", i=NB)
                    nc.scalar.copy(by_position[:, bass.ds(G * t, G), :],
                                   ps[QB[h % 4]].rearrange("f (i p) -> f i p", i=G)).then_inc(q_kept, 1)

            def copy_pos(t, par):
                after(act, pos_stored[par], 8 * (t - par))
                act.wait_ge(pos_done, RH * t + RH)
                for n in range(2):
                    nc.scalar.copy(pos[:, par, 2 * n:2 * n + 2, :].rearrange("r i c -> r (i c)"),
                                   ps[PB[n]]).then_inc(pos_copied, 1)

            pipelined(act, TURNS, ((1, keep_q), (0, keep_h), (1, copy_pos)))
            act.wait_ge(q_kept, RH * TURNS)


def relative_attention_pass(nc, ps2, ps, w, hT, qT, x3_dram, pos_dram, x4_dram):
    POS = 4
    TURNS = P // POS
    with ExitStack() as ctx:
        def sb(nm, shape, dt=F32):
            return ctx.enter_context(nc.sbuf_tensor("ra_" + nm, shape, dt))

        def sem(nm):
            return nc.alloc_semaphore("ra_" + nm)

        wv = sb("wv", [P, RH * P])
        wo = sb("wo", [P, RH, P])
        u_bias = sb("u_bias", [P, RH])
        b_out = sb("b_out", [P, P])
        minus_half = sb("minus_half", [P, 1])
        hst = sb("hst", [P, 2, P])
        qu = sb("qu", [P, 2, RH, P])
        v = sb("v", [P, 2, RH * P])
        pos = sb("pos", [P, 2, RH * SEQ])
        s = sb("s", [P, RH, SEQ])
        nmax = sb("nmax", [P, RH])
        rsum = sb("rsum", [P, RH])
        rinv = sb("rinv", [P, RH])
        pTb = sb("pTb", [P, 2, RH, P])
        oT = sb("oT", [P, 2, RH, P])
        xr = sb("xr", [P, 2, P])
        res = sb("res", [P, P])
        stats = sb("stats", [P, 6])
        mv = sb("mv", [P, 2])
        ve = sb("ve", [P, 1])
        rstd = sb("rstd", [P, 1])
        x4 = sb("x4", [P, 2, P])

        weights_in = sem("weights_in")
        consts = sem("consts")
        pos_in = [sem("pos_in0"), sem("pos_in1")]
        xr_in = [sem("xr_in0"), sem("xr_in1")]
        h_staged = sem("h_staged")
        qu_done = sem("qu_done")
        v_done = sem("v_done")
        v_copied = sem("v_copied")
        c_done = sem("c_done")
        s_done = sem("s_done")
        max_done = sem("max_done")
        sub_done = sem("sub_done")
        exp_done = sem("exp_done")
        pt_done = sem("pt_done")
        pv_done = sem("pv_done")
        o_copied = sem("o_copied")
        op_done = sem("op_done")
        bout_done = sem("bout_done")
        res_done = sem("res_done")
        var_done = sem("var_done")
        rstd_done = sem("rstd_done")
        x4_done = sem("x4_done")
        stored = [sem("stored0"), sem("stored1")]
        soft_link = sem("soft_link")
        norm_link = sem("norm_link")
        VB, OB, PB = (0, 1), (4, 5), (6, 7)
        content = ps2
        SCALE = float(P) ** -0.5
        block = ctx.enter_context(nc.Block())

        @block.sync
        def _(sp):
            for dst, src in ((wv[:], w["r_v"]), (wo[:], w["r_out"].rearrange("(h f) d -> f h d", f=P)),
                             (u_bias[:], w["r_uT"]), (b_out[:], w["r_bout"].to_broadcast([P, P]))):
                sp.dma_start(dst, src).then_inc(weights_in, 16)

            def tile_rows(dram, t, p):
                return dram[:, bass.ds(t * POS + p, 1), :].rearrange("i o c -> (i o) c")

            def load_pos(t, par):
                after(sp, s_done, t - 1)
                for p in range(POS):
                    sp.dma_start(pos[p * SEQ:(p + 1) * SEQ, par, :], tile_rows(pos_dram, t, p)
                                 ).then_inc(pos_in[par], 16)

            def load_xr(t, par):
                after(sp, res_done, t - 1)
                for p in range(POS):
                    sp.dma_start(xr[p * SEQ:(p + 1) * SEQ, par, :], tile_rows(x3_dram, t, p)
                                 ).then_inc(xr_in[par], 16)

            def store(t, par):
                sp.wait_ge(x4_done, t + 1)
                for p in range(POS):
                    sp.dma_start(tile_rows(x4_dram, t, p), x4[p * SEQ:(p + 1) * SEQ, par, :]
                                 ).then_inc(stored[par], 16)

            pipelined(sp, TURNS, ((0, load_pos), (2, load_xr), (4, store)))
            for par in range(2):
                sp.wait_ge(stored[par], 16 * POS * TURNS // 2)

        @block.gpsimd
        def _(pool):
            nc.gpsimd.memset(minus_half[:], -0.5).then_inc(consts, 1)
            nc.gpsimd.memset(pTb[:], 0.0).then_inc(consts, 1)
            pool.wait_ge(weights_in, 64)
            pool.wait_ge(consts, 2)

            def stage(t, par):
                after(pool, v_done, 2 * t - 2)
                if not isinstance(t, int):
                    pool.nop(nofuse=True)
                nc.gpsimd.tensor_copy(hst[:, par, :].rearrange("f (p i) -> f p i", p=POS),
                                      hT.rearrange("f (i p) -> f p i", p=P)[:, bass.ds(t * POS, POS), :]
                                      ).then_inc(h_staged, 1)
                after(pool, c_done, t - 1)
                if not isinstance(t, int):
                    pool.nop(nofuse=True)
                nc.gpsimd.tensor_tensor(qu[:, par], qT[:, :, bass.ds(t * P, P)],
                                        u_bias[:].unsqueeze(2).to_broadcast([P, RH, P]),
                                        ALU.add).then_inc(qu_done, 1)

            def subtract_max(t, par):
                pool.wait_ge(max_done, t + 1)
                nc.gpsimd.tensor_tensor(s[:], s[:], nmax[:].unsqueeze(2).to_broadcast([P, RH, SEQ]),
                                        ALU.add).then_inc(sub_done, 1)

            def add_bias(t, par):
                pool.wait_ge(xr_in[par], 32 * (t - par) + 64)
                nc.gpsimd.tensor_tensor(xr[:, par, :], xr[:, par, :], b_out[:], ALU.add
                                        ).then_inc(bout_done, 1)

            def power(t, par):
                pool.wait_ge(var_done, t + 1)
                nc.gpsimd.tensor_tensor(rstd[:], ve[:], minus_half[:], ALU.pow).then_inc(rstd_done, 1)

            pipelined(pool, TURNS, ((0, stage), (1, subtract_max), (4, power), (3, add_bias)))

        @block.tensor
        def _(pe):
            pe.wait_ge(weights_in, 64)

            def scores(t, par):
                after(pe, s_done, t)
                wait_alone(pe, qu_done, t + 1)
                for h in range(RH):
                    last = nc.tensor.matmul(content[:, h * P:(h + 1) * P], qu[:, par, h, :],
                                            qT[:, h, bass.ds(t * P, P)], start=True, stop=True)
                last.then_inc(c_done, 1)

            def values(t, par):
                pe.wait_ge(h_staged, t + 1)
                for n in range(2):
                    after(pe, v_copied, 2 * t - 1 + n)
                    nc.tensor.matmul(ps[VB[n]], hst[:, par, :], wv[:, n * BANK:(n + 1) * BANK],
                                     start=True, stop=True).then_inc(v_done, 1)

            def probs_v(t, par):
                pe.wait_ge(v_copied, 2 * t + 2)
                pe.wait_ge(pt_done, t + 1)
                for n in range(2):
                    after(pe, o_copied, 2 * t - 1 + n)
                    for j in range(4):
                        h = 4 * n + j
                        last = nc.tensor.matmul(ps[OB[n]][:, j * P:(j + 1) * P],
                                                v[:, par, h * P:(h + 1) * P], pTb[:, par, h, :],
                                                start=True, stop=True)
                    last.then_inc(pv_done, 1)

            def output(t, par):
                after(pe, res_done, t - 1)
                pe.wait_ge(o_copied, 2 * t + 2)
                for h in range(RH):
                    last = nc.tensor.matmul(ps[PB[par]][:, 0:P], oT[:, par, h, :], wo[:, h, :],
                                            start=(h == 0), stop=(h == RH - 1))
                last.then_inc(op_done, 1)

            pipelined(pe, TURNS, ((0, scores), (0, values), (1, probs_v), (2, output)))

        @block.scalar
        def _(act):
            def keep_v(t, par):
                after(act, pv_done, 2 * t - 2)
                for n in range(2):
                    act.wait_ge(v_done, 2 * t + n + 1)
                    nc.scalar.copy(v[:, par, n * BANK:(n + 1) * BANK], ps[VB[n]]).then_inc(v_copied, 1)

            def exponent(t, par):
                act.wait_ge(sub_done, t + 1)
                nc.scalar.activation(s[:], s[:], ACT.Exp, scale=SCALE).then_inc(exp_done, 1)

            def keep_o(t, par):
                after(act, op_done, t - 1)
                for n in range(2):
                    act.wait_ge(pv_done, 2 * t + n + 1)
                    nc.scalar.copy(oT[:, par, 4 * n:4 * n + 4, :].rearrange("p h t -> p (h t)"),
                                   ps[OB[n]]).then_inc(o_copied, 1)

            pipelined(act, TURNS, ((0, keep_v), (0, exponent), (1, keep_o)))

        @block.vector
        def _(dve):
            dve.wait_ge(weights_in, 64)
            dve.wait_ge(consts, 2)

            def masked_max(t, par):
                after(dve, pt_done, t)
                dve.wait_ge(pos_in[par], 32 * (t - par) + 64)
                dve.wait_ge(c_done, t + 1)
                blocks = content.rearrange("r (h c) -> r h c", h=RH)
                for p in range(POS):
                    rows = slice(p * SEQ, (p + 1) * SEQ)
                    last = nc.vector.tensor_tensor(
                        s[rows], blocks[rows, :, rows],
                        pos[rows, par, :].rearrange("r (h j) -> r h j", h=RH), ALU.add)
                last.then_inc(s_done, 1)
                dve.wait_ge(s_done, t + 1)
                nc.vector.tensor_reduce(nmax[:], s[:], AX.X, ALU.max, negate=True).then_inc(max_done, 1)

            def probabilities(t, par):
                link = Chain(dve, soft_link, t, 3)
                dve.wait_ge(exp_done, t + 1)
                link(nc.vector.tensor_reduce(rsum[:], s[:], AX.X, ALU.add))
                link(nc.vector.reciprocal(rinv[:], rsum[:]))
                link(nc.vector.tensor_tensor(s[:], s[:], rinv[:].unsqueeze(2).to_broadcast([P, RH, SEQ]),
                                             ALU.mult))
                after(dve, pv_done, 2 * t - 2)
                for p in range(POS):
                    rows = slice(p * SEQ, (p + 1) * SEQ)
                    last = nc.vector.transpose(pTb[rows, par, :, rows], s[rows])
                last.then_inc(pt_done, 1)
                link.end()

            def residual(t, par):
                link = Chain(dve, norm_link, t, 2)
                dve.wait_ge(op_done, t + 1)
                dve.wait_ge(bout_done, t + 1)
                after(dve, x4_done, t)
                nc.vector.tensor_tensor(res[:], ps[PB[par]][:, 0:P], xr[:, par, :], ALU.add
                                        ).then_inc(res_done, 1)
                dve.wait_ge(res_done, t + 1)
                link(nc.vector.bn_stats(stats[:], res[:]), alone=True)
                link(nc.vector.bn_aggr(mv[:], stats[:]))
                nc.vector.tensor_scalar(ve[:], mv[:, 1:2], EPS, None, ALU.add).then_inc(var_done, 1)
                link.end()

            def norm(t, par):
                after(dve, stored[par], 32 * (t - par))
                dve.wait_ge(rstd_done, t + 1)
                nc.vector.tensor_scalar(x4[:, par, :], res[:], mv[:, 0:1], rstd[:, 0:1],
                                        ALU.subtract, ALU.mult).then_inc(x4_done, 1)

            pipelined(dve, TURNS, ((0, masked_max), (3, residual), (0, probabilities), (3, norm)))




def routed_linear_pass(nc, ps2s, ps, gate_dram, wexp_dram, ident, x_res, out):
    N = E * P
    with ExitStack() as ctx:
        def sb(nm, shape, dt=F32):
            return ctx.enter_context(nc.sbuf_tensor("l_" + nm, shape, dt))

        def sem(nm):
            return nc.alloc_semaphore("l_" + nm)

        wexp = sb("wexp", [P, N])
        gate = sb("gate", [P, E])
        order = sb("order", [P, E])
        minus_half = sb("minus_half", [P, 1])
        stage = sb("stage", [P, 2, P])
        xT = sb("xT", [P, 2, P])
        smax = sb("smax", [P, 8])
        val = sb("val", [P, E])
        vmax = sb("vmax", [P, 1])
        onehot = sb("onehot", [P, E])
        acc = sb("acc", [P, 2, P])
        stats = sb("stats", [P, 6])
        mv = sb("mv", [P, 2])
        ve = sb("ve", [P, 1])
        rstd = sb("rstd", [P, 1])
        y = sb("y", [P, 2, P])

        weights_in = sem("weights_in")
        consts = sem("consts")
        staged = sem("staged")
        t_done = sem("t_done")
        t_copied = sem("t_copied")
        g_done = sem("g_done")
        e_done = sem("e_done")
        doubled = sem("doubled")
        mixed = sem("mixed")
        var_done = sem("var_done")
        rstd_done = sem("rstd_done")
        y_done = sem("y_done")
        link_sem = sem("link")
        stored = [sem("stored0"), sem("stored1")]
        TB, GB = 0, (1, 6)
        block = ctx.enter_context(nc.Block())

        @block.sync
        def _(sp):
            sp.dma_start(wexp[:], wexp_dram).then_inc(weights_in, 16)
            sp.dma_start(gate[:], gate_dram).then_inc(weights_in, 16)

            def back(t, par):
                sp.wait_ge(y_done, t + 1)
                sp.dma_start(out[t], y[:, par, :]).then_inc(stored[par], 16)

            skewed(sp, NB, lambda t, par: None, back)
            for par in range(2):
                sp.wait_ge(stored[par], 16 * NB // 2)

        @block.gpsimd
        def _(pool):
            nc.gpsimd.memset(minus_half[:], -0.5)
            for e in range(E):
                last = nc.gpsimd.memset(order[:, e:e + 1], float(E - e))
            last.then_inc(consts, 1)
            pool.wait_ge(consts, 1)

            def back(t, par):
                pool.wait_ge(var_done, t + 1)
                nc.gpsimd.tensor_tensor(rstd[:], ve[:], minus_half[:], ALU.pow).then_inc(rstd_done, 1)

            skewed(pool, NB, lambda t, par: None, back)

        @block.scalar
        def _(act):
            def front(t, par):
                after(act, t_done, t - 1)
                after(act, doubled, t - 1)
                if not isinstance(t, int):
                    act.nop(nofuse=True)
                nc.scalar.copy(stage[:, par, :], x_res[:, bass.ds(t * P, P)]).then_inc(staged, 1)
                act.wait_ge(t_done, t + 1)
                after(act, e_done, t - 1)
                nc.scalar.copy(xT[:, par, :], ps[TB][:, 0:P]).then_inc(t_copied, 1)

            def back(t, par):
                after(act, mixed, t - 1)
                after(act, y_done, t - 1)
                act.wait_ge(staged, t + 1)
                nc.scalar.mul(acc[:, par, :], stage[:, par, :], 2.0).then_inc(doubled, 1)

            skewed(act, NB, front, back)

        @block.tensor
        def _(pe):
            pe.wait_ge(weights_in, 32)

            def front(t, par):
                pe.wait_ge(staged, t + 1)
                after(pe, t_copied, t)
                nc.tensor.transpose(ps[TB][:, 0:P], stage[:, par, :], ident[:]).then_inc(t_done, 1)

            def back(t, par):
                pe.wait_ge(t_copied, t + 1)
                after(pe, mixed, t - 1)
                nc.tensor.matmul(ps[GB[par]][:, 0:E], xT[:, par, :], gate[:],
                                 start=True, stop=True).then_inc(g_done, 1)
                for n in range(2):
                    last = nc.tensor.matmul(ps2s[par][:, n * BANK:(n + 1) * BANK], xT[:, par, :],
                                            wexp[:, n * BANK:(n + 1) * BANK], start=True, stop=True)
                last.then_inc(e_done, 1)

            skewed(pe, NB, front, back)

        @block.vector
        def _(dve):
            dve.wait_ge(weights_in, 32)
            dve.wait_ge(consts, 1)

            def back(t, par):
                link = Chain(dve, link_sem, t, 13)
                dve.wait_ge(e_done, t + 1)
                after(dve, y_done, t)
                scores = ps[GB[par]][:, 0:E]
                link(nc.vector.tensor_reduce(smax[:, 0:1], scores, AX.X, ALU.max))
                link(nc.vector.scalar_tensor_tensor(out=val[:], in0=scores, scalar=smax[:, 0:1],
                                                    in1=order[:], op0=ALU.is_equal, op1=ALU.mult))
                link(nc.vector.tensor_reduce(vmax[:], val[:], AX.X, ALU.max))
                link(nc.vector.tensor_scalar(onehot[:], val[:], vmax[:, 0:1], None, ALU.is_equal))
                dve.wait_ge(doubled, t + 1)
                for e in range(E):
                    ins = nc.vector.scalar_tensor_tensor(
                        out=acc[:, par, :], in0=ps2s[par][:, e * P:(e + 1) * P],
                        scalar=onehot[:, e:e + 1], in1=acc[:, par, :], op0=ALU.mult, op1=ALU.add)
                    if e < E - 1:
                        link(ins)
                ins.then_inc(mixed, 1)
                dve.wait_ge(mixed, t + 1)
                link(nc.vector.bn_stats(stats[:], acc[:, par, :]), alone=True)
                link(nc.vector.bn_aggr(mv[:], stats[:]))
                nc.vector.tensor_scalar(ve[:], mv[:, 1:2], EPS, None, ALU.add).then_inc(var_done, 1)
                dve.wait_ge(rstd_done, t + 1)
                after(dve, stored[par], 8 * (t - par))
                nc.vector.tensor_scalar(y[:, par, :], acc[:, par, :], mv[:, 0:1], rstd[:, 0:1],
                                        ALU.subtract, ALU.mult).then_inc(y_done, 1)
                link.end()

            skewed(dve, NB, lambda t, par: None, back)


def build(nc, a, out):
    def scratch(name, shape):
        return nc.dram_tensor(name, shape, F32, kind="Internal").ap()

    x1_dram = scratch("x1_scratch", (NB, P, P))
    x3_dram = scratch("x3_scratch", (NB, P, P))
    x4_dram = scratch("x4_scratch", (NB, P, P))
    xe_dram = scratch("xe_scratch", (TOKENS, P))
    ye_dram = scratch("ye_scratch", (TOKENS + 1, P))
    pos_dram = scratch("pos_scratch", (NB, P, RH * SEQ))
    with ExitStack() as ctx:
        banks = ctx.enter_context(nc.psum_tensor("banks", [P, 8 * BANK], F32))
        ps = [banks[:, i * BANK:(i + 1) * BANK] for i in range(8)]
        ident = ctx.enter_context(nc.sbuf_tensor("ident", [P, P], F32))
        x_res = ctx.enter_context(nc.sbuf_tensor("x_res", [P, NB * P], F32))
        p_tok = ctx.enter_context(nc.sbuf_tensor("p_tok", [P, NB], F32))
        slot = ctx.enter_context(nc.sbuf_tensor("slot", [P, NB], U32))
        ident_made = ctx.enter_context(nc.semaphore("ident_made"))
        with nc.Block() as block:
            @block.gpsimd
            def _(pool):
                make_identity(nc, pool, ident, ident_made)
                pool.wait_ge(ident_made, 2)

        def keep_x(t):
            return x_res[:, bass.ds(t * P, P)]

        with nc.cleanup_on_exit():
            mamba_pass(nc, ps, {"x": a["x"], "xT": a["xT"]}, a, x1_dram)
            cross_attention_pass(nc, ps, "xa0", x1_dram, a["ctxT"], {n: a["x0_" + n] for n in "qkvo"},
                                 P ** -0.5, a["bias"], ident, keep_x)
        with nc.cleanup_on_exit():
            routing_pass(nc, ps, a["wr"], ident, x_res, p_tok, slot, xe_dram, ye_dram)
            experts_pass(nc, ps, a["w1"], a["w2"], ident, xe_dram, ye_dram)
            with nc.sbuf_tensor("r_pad", [P, RH, 2 * SEQ], F32) as r_pad, \
                    nc.sbuf_tensor("qT", [P, RH, TOKENS], F32) as qT:
                relative_setup(nc, ps, a["r_peT"], a["r_wr"], r_pad)
                relative_project_pass(nc, ps, a, ident, r_pad, x_res, p_tok, slot, ye_dram, qT,
                                      x3_dram, pos_dram)
                relative_attention_pass(nc, banks[:, 2 * BANK:4 * BANK], ps, a, x_res[:], qT, x3_dram,
                                        pos_dram, x4_dram)
        with nc.cleanup_on_exit():
            cross_attention_pass(nc, ps, "xa1", x4_dram, a["ctxT"], {n: a["x1_" + n] for n in "qkvo"},
                                 DH ** -0.5, None, ident, keep_x)
            routed_linear_pass(nc, [banks[:, i * BANK:(i + 2) * BANK] for i in (2, 4)], ps,
                               a["gateT"], a["wexpT"], ident, x_res, out)


def distance_table():
    pos = np.arange(SEQ, dtype=np.float32)[:, None]
    div = np.exp(np.arange(0, P, 2, dtype=np.float32) * np.float32(-math.log(10000.0) / P))
    ang = pos * div
    return np.stack([np.sin(ang), np.cos(ang)], axis=-1).reshape(SEQ, P)[::-1].T


def layout(inp):
    a = {k: np.asarray(v) for k, v in inp.items()}
    return {
        "x": a["x"], "xT": a["x"].reshape(TOKENS, P).T, "ctxT": a["ctx_1024"].reshape(TOKENS, P).T,
        "bias": a["fside_1x1xSxS2_0"].reshape(P, P),
        "W_inT": a["L0_attn_W_in"].T, "W_x": a["L0_attn_W_x"], "W_dtT": a["L0_attn_W_dt"].T,
        "W_outT": a["L0_attn_W_out"].T,
        "per_channel": np.concatenate(
            [a["L0_attn_conv_w"].reshape(2 * P, 4), a["L0_attn_conv_b"][:, None],
             a["L0_attn_b_dt"][:, None], a["L0_attn_D"][:, None]], axis=1),
        "x0_q": a["L0_xattn_Wq"].T, "x0_k": a["L0_xattn_Wk"].T, "x0_v": a["L0_xattn_Wv"].T,
        "x0_o": a["L0_xattn_Wp"].T,
        "wr": a["L0_ffn_Wr"], "w1": a["L0_ffn_W1"], "w2": a["L0_ffn_W2"],
        "r_q": a["L1_attn_Wq"], "r_v": a["L1_attn_Wv"], "r_wr": a["L1_attn_Wr"],
        "r_peT": distance_table(), "r_uT": a["L1_attn_u_bias"].T,
        "r_chan": np.concatenate([a["L1_attn_gamma"][:, None], a["L1_attn_beta"][:, None],
                                  a["L1_attn_v_bias"].T], axis=1),
        "r_bout": a["L1_attn_bout"].reshape(1, P), "r_out": a["L1_attn_Wout"],
        "x1_q": a["L1_xattn_w_q"], "x1_k": a["L1_xattn_w_k"], "x1_v": a["L1_xattn_w_v"],
        "x1_o": a["L1_xattn_w_o"],
        "gateT": a["L1_ffn_gate_w"].T,
        "wexpT": a["L1_ffn_expert_w"].transpose(2, 0, 1).reshape(P, E * P),
    }


def kernel(**inputs):
    import concourse.bacc as _bacc
    from concourse.bass_utils import run_bass_kernel_spmd as _run

    nc = _bacc.Bacc("TRN2", target_bir_lowering=False, num_devices=1)
    arrays, args = {}, {}

    def give(name, a):
        a = np.ascontiguousarray(a)
        arrays["in_" + name] = a
        args[name] = nc.dram_tensor("in_" + name, a.shape, mybir.dt.from_np(a.dtype),
                                    kind="ExternalInput").ap()

    for name, a in layout(inputs).items():
        give(name, a)
    out = nc.dram_tensor("out_0_dram", (NB, P, P), F32, kind="ExternalOutput").ap()
    build(nc, args, out)
    r = _run(nc, [arrays], core_ids=[0])
    return r.results[0]["out_0_dram"]
```

```python
from contextlib import ExitStack
import math

import numpy as np

import concourse.bass as bass
from concourse import mybir

F32 = mybir.dt.float32
BF16 = mybir.dt.bfloat16
I32 = mybir.dt.int32
U32 = mybir.dt.uint32
ALU = mybir.AluOpType
ACT = mybir.ActivationFunctionType
AX = mybir.AxisListType

P = 128
NB = 32
EPS = 1e-5
BANK = 512


def wait_alone(eng, sem, value):
    eng.wait_ge(sem, value)
    eng.nop(nofuse=True)


def after(eng, sem, value):
    if not isinstance(value, int) or value > 0:
        eng.wait_ge(sem, value)


def pipelined(eng, turns, steps):
    deepest = max(lag for lag, _ in steps)
    head = 2 * ((deepest + 3) // 2)

    def cycle(k, c):
        for lag, do in steps:
            if not isinstance(k, int) or 0 <= k - lag < turns:
                do(k - lag, (c - lag) % 2)

    for k in range(head):
        cycle(k, k)
    with eng.Fori(head // 2, turns // 2) as i:
        cycle(2 * i, 0)
        cycle(2 * i + 1, 1)
    for k in range(turns, turns + deepest):
        cycle(k, k)


def of(do, part):
    return lambda t, par: do(t, par, part)


class Chain:

    def __init__(self, eng, sem, turn, per_turn, before=0):
        self.eng, self.sem, self.per_turn = eng, sem, per_turn
        self.base = turn * per_turn + before
        self.n = 0

    def __call__(self, ins, alone=False):
        self.n += 1
        ins.then_inc(self.sem, 1)
        self.eng.wait_ge(self.sem, self.base + self.n)
        if alone:
            self.eng.nop(nofuse=True)

    def end(self):
        assert self.n == self.per_turn, (self.n, self.per_turn)


def make_identity(nc, pool, ident, sem):
    nc.gpsimd.memset(ident[:], 0.0).then_inc(sem, 1)
    pool.wait_ge(sem, 1)
    nc.gpsimd.affine_select(out=ident[:], in_=ident[:], compare_op=ALU.not_equal, fill=1.0, base=0,
                            pattern=[[-1, P]], channel_multiplier=1).then_inc(sem, 1)


def mamba_pass(nc, banks, ps, dram, w, out):
    SEQS = 4
    T = SEQS * P
    TURNS = NB // SEQS
    PAD = 3
    with ExitStack() as ctx:
        def sb(name, shape, dt=F32):
            return ctx.enter_context(nc.sbuf_tensor("m_" + name, shape, dt))

        def sem(name):
            return nc.alloc_semaphore("m_" + name)

        w_in = sb("w_in", [P, 4 * P])
        w_x_dt = sb("w_x_dt", [P, 2, 2 * P])
        w_x_b = sb("w_x_b", [16, 2 * P])
        w_x_c = sb("w_x_c", [16, 2 * P])
        w_dt = sb("w_dt", [P, 2, 2 * P])
        w_out = sb("w_out", [P, 2, P])
        w_comb = sb("w_comb", [P, 2, 2 * P])
        w_gate = sb("w_gate", [P, 2, 2, P])
        per_channel = sb("per_channel", [P, 2, 7])
        conv_w = per_channel[:, :, 0:4]
        conv_b = per_channel[:, :, 4]
        b_dt = per_channel[:, :, 5]
        d_skip = per_channel[:, :, 6]
        sixteenth = sb("sixteenth", [16, P])
        minus_half = sb("minus_half", [P, SEQS])
        xT = sb("xT", [P, T])
        x_tok = sb("x_tok", [P, SEQS, P])
        conv = sb("conv", [P, 2, T])
        sig = sb("sig", [P, 2, T])
        sigz = sb("sigz", [P, 2, T])
        zs = sb("zs", [P, 2, 2, T])
        xc = sb("xc", [P, 2, 2, T])
        gate = sb("gate", [P, 2, 2, T])
        relu = sb("relu", [P, 2, T])
        soft = sb("soft", [P, 2, T])
        sp = sb("sp", [P, 2, T])
        g = sb("g", [P, 2, T])
        alpha = sb("alpha", [P, 2, T])
        alpha_c = sb("alpha_c", [P, 2, T])
        gated = sb("gated", [P, 2, T])
        hid = sb("hid", [P, 2, T])
        hc = sb("hc", [P, 2, T])
        y = sb("y", [P, 2, T])
        res = sb("res", [P, SEQS, P])
        stats = sb("stats", [P, SEQS, 6])
        mv = sb("mv", [P, SEQS, 2])
        ve = sb("ve", [P, SEQS])
        rstd = sb("rstd", [P, SEQS])
        x1 = sb("x1", [P, SEQS, P])

        weights_in = sem("weights_in")
        consts = sem("consts")
        wprod = sem("wprod")
        wcomb_ready = sem("wcomb_ready")
        xT_in = sem("xT_in")
        x_in = sem("x_in")
        inproj_done = sem("inproj_done")
        taps_ready = sem("taps_ready")
        conv_done = sem("conv_done")
        ez_done = sem("ez_done")
        ez_bound = sem("ez_bound")
        sigz_done = sem("sigz_done")
        zs_done = sem("zs_done")
        ec_done = sem("ec_done")
        ec_bound = sem("ec_bound")
        sig_done = sem("sig_done")
        xc_done = sem("xc_done")
        gate_sums = sem("gate_sums")
        gate_exp = sem("gate_exp")
        gate_bound = sem("gate_bound")
        gates = sem("gates")
        dt_done = sem("dt_done")
        absd = sem("absd")
        soft_done = sem("soft_done")
        sp_done = sem("sp_done")
        g_done = sem("g_done")
        alpha_done = sem("alpha_done")
        gated_done = sem("gated_done")
        scan_done = sem("scan_done")
        hc_done = sem("hc_done")
        yskip = sem("yskip")
        y_done = sem("y_done")
        out_done = sem("out_done")
        res_done = sem("res_done")
        var_done = sem("var_done")
        rstd_done = sem("rstd_done")
        x1_done = sem("x1_done")
        stored = sem("stored")
        relu_done = sem("relu_done")
        clipped = sem("clipped")
        sigz_link = sem("sigz_link")
        sig_link = sem("sig_link")
        soft_link = sem("soft_link")
        gate_link = sem("gate_link")
        alpha_link = sem("alpha_link")
        tap_link = sem("tap_link")
        clip_link = sem("clip_link")
        norm_link = sem("norm_link")
        g_link = sem("g_link")
        gated_link = sem("gated_link")

        XP, Z, DT, GT = (0, 1), (2, 3), (4, 5), (6, 7)
        OUT = 6
        both = {k: banks[:, i * BANK:(i + 2) * BANK].rearrange("p (h t) -> p h t", h=2)
                for k, i in (("z", Z[0]), ("dt", DT[0]), ("gate", GT[0]))}
        LARGE = 1e18

        block = ctx.enter_context(nc.Block())
        WEIGHT_DMAS = 7

        @block.sync
        def _(sp_):
            for dst, src in (
                (w_in[:], w["W_inT"]),
                (per_channel[:], w["per_channel"].rearrange("(k p) t -> p k t", k=2)),
                (w_x_dt[:], w["W_x"][32:].rearrange("(k p) i -> p k i", k=2)),
                (w_dt[:], w["W_dtT"].rearrange("(k p) o -> p k o", k=2)),
                (w_x_b[:], w["W_x"][0:16]),
                (w_x_c[:], w["W_x"][16:32]),
                (w_out[:], w["W_outT"].rearrange("(k p) o -> p k o", k=2)),
            ):
                sp_.dma_start(dst, src).then_inc(weights_in, 16)

            def load_channels(t, par):
                after(sp_, inproj_done, 4 * t)
                sp_.dma_start(xT[:], dram["xT"][:, bass.ds(t * T, T)]).then_inc(xT_in, 16)

            def load_tokens(t, par):
                after(sp_, res_done, t)
                sp_.dma_start(x_tok[:], dram["x"][bass.ds(t * SEQS, SEQS)].rearrange("b s d -> s b d")
                              ).then_inc(x_in, 16)

            def store(t, par):
                sp_.wait_ge(x1_done, t + 1)
                sp_.dma_start(out[bass.ds(t * SEQS, SEQS)].rearrange("b s d -> s b d"), x1[:]
                              ).then_inc(stored, 16)

            pipelined(sp_, TURNS, ((0, load_channels), (3, store), (2, load_tokens)))
            sp_.wait_ge(stored, 16 * TURNS)

        @block.tensor
        def _(pe):
            pe.wait_ge(weights_in, 16 * WEIGHT_DMAS)
            pe.wait_ge(consts, 1)
            for k in range(2):
                for m in range(2):
                    last = nc.tensor.matmul(ps[k][:, 0:2 * P], w_x_dt[:, m, k * P:(k + 1) * P],
                                            w_dt[:, m, :], start=(m == 0), stop=(m == 1))
                last.then_inc(wprod, 1)
            for q, wx in enumerate((w_x_b, w_x_c)):
                for k in range(2):
                    last = nc.tensor.matmul(ps[2][:, (2 * k + q) * P:(2 * k + q + 1) * P],
                                            wx[:, k * P:(k + 1) * P], sixteenth[:],
                                            start=True, stop=True)
            last.then_inc(wprod, 1)
            pe.wait_ge(wcomb_ready, 3)

            def project(t, par, half):
                pe.wait_ge(xT_in, t * 16 + 16)
                for q in (2 * half, 2 * half + 1):
                    if half == 0:
                        after(pe, conv_done, t * 2 - 1 + q)
                    else:
                        after(pe, zs_done, t)
                    nc.tensor.matmul(ps[(XP + Z)[q]], w_in[:, q * P:(q + 1) * P], xT[:],
                                     start=True, stop=True).then_inc(inproj_done, 1)

            def step_sums(t, par):
                pe.wait_ge(xc_done, t + 1)
                after(pe, sp_done, t)
                for h, bank in enumerate(DT):
                    for k in range(2):
                        last = nc.tensor.matmul(ps[bank], w_comb[:, k, h * P:(h + 1) * P],
                                                xc[:, par, k, :], start=(k == 0), stop=(k == 1))
                    last.then_inc(dt_done, 1)

            def gate_sum(t, par):
                after(pe, res_done, t - 1)
                after(pe, gate_exp, t)
                for q, bank in enumerate(GT):
                    for k in range(2):
                        last = nc.tensor.matmul(ps[bank], w_gate[:, k, q, :], xc[:, par, k, :],
                                                start=(k == 0), stop=(k == 1))
                    last.then_inc(gate_sums, 1)

            def project_out(t, par):
                last_turn = isinstance(t, int) and t == TURNS - 1
                pe.wait_ge(gate_exp, TURNS if last_turn else t + 2)
                pe.wait_ge(y_done, t * 2 + 2)
                for b in range(SEQS):
                    for k in range(2):
                        last = nc.tensor.matmul(ps[OUT][:, b * P:(b + 1) * P],
                                                y[:, k, b * P:(b + 1) * P], w_out[:, k, :],
                                                start=(k == 0), stop=(k == 1))
                last.then_inc(out_done, 1)

            pipelined(pe, TURNS, ((0, of(project, 0)), (1, step_sums), (0, of(project, 1)),
                                  (1, gate_sum), (2, project_out)))

        @block.scalar
        def _(act):
            nc.scalar.preload_act_table_set("natural_log_exp_and_others")
            for k in range(2):
                act.wait_ge(wprod, k + 1)
                nc.scalar.copy(w_comb[:, k, :], ps[k][:, 0:2 * P]).then_inc(wcomb_ready, 1)
            act.wait_ge(wprod, 3)
            nc.scalar.copy(w_gate[:].rearrange("p k q c -> p (k q c)"), ps[2]).then_inc(wcomb_ready, 1)

            def last_tap(t, par):
                after(act, xc_done, t)
                for h in range(2):
                    act.wait_ge(inproj_done, t * 4 + h + 1)
                    nc.scalar.activation(conv[:, h, :], ps[XP[h]], ACT.Identity,
                                         bias=conv_b[:, h:h + 1], scale=conv_w[:, h, 3:4]
                                         ).then_inc(taps_ready, 1)

            def first_exps(t, par):
                after(act, zs_done, t)
                act.wait_ge(inproj_done, t * 4 + 4)
                nc.scalar.activation(sigz[:], both["z"], ACT.Exp, scale=-1.0).then_inc(ez_done, 1)
                act.wait_ge(conv_done, t * 2 + 2)
                nc.scalar.activation(sig[:], conv[:], ACT.Exp, scale=-1.0).then_inc(ec_done, 1)

            def sigmoids(t, par):
                for v, bound, link_sem, done in ((sigz, ez_bound, sigz_link, sigz_done),
                                                 (sig, ec_bound, sig_link, sig_done)):
                    link = Chain(act, link_sem, t, 1)
                    act.wait_ge(bound, t + 1)
                    link(nc.scalar.activation(v[:], v[:], ACT.Ln, bias=1.0))
                    nc.scalar.activation(v[:], v[:], ACT.Exp, scale=-1.0).then_inc(done, 1)
                    link.end()

            def softness(t, par):
                link = Chain(act, soft_link, t, 1)
                after(act, sp_done, t)
                for h in range(2):
                    act.wait_ge(dt_done, t * 2 + h + 1)
                    nc.scalar.activation(soft[:, h, :], ps[DT[h]], ACT.Abs, bias=b_dt[:, h:h + 1]
                                         ).then_inc(absd, 1)
                act.wait_ge(absd, t * 2 + 2)
                link(nc.scalar.activation(soft[:], soft[:], ACT.Exp, scale=-1.0))
                nc.scalar.activation(soft[:], soft[:], ACT.Ln, bias=1.0).then_inc(soft_done, 1)
                link.end()

            def gate_exps(t, par):
                after(act, hc_done, t * 2 - 2)
                act.wait_ge(gate_sums, t * 2 + 2)
                nc.scalar.activation(gate[:, par], both["gate"], ACT.Exp, scale=-1.0
                                     ).then_inc(gate_exp, 1)

            def gate_ends(t, par):
                link = Chain(act, gate_link, t, 1)
                act.wait_ge(gate_bound, t + 1)
                link(nc.scalar.activation(gate[:, par], gate[:, par], ACT.Ln, bias=1.0))
                nc.scalar.activation(gate[:, par], gate[:, par], ACT.Exp, scale=-1.0
                                     ).then_inc(gates, 1)
                link.end()

            def alphas(t, par):
                link = Chain(act, alpha_link, t, 1)
                after(act, gated_done, t)
                act.wait_ge(sp_done, t + 1)
                nc.scalar.activation(g[:], sp[:], ACT.Exp, scale=-0.1).then_inc(g_done, 1)
                after(act, clipped, t)
                act.wait_ge(g_done, t + 1)
                link(nc.scalar.activation(alpha[:], g[:], ACT.Ln, bias=1.0))
                nc.scalar.activation(alpha[:], alpha[:], ACT.Exp, scale=-1.0).then_inc(alpha_done, 1)
                link.end()

            pipelined(act, TURNS, ((0, last_tap), (1, softness), (0, first_exps), (1, alphas),
                                   (1, gate_exps), (0, sigmoids), (1, gate_ends)))

        @block.gpsimd
        def _(pool):
            nc.gpsimd.memset(sixteenth[:], 1.0 / 16).then_inc(consts, 1)
            nc.gpsimd.memset(minus_half[:], -0.5).then_inc(consts, 1)
            pool.wait_ge(consts, 2)

            def gate_values(t, par):
                for h in range(2):
                    pool.wait_ge(scan_done, t * 2 + h + 1)
                    nc.gpsimd.tensor_tensor(hc[:, h, :], hid[:, h, :], gate[:, par, 1, :], ALU.mult
                                            ).then_inc(hc_done, 1)

            def gate_output(t, par):
                after(pool, out_done, t)
                for h in range(2):
                    pool.wait_ge(yskip, t * 2 + h + 1)
                    nc.gpsimd.tensor_tensor(y[:, h, :], hc[:, h, :], zs[:, par, h, :], ALU.mult
                                            ).then_inc(y_done, 1)

            def one_minus_alpha(t, par):
                link = Chain(pool, g_link, t, 1)
                pool.wait_ge(alpha_done, t + 1)
                link(nc.gpsimd.tensor_tensor(g[:], g[:], alpha[:], ALU.mult))
                link.end()

            def gate_inputs(t, par):
                link = Chain(pool, gated_link, t, 1)
                after(pool, scan_done, t * 2)
                pool.wait_ge(gates, t + 1)
                link(nc.gpsimd.tensor_tensor(gated[:], xc[:, par],
                                             gate[:, par, 0, :].unsqueeze(1).to_broadcast([P, 2, T]),
                                             ALU.mult))
                nc.gpsimd.tensor_tensor(gated[:], gated[:], g[:], ALU.mult).then_inc(gated_done, 1)
                link.end()

            def power(t, par):
                pool.wait_ge(var_done, t + 1)
                nc.gpsimd.tensor_tensor(rstd[:], ve[:], minus_half[:], ALU.pow).then_inc(rstd_done, 1)

            pipelined(pool, TURNS, ((2, gate_values), (2, gate_output), (1, one_minus_alpha),
                                    (1, gate_inputs), (2, power)))

        @block.vector
        def _(dve):
            dve.wait_ge(weights_in, 16 * WEIGHT_DMAS)

            def tap(t, h, k, ins_link):
                back = PAD - k
                view = conv[:, h, :].rearrange("p (b s) -> p b s", b=SEQS)[:, :, back:]
                x = ps[XP[h]].rearrange("p (b s) -> p b s", b=SEQS)[:, :, 0:P - back]
                ins = nc.vector.scalar_tensor_tensor(
                    out=view, in0=x, scalar=conv_w[:, h, k:k + 1], in1=view,
                    op0=ALU.mult, op1=ALU.add)
                if ins_link is None:
                    ins.then_inc(conv_done, 1)
                else:
                    ins_link(ins)

            def middle_taps(t, par):
                link = Chain(dve, tap_link, t, 4)
                for k in (2, 1):
                    for h in range(2):
                        dve.wait_ge(taps_ready, t * 2 + h + 1)
                        tap(t, h, k, link)
                link.end()

            def first_tap(t, par):
                for h in range(2):
                    tap(t, h, 0, None)

            def bounds(t, par):
                for v, made, bound in ((sigz, ez_done, ez_bound), (sig, ec_done, ec_bound)):
                    dve.wait_ge(made, t + 1)
                    nc.vector.tensor_scalar(v[:], v[:], LARGE, None, ALU.min).then_inc(bound, 1)

            def silus(t, par):
                after(dve, y_done, t * 2 - 2)
                dve.wait_ge(sigz_done, t + 1)
                nc.vector.tensor_tensor(zs[:, par], both["z"], sigz[:], ALU.mult).then_inc(zs_done, 1)
                after(dve, gated_done, t - 1)
                after(dve, gate_sums, t * 2 - 2)
                after(dve, yskip, t * 2 - 2)
                dve.wait_ge(sig_done, t + 1)
                nc.vector.tensor_tensor(xc[:, par], conv[:], sig[:], ALU.mult).then_inc(xc_done, 1)

            def relus(t, par):
                after(dve, sp_done, t)
                for h in range(2):
                    dve.wait_ge(absd, t * 2 + h + 1)
                    nc.vector.tensor_scalar(relu[:, h, :], ps[DT[h]], b_dt[:, h:h + 1], 0.0,
                                            ALU.add, ALU.max).then_inc(relu_done, 1)

            def softplus(t, par):
                dve.wait_ge(relu_done, t * 2 + 2)
                dve.wait_ge(soft_done, t + 1)
                nc.vector.tensor_tensor(sp[:], relu[:], soft[:], ALU.add).then_inc(sp_done, 1)

            def gate_bounds(t, par):
                dve.wait_ge(gate_exp, t + 1)
                nc.vector.tensor_scalar(gate[:, par], gate[:, par], LARGE, None, ALU.min
                                        ).then_inc(gate_bound, 1)

            def clip(t, par):
                link = Chain(dve, clip_link, t, 1)
                after(dve, scan_done, t * 2)
                dve.wait_ge(alpha_done, t + 1)
                link(nc.vector.tensor_scalar(alpha_c[:], alpha[:], 0.01, 0.99, ALU.max, ALU.min))
                nc.vector.memset(alpha_c[:, :, 0:T:P], 0.0).then_inc(clipped, 1)
                link.end()

            def scan(t, par):
                after(dve, hc_done, t * 2)
                dve.wait_ge(clipped, t + 1)
                dve.wait_ge(gated_done, t + 1)
                for h in range(2):
                    nc.vector.tensor_tensor_scan(hid[:, h, :], alpha_c[:, h, :], gated[:, h, :], 0.0,
                                                 ALU.mult, ALU.add).then_inc(scan_done, 1)

            def skip(t, par):
                for h in range(2):
                    dve.wait_ge(hc_done, t * 2 + h + 1)
                    nc.vector.scalar_tensor_tensor(out=hc[:, h, :], in0=xc[:, par, h, :],
                                                   scalar=d_skip[:, h:h + 1], in1=hc[:, h, :],
                                                   op0=ALU.mult, op1=ALU.add).then_inc(yskip, 1)

            def residual(t, par):
                link = Chain(dve, norm_link, t, 2)
                after(dve, x1_done, t)
                dve.wait_ge(out_done, t + 1)
                dve.wait_ge(x_in, t * 16 + 16)
                nc.vector.tensor_tensor(res[:], ps[OUT].rearrange("p (b d) -> p b d", b=SEQS),
                                        x_tok[:], ALU.add).then_inc(res_done, 1)
                dve.wait_ge(res_done, t + 1)
                for b in range(SEQS):
                    ins = nc.vector.bn_stats(stats[:, b, :], res[:, b, :])
                link(ins, alone=True)
                for b in range(SEQS):
                    ins = nc.vector.bn_aggr(mv[:, b, :], stats[:, b, :])
                link(ins)
                nc.vector.tensor_scalar(ve[:], mv[:, :, 1], EPS, None, ALU.add).then_inc(var_done, 1)
                link.end()

            def norm(t, par):
                dve.wait_ge(rstd_done, t + 1)
                after(dve, stored, t * 16)
                for b in range(SEQS):
                    ins = nc.vector.tensor_scalar(x1[:, b, :], res[:, b, :], mv[:, b, 0:1],
                                                  rstd[:, b:b + 1], ALU.subtract, ALU.mult)
                ins.then_inc(x1_done, 1)

            pipelined(dve, TURNS, ((0, middle_taps), (2, scan), (1, relus), (0, first_tap),
                                   (1, softplus), (3, norm), (0, bounds), (2, skip), (1, clip),
                                   (1, gate_bounds), (0, silus), (2, residual)))


E, F, CAP = 8, 512, NB * P // 8
TOKENS = NB * P
HEADS, DH = 16, 64
GROUP = 4
GROUPS = HEADS // GROUP


def cross_attention_pass(nc, ps, name, x_dram, ctxT_dram, w, scale, bias_dram, ident, x_out,
                         routed=None, dispatch=None):
    with ExitStack() as ctx:
        def sb(nm, shape, dt=F32):
            return ctx.enter_context(nc.sbuf_tensor(f"{name}_{nm}", shape, dt))

        def sem(nm):
            return nc.alloc_semaphore(f"{name}_{nm}")

        wq = sb("wq", [P, HEADS * DH])
        wk = sb("wk", [P, HEADS * DH])
        wv = sb("wv", [P, HEADS * DH])
        wo = sb("wo", [P, HEADS // 2, P])
        bias = sb("bias", [P, P]) if bias_dram is not None else None
        minus_half = sb("minus_half", [P, 1])
        xa = sb("xa", [P, 2, P])
        xr = sb("xr", [P, P])
        ctxT = sb("ctxT", [P, 2, P])
        xT = sb("xT", [P, P])
        qT = sb("qT", [P, 2, 8, P])
        kT = sb("kT", [P, 2, 8, P])
        v = sb("v", [P, 2, HEADS * DH])
        ss = sb("ss", [P, GROUPS, GROUP, P]) if bias_dram is not None else None
        nmax = sb("nmax", [P, GROUPS, GROUP])
        prob = sb("prob", [P, GROUPS, GROUP, P])
        rsum = sb("rsum", [P, GROUPS, GROUP])
        rinv = sb("rinv", [P, GROUPS, GROUP])
        pT = sb("pT", [P, 2, GROUP, P])
        oT = sb("oT", [P, 8, P])
        res = sb("res", [P, P])
        stats = sb("stats", [P, 6])
        mv = sb("mv", [P, 2])
        ve = sb("ve", [P, 1])
        rstd = sb("rstd", [P, 1])

        mode = "routed" if routed is not None else "dispatch" if dispatch is not None else None
        if mode is not None:
            order = sb("order", [P, E])
            x5 = sb("x5", [P, 2, P])
            x5T = sb("x5T", [P, P])
            smax = sb("smax", [P, 1])
            val = sb("val", [P, E])
            vmax = sb("vmax", [P, 1])
        if dispatch is not None:
            gate_dram, p_tok, slot, xe_dram, ye_dram = dispatch
            gate = sb("gate", [P, E])
            zeros = sb("zeros", [P, BANK])
            diff = sb("diff", [P, E])
            ex = sb("ex", [P, E])
            esum = sb("esum", [P, 1])
            onehot = sb("onehot", [P, E], BF16)
            before = sb("before", [P, P], BF16)
            ones = sb("ones", [P, P], BF16)
            taken = sb("taken", [P, E])
            limit = sb("limit", [P, E])
            place = sb("place", [P, E])
            over = sb("over", [P, E])
            slot_f = sb("slot_f", [P, 2])
            slot_now = sb("slot_now", [P, 2], U32)
        if routed is not None:
            gate_dram, wexp_dram, out = routed
            wexp = sb("wexp", [P, E * P])
            gate = sb("gate", [P, E])
            onehot = sb("onehot", [P, E])
            acc = sb("acc", [P, 2, P])
            stats2 = sb("stats2", [P, 6])
            mv2 = sb("mv2", [P, 2])
            ve2 = sb("ve2", [P, 1])
            rstd2 = sb("rstd2", [P, 1])
            y = sb("y", [P, 2, P])

        weight_in = {n: sem(n + "_in") for n in ("k", "q", "v", "o", "bias", "gate", "experts")}
        consts = sem("consts")
        xa_in = [sem("xa_in0"), sem("xa_in1")]
        xr_in = sem("xr_in")
        ctx_in = [sem("ctx_in0"), sem("ctx_in1")]
        fill_done = sem("fill_done")
        act_copied = sem("act_copied")
        v_copied = sem("v_copied")
        s_done = sem("s_done")
        biased = sem("biased")
        nmax_done = sem("nmax_done")
        exp_done = sem("exp_done")
        rinv_done = sem("rinv_done")
        norm_done = sem("norm_done")
        t_done = sem("t_done")
        pt_copied = sem("pt_copied")
        pv_done = sem("pv_done")
        ot_copied = sem("ot_copied")
        op_done = sem("op_done")
        res_done = sem("res_done")
        var_done = sem("var_done")
        rstd_done = sem("rstd_done")
        x_done = sem("x_done")
        ln_link = sem("ln_link")

        x5_turned = sem("x5_turned")
        x5_copied = sem("x5_copied")
        doubled = sem("doubled")
        g_done = sem("g_done")
        g_read = sem("g_read")
        e_done = sem("e_done")
        mixed = sem("mixed")
        var2_done = sem("var2_done")
        rstd2_done = sem("rstd2_done")
        y_done = sem("y_done")
        choose_link = sem("choose_link")
        mix_link = sem("mix_link")
        ln2_link = sem("ln2_link")
        esum_done = sem("esum_done")
        p_kept = sem("p_kept")
        onehot_done = sem("onehot_done")
        ranked = sem("ranked")
        ranks_read = sem("ranks_read")
        x_kept = sem("x_kept")
        slot_done = sem("slot_done")
        slot_kept = sem("slot_kept")
        place_link = sem("place_link")
        rank_link = sem("rank_link")
        cleared = sem("cleared")
        scattered = [sem("scattered0"), sem("scattered1")]
        y_stored = [sem("y_stored0"), sem("y_stored1")]

        SC, PT, OT, FILL, OP = (0, 1), (2, 3), 4, (5, 6), 7
        n_consts = {"routed": 2, "dispatch": 6, None: 1}[mode]

        def steps(*all_steps):
            return [s[:2] for s in all_steps if len(s) == 2 or (mode is not None and mode in s[2])]

        block = ctx.enter_context(nc.Block())

        @block.sync
        def _(sp):
            def load_weights():
                loads = [("k", wk[:], w["k"]), ("q", wq[:], w["q"]), ("v", wv[:], w["v"])]
                if bias is not None:
                    loads.append(("bias", bias[:], bias_dram))
                loads.append(("o", wo[:], w["o"].rearrange("(j p) o -> p j o", p=P)))
                if mode is not None:
                    loads.append(("gate", gate[:], gate_dram))
                if routed is not None:
                    loads.append(("experts", wexp[:], wexp_dram))
                for n, dst, src in loads:
                    sp.dma_start(dst, src).then_inc(weight_in[n], 16)

            def clear():
                sp.wait_ge(consts, 2)
                for n in range(8):
                    sp.dma_start(xe_dram[n * CAP:(n + 1) * CAP].rearrange("(p r) d -> p (r d)", p=P),
                                 zeros[:]).then_inc(cleared, 16)
                sp.dma_start(ye_dram[TOKENS:TOKENS + 1], zeros[0:1, 0:P]).then_inc(cleared, 16)

            def load_next(t, par):
                if dispatch is not None and isinstance(t, int) and t == 2:
                    clear()
                after(sp, fill_done, 7 * t - 13)
                sp.dma_start(xa[:, par, :], x_dram[t]).then_inc(xa_in[par], 16)
                after(sp, fill_done, 7 * t - 7)
                sp.dma_start(ctxT[:, par, :], ctxT_dram[:, bass.ds(t * P, P)]).then_inc(ctx_in[par], 16)
                if isinstance(t, int) and t == 0:
                    load_weights()

            def load_residual(t, par):
                after(sp, res_done, t)
                sp.dma_start(xr[:], x_dram[t]).then_inc(xr_in, 16)

            def store(t, par):
                sp.wait_ge(y_done, t + 1)
                sp.dma_start(out[t], y[:, par, :]).then_inc(y_stored[par], 16)

            pipelined(sp, NB, steps((0, load_next), (2, load_residual), (6, store, "routed")))
            if routed is not None:
                for par in range(2):
                    sp.wait_ge(y_stored[par], 16 * NB // 2)

        def first_needs(eng, t, name):
            if isinstance(t, int) and t == 0:
                eng.wait_ge(weight_in[name], 16)

        def bank_of(par, f):
            if mode is not None:
                return FILL[(0, 1, 1, 0, 0, 1, 1)[f]]
            return FILL[(par + f) % 2]

        @block.tensor
        def _(pe):
            def fill(t, par, f):
                out = ps[bank_of(par, f)]
                if f == 0:
                    if mode is None:
                        after(pe, v_copied, 2 * t - 1)
                    else:
                        after(pe, act_copied, 5 * t)
                        after(pe, g_read, t - 3)
                    pe.wait_ge(xa_in[par], 8 * (t - par) + 16)
                    nc.tensor.transpose(out[:, 0:P], xa[:, par, :], ident[:]).then_inc(fill_done, 1)
                elif f in (1, 2, 3, 4):
                    if f == 1:
                        after(pe, v_copied, 2 * t)
                        pe.wait_ge(ctx_in[par], 8 * (t - par) + 16)
                    elif mode is None:
                        pe.wait_ge(act_copied, 5 * t + f - 1)
                    else:
                        pe.wait_ge(act_copied, 5 * t + f - (f == 3))
                        if f == 3 and routed is not None:
                            after(pe, mixed, 2 * t - 7)
                        elif f == 3:
                            after(pe, ranks_read, t - 3)
                    half = (f - 1) % 2
                    first_needs(pe, t, "k" if f < 3 else "q")
                    weight, tokens = (wk, ctxT[:, par, :]) if f < 3 else (wq, xT[:])
                    for j in range(4):
                        pair = 4 * half + j
                        last = nc.tensor.matmul(out[:, j * P:(j + 1) * P],
                                                weight[:, pair * P:(pair + 1) * P], tokens,
                                                start=True, stop=True)
                    last.then_inc(fill_done, 1)
                else:
                    if mode is None:
                        pe.wait_ge(act_copied, 5 * t + f - 1)
                    elif f == 5 and routed is not None:
                        after(pe, mixed, 2 * t - 6)
                    elif f == 5:
                        pe.wait_ge(act_copied, 5 * t + 4)
                    else:
                        pe.wait_ge(v_copied, 2 * t + 1)
                    first_needs(pe, t, "v")
                    nc.tensor.matmul(out[:], ctxT[:, par, :], wv[:, (f - 5) * BANK:(f - 4) * BANK],
                                     start=True, stop=True).then_inc(fill_done, 1)

            def scores(t, par, g):
                after(pe, exp_done if bias is None else biased, 4 * t + g - 1)
                pe.wait_ge(act_copied, 5 * t + 5)
                for j in range(GROUP):
                    pair = GROUP * (g // 2) + j
                    r = DH * (g % 2)
                    last = nc.tensor.matmul(ps[SC[g % 2]][:, j * P:(j + 1) * P],
                                            qT[r:r + DH, par, pair, :], kT[r:r + DH, par, pair, :],
                                            start=True, stop=True)
                last.then_inc(s_done, 1)

            def transposes(t, par, g):
                pe.wait_ge(norm_done, 4 * t + g + 1)
                after(pe, pt_copied, 4 * t + g - 1)
                for j in range(GROUP):
                    last = nc.tensor.transpose(ps[PT[g % 2]][:, j * P:(j + 1) * P],
                                               prob[:, g, j, :], ident[:])
                last.then_inc(t_done, 1)

            def values(t, par, g):
                pe.wait_ge(pt_copied, 4 * t + g + 1)
                if g == 0:
                    after(pe, ot_copied, 2 * t)
                    pe.wait_ge(v_copied, 2 * t + 2)
                if g == 2:
                    pe.wait_ge(ot_copied, 2 * t + 1)
                for j in range(GROUP):
                    h = 2 * (GROUP * (g // 2) + j) + g % 2
                    r = DH * (g % 2)
                    last = nc.tensor.matmul(ps[OT][r:r + DH, j * P:(j + 1) * P],
                                            v[:, par, h * DH:(h + 1) * DH], pT[:, g % 2, j, :],
                                            start=True, stop=True)
                last.then_inc(pv_done, 1)

            def out_projection(t, par):
                first_needs(pe, t, "o")
                pe.wait_ge(ot_copied, 2 * t + 2)
                after(pe, res_done, t)
                for j in range(8):
                    last = nc.tensor.matmul(ps[OP][:, 0:P], oT[:, j, :], wo[:, j, :],
                                            start=(j == 0), stop=(j == 7))
                last.then_inc(op_done, 1)

            def left(eng, t, count):
                eng.wait_ge(act_copied, min(count, 5 * NB) if isinstance(t, int) else count)

            def turn_x5(t, par):
                left(pe, t, 5 * t + 20)
                if routed is not None:
                    after(pe, mixed, 2 * t - 1)
                else:
                    after(pe, ranks_read, t)
                pe.wait_ge(x_done, t + 1)
                nc.tensor.transpose(ps[FILL[0]][:, 0:P], x5[:, par, :], ident[:]).then_inc(x5_turned, 1)

            def choice(t, par):
                first_needs(pe, t, "gate")
                pe.wait_ge(x5_copied, t + 1)
                nc.tensor.matmul(ps[FILL[0]][:, 0:E], x5T[:], gate[:], start=True, stop=True
                                 ).then_inc(g_done, 1)

            def ranks(t, par):
                left(pe, t, 5 * t + 21)
                pe.wait_ge(onehot_done, t + 1)
                if isinstance(t, int) and t == 0:
                    pe.wait_ge(consts, n_consts)
                nc.tensor.matmul(ps[FILL[0]][:, 0:E], before[:], onehot[:], start=True, stop=True)
                nc.tensor.matmul(ps[FILL[0]][:, E:2 * E], ones[:], onehot[:], start=True, stop=True
                                 ).then_inc(ranked, 1)

            def expert_products(t, par, n):
                first_needs(pe, t, "experts")
                left(pe, t, 5 * t + (21, 23)[n])
                if n == 0:
                    pe.wait_ge(g_read, t + 1)
                else:
                    after(pe, mixed, 2 * t)
                nc.tensor.matmul(ps[FILL[n]], x5T[:], wexp[:, n * BANK:(n + 1) * BANK],
                                 start=True, stop=True).then_inc(e_done, 1)

            pipelined(pe, NB, steps(
                (2, of(scores, 2)), (3, of(values, 3)), (2, of(transposes, 0)),
                (1, of(fill, 4)), (1, of(fill, 5)),
                (2, of(scores, 3)), (4, turn_x5, "routed dispatch"), (3, out_projection),
                (4, choice, "routed dispatch"), (2, of(values, 0)),
                (2, of(transposes, 1)), (1, of(fill, 6)),
                (1, of(scores, 0)), (2, of(values, 1)), (2, of(transposes, 2)),
                (0, of(fill, 0)), (0, of(fill, 1)), (4, of(expert_products, 0), "routed"),
                (4, ranks, "dispatch"),
                (1, of(scores, 1)), (2, of(values, 2)), (2, of(transposes, 3)),
                (0, of(fill, 2)), (0, of(fill, 3)), (4, of(expert_products, 1), "routed")))

        @block.scalar
        def _(act):
            def copy(t, par, f):
                act.wait_ge(fill_done, 7 * t + f + 1)
                src = ps[bank_of(par, f)]
                if f == 0:
                    after(act, fill_done, 7 * t - 2)
                    ins = nc.scalar.copy(xT[:], src[:, 0:P])
                elif f in (1, 2):
                    after(act, s_done, 4 * t - 4)
                    ins = nc.scalar.copy(kT[:, par, 4 * (f - 1):4 * f, :].rearrange("p j t -> p (j t)"),
                                         src[:])
                else:
                    after(act, s_done, 4 * t - 4)
                    ins = nc.scalar.mul(qT[:, par, 4 * (f - 3):4 * (f - 2), :]
                                        .rearrange("p j t -> p (j t)"), src[:], scale)
                ins.then_inc(act_copied, 1)

            def exps(t, par, g):
                act.wait_ge(nmax_done, 4 * t + g + 1)
                after(act, t_done, 4 * t + g - 3)
                after(act, rinv_done, 4 * t + g - 3)
                for j in range(GROUP):
                    src = ps[SC[g % 2]][:, j * P:(j + 1) * P] if bias is None else ss[:, g, j, :]
                    last = nc.scalar.activation(prob[:, g, j, :], src, ACT.Exp,
                                                bias=nmax[:, g, j:j + 1],
                                                accum_out=rsum[:, g, j:j + 1])
                last.then_inc(exp_done, 1)

            def copy_values(t, par, half):
                act.wait_ge(pv_done, 4 * t + 2 * half + 2)
                after(act, op_done, t)
                nc.scalar.copy(oT[:, 4 * half:4 * half + 4, :].rearrange("p j t -> p (j t)"),
                               ps[OT]).then_inc(ot_copied, 1)

            def copy_x5(t, par):
                act.wait_ge(x5_turned, t + 1)
                if routed is not None:
                    after(act, e_done, 2 * t)
                else:
                    after(act, g_done, t)
                nc.scalar.copy(x5T[:], ps[FILL[0]][:, 0:P]).then_inc(x5_copied, 1)
                if routed is not None:
                    after(act, y_done, t - 1)
                    nc.scalar.mul(acc[:, par, :], x5[:, par, :], 2.0).then_inc(doubled, 1)
                else:
                    nc.scalar.copy(x_out(t, par), x5[:, par, :]).then_inc(x_kept, 1)

            def exp_scores(t, par):
                act.wait_ge(g_read, t + 1)
                after(act, p_kept, t)
                nc.scalar.activation(ex[:], diff[:], ACT.Exp, accum_out=esum[:]).then_inc(esum_done, 1)

            pipelined(act, NB, steps(
                (3, of(copy_values, 1)), (1, of(copy, 4)), (2, of(exps, 2)),
                (4, copy_x5, "routed dispatch"), (2, of(exps, 3)),
                (4, exp_scores, "dispatch"),
                (2, of(copy_values, 0)), (0, of(copy, 0)), (1, of(exps, 0)), (0, of(copy, 1)),
                (0, of(copy, 2)), (1, of(exps, 1)), (0, of(copy, 3))))
            if dispatch is not None:
                act.wait_ge(x_kept, NB)

        @block.gpsimd
        def _(pool):
            nc.gpsimd.memset(minus_half[:], -0.5).then_inc(consts, 1)
            if dispatch is not None:
                nc.gpsimd.memset(zeros[:], 0.0).then_inc(consts, 1)
                nc.gpsimd.memset(ones[:], 1.0).then_inc(consts, 1)
                nc.gpsimd.memset(before[:], 1.0).then_inc(consts, 1)
                for e in range(E):
                    nc.gpsimd.memset(taken[:, e:e + 1], float(CAP * e))
                    nc.gpsimd.memset(limit[:, e:e + 1], float(CAP * e + CAP))
            if mode is not None:
                for e in range(E):
                    last = nc.gpsimd.memset(order[:, e:e + 1], float(E - e))
                last.then_inc(consts, 1)
            if dispatch is not None:
                pool.wait_ge(consts, 5)
                nc.gpsimd.affine_select(out=before[:], in_=before[:], compare_op=ALU.is_gt, fill=0.0,
                                        base=0, pattern=[[1, P]], channel_multiplier=-1
                                        ).then_inc(consts, 1)

            def scatter(t, par):
                if isinstance(t, int) and t == 0:
                    pool.wait_ge(cleared, 16 * 9)
                wait_alone(pool, slot_done, t + 1)
                nc.gpsimd.indirect_dma_start(
                    out=xe_dram[:, :],
                    out_offset=bass.IndirectOffsetOnAxis(ap=slot_now[:, par:par + 1], axis=0),
                    in_=x5[:, par, :], in_offset=None,
                    bounds_check=TOKENS - 1, oob_is_err=False).then_inc(scattered[par], 16)

            def normalise(t, par, g):
                pool.wait_ge(rinv_done, 4 * t + g + 1)
                nc.gpsimd.tensor_tensor(prob[:, g], prob[:, g],
                                        rinv[:, g, :].unsqueeze(2).to_broadcast([P, GROUP, P]),
                                        ALU.mult).then_inc(norm_done, 1)

            def power(t, par):
                pool.wait_ge(var_done, t + 1)
                nc.gpsimd.tensor_tensor(rstd[:], ve[:], minus_half[:], ALU.pow).then_inc(rstd_done, 1)

            def power_routed(t, par):
                pool.wait_ge(var2_done, t + 1)
                nc.gpsimd.tensor_tensor(rstd2[:], ve2[:], minus_half[:], ALU.pow
                                        ).then_inc(rstd2_done, 1)

            pool.wait_ge(consts, 1)
            pipelined(pool, NB, steps(
                (2, of(normalise, 1)), (2, of(normalise, 2)), (2, of(normalise, 3)),
                (5, power_routed, "routed"), (3, power), (1, of(normalise, 0)),
                (4, scatter, "dispatch")))
            if dispatch is not None:
                for par in range(2):
                    pool.wait_ge(scattered[par], 16 * NB // 2)

        @block.vector
        def _(dve):
            def copy_v(t, par, n):
                dve.wait_ge(fill_done, 7 * t + 6 + n)
                after(dve, pv_done, 4 * t - 4)
                nc.vector.tensor_copy(v[:, par, n * BANK:(n + 1) * BANK], ps[bank_of(par, 5 + n)]
                                      ).then_inc(v_copied, 1)

            def maxima(t, par, g):
                dve.wait_ge(s_done, 4 * t + g + 1)
                src = ps[SC[g % 2]].rearrange("p (j k) -> p j k", j=GROUP)
                after(dve, exp_done, 4 * t + g - 3)
                if bias is not None:
                    first_needs(dve, t, "bias")
                    nc.vector.tensor_tensor(ss[:, g], src,
                                            bias[:].unsqueeze(1).to_broadcast([P, GROUP, P]), ALU.add
                                            ).then_inc(biased, 1)
                    dve.wait_ge(biased, 4 * t + g + 1)
                    src = ss[:, g]
                nc.vector.tensor_reduce(nmax[:, g, :], src, AX.X, ALU.max, negate=True
                                        ).then_inc(nmax_done, 1)

            def inverse(t, par, g):
                dve.wait_ge(exp_done, 4 * t + g + 1)
                after(dve, norm_done, 4 * t + g - 3)
                nc.vector.reciprocal(rinv[:, g, :], rsum[:, g, :]).then_inc(rinv_done, 1)

            def copy_pt(t, par, g):
                dve.wait_ge(t_done, 4 * t + g + 1)
                after(dve, pv_done, 4 * t + g - 1)
                nc.vector.tensor_copy(pT[:, g % 2].rearrange("p j t -> p (j t)"), ps[PT[g % 2]]
                                      ).then_inc(pt_copied, 1)

            def residual(t, par):
                link = Chain(dve, ln_link, t, 2)
                after(dve, x_done, t)
                dve.wait_ge(op_done, t + 1)
                dve.wait_ge(xr_in, 16 * t + 16)
                nc.vector.tensor_tensor(res[:], ps[OP][:, 0:P], xr[:], ALU.add).then_inc(res_done, 1)
                dve.wait_ge(res_done, t + 1)
                link(nc.vector.bn_stats(stats[:], res[:]), alone=True)
                link(nc.vector.bn_aggr(mv[:], stats[:]))
                nc.vector.tensor_scalar(ve[:], mv[:, 1:2], EPS, None, ALU.add).then_inc(var_done, 1)
                link.end()

            def norm(t, par):
                dve.wait_ge(rstd_done, t + 1)
                if mode is not None:
                    after(dve, x5_turned, t - 1)
                if routed is not None:
                    after(dve, doubled, t - 1)
                if dispatch is not None:
                    after(dve, x_kept, t - 1)
                    after(dve, scattered[par], 8 * (t - par))
                nc.vector.tensor_scalar(x_out(t, par) if mode is None else x5[:, par, :], res[:],
                                        mv[:, 0:1], rstd[:, 0:1],
                                        ALU.subtract, ALU.mult).then_inc(x_done, 1)

            def choose(t, par):
                link = Chain(dve, choose_link, t, 3)
                scores = ps[FILL[0]][:, 0:E]
                dve.wait_ge(g_done, t + 1)
                after(dve, mixed, 2 * t)
                link(nc.vector.tensor_reduce(smax[:], scores, AX.X, ALU.max))
                nc.vector.scalar_tensor_tensor(out=val[:], in0=scores, scalar=smax[:, 0:1],
                                               in1=order[:], op0=ALU.is_equal, op1=ALU.mult
                                               ).then_inc(g_read, 1)
                dve.wait_ge(g_read, t + 1)
                link(nc.vector.tensor_reduce(vmax[:], val[:], AX.X, ALU.max))
                link(nc.vector.tensor_scalar(onehot[:], val[:], vmax[:, 0:1], None, ALU.is_equal))
                link.end()

            def choose_expert(t, par):
                link = Chain(dve, choose_link, t, 3)
                scores = ps[FILL[0]][:, 0:E]
                dve.wait_ge(g_done, t + 1)
                after(dve, esum_done, t)
                link(nc.vector.tensor_reduce(smax[:], scores, AX.X, ALU.max))
                nc.vector.tensor_scalar(diff[:], scores, smax[:, 0:1], None, ALU.subtract
                                        ).then_inc(g_read, 1)
                dve.wait_ge(g_read, t + 1)
                link(nc.vector.scalar_tensor_tensor(out=val[:], in0=diff[:], scalar=0.0, in1=order[:],
                                                    op0=ALU.is_equal, op1=ALU.mult))
                link(nc.vector.tensor_reduce(vmax[:], val[:], AX.X, ALU.max))
                nc.vector.tensor_scalar(onehot[:], val[:], vmax[:, 0:1], None, ALU.is_equal
                                        ).then_inc(onehot_done, 1)
                link.end()

            def read_ranks(t, par):
                link = Chain(dve, place_link, t, 1)
                dve.wait_ge(ranked, t + 1)
                link(nc.vector.tensor_tensor(place[:], ps[FILL[0]][:, 0:E], taken[:], ALU.add))
                nc.vector.tensor_tensor(taken[:], ps[FILL[0]][:, E:2 * E], taken[:], ALU.add
                                        ).then_inc(ranks_read, 1)
                link.end()

            def place_tokens(t, par):
                link = Chain(dve, rank_link, t, 5)
                dve.wait_ge(ranks_read, t + 1)
                after(dve, slot_kept, t)
                link(nc.vector.tensor_tensor(over[:], place[:], limit[:], ALU.is_ge))
                link(nc.vector.scalar_tensor_tensor(out=place[:], in0=over[:], scalar=float(TOKENS),
                                                    in1=place[:], op0=ALU.mult, op1=ALU.add))
                link(nc.vector.tensor_tensor(place[:], place[:], onehot[:], ALU.mult))
                link(nc.vector.tensor_reduce(slot_f[:, 0:1], place[:], AX.X, ALU.add))
                link(nc.vector.tensor_scalar(slot_f[:, 1:2], slot_f[:, 0:1], float(TOKENS), None, ALU.min))
                after(dve, scattered[par], 8 * (t - par))
                nc.vector.tensor_copy(slot_now[:, par:par + 1], slot_f[:, 1:2]).then_inc(slot_done, 1)
                wait_alone(dve, slot_done, t + 1)
                nc.vector.tensor_copy(slot[:, bass.ds(t, 1)], slot_f[:, 1:2]).then_inc(slot_kept, 1)
                wait_alone(dve, esum_done, t + 1)
                nc.vector.reciprocal(p_tok[:, bass.ds(t, 1)], esum[:]).then_inc(p_kept, 1)
                link.end()

            def mix(t, par, n):
                half = E // 2
                link = Chain(dve, mix_link, t, 2 * (half - 1), before=n * (half - 1))
                dve.wait_ge(doubled, t + 1)
                if n == 1:
                    dve.wait_ge(mixed, 2 * t + 1)
                dve.wait_ge(e_done, 2 * t + n + 1)
                for j in range(half):
                    e = n * half + j
                    ins = nc.vector.scalar_tensor_tensor(
                        out=acc[:, par, :], in0=ps[FILL[n]][:, j * P:(j + 1) * P],
                        scalar=onehot[:, e:e + 1], in1=acc[:, par, :], op0=ALU.mult, op1=ALU.add)
                    if j < half - 1:
                        link(ins)
                ins.then_inc(mixed, 1)

            def stats_routed(t, par):
                link = Chain(dve, ln2_link, t, 2)
                wait_alone(dve, mixed, 2 * t + 2)
                link(nc.vector.bn_stats(stats2[:], acc[:, par, :]), alone=True)
                after(dve, y_done, t)
                if not isinstance(t, int):
                    dve.nop(nofuse=True)
                link(nc.vector.bn_aggr(mv2[:], stats2[:]))
                nc.vector.tensor_scalar(ve2[:], mv2[:, 1:2], EPS, None, ALU.add).then_inc(var2_done, 1)
                link.end()

            def norm_routed(t, par):
                after(dve, y_stored[par], 8 * (t - par))
                dve.wait_ge(rstd2_done, t + 1)
                nc.vector.tensor_scalar(y[:, par, :], acc[:, par, :], mv2[:, 0:1], rstd2[:, 0:1],
                                        ALU.subtract, ALU.mult).then_inc(y_done, 1)

            dve.wait_ge(consts, n_consts)
            pipelined(dve, NB, steps(
                (5, of(mix, 1), "routed"), (2, of(maxima, 2)), (2, of(inverse, 1)),
                (2, of(copy_pt, 0)), (1, of(copy_v, 0)),
                (2, of(maxima, 3)), (2, of(inverse, 2)), (4, choose, "routed"),
                (4, choose_expert, "dispatch"), (2, of(copy_pt, 1)), (1, of(copy_v, 1)),
                (1, of(maxima, 0)), (2, of(inverse, 3)), (2, of(copy_pt, 2)),
                (5, stats_routed, "routed"), (3, residual),
                (4, of(mix, 0), "routed"), (4, read_ranks, "dispatch"),
                (1, of(maxima, 1)), (1, of(inverse, 0)), (3, norm), (5, norm_routed, "routed"),
                (2, of(copy_pt, 3)), (4, place_tokens, "dispatch")))
            dve.wait_ge(x_done, NB)
            if dispatch is not None:
                dve.wait_ge(slot_kept, NB)
                dve.wait_ge(p_kept, NB)




def experts_pass(nc, ps, w1_dram, w2_dram, ident, xe_dram, ye_dram):
    S = CAP // P
    C = F // P
    with ExitStack() as ctx:
        def sb(nm, shape, dt=F32):
            return ctx.enter_context(nc.sbuf_tensor("f_" + nm, shape, dt))

        def sem(nm):
            return nc.alloc_semaphore("f_" + nm)

        xe = sb("xe", [P, 2, S, P])
        w1 = sb("w1", [P, 2, F])
        w2 = sb("w2", [P, 2, C, P])
        xeT = sb("xeT", [P, 2, CAP])
        hT = sb("hT", [P, 2, C, CAP])
        ye = sb("ye", [P, S, P])
        xe_in = [sem("xe_in0"), sem("xe_in1")]
        w1_in = [sem("w1_in0"), sem("w1_in1")]
        w2_in = [sem("w2_in0"), sem("w2_in1")]
        t_done = sem("t_done")
        t_copied = sem("t_copied")
        h_done = sem("h_done")
        h_act = sem("h_act")
        h_dve = sem("h_dve")
        y_done = sem("y_done")
        y_copied = sem("y_copied")
        stored = sem("stored")
        TB, HB, YB = (0, 1), (2, 3, 4, 5), (6, 7)
        block = ctx.enter_context(nc.Block())

        @block.sync
        def _(sp):
            def load(t, par):
                after(sp, t_done, t - 1)
                sp.dma_start(xe[:, par], xe_dram[bass.ds(t * CAP, CAP)].rearrange("(s p) d -> p s d", p=P)
                             ).then_inc(xe_in[par], 16)
                after(sp, h_done, C * (t - 1))
                sp.dma_start(w1[:, par, :], w1_dram[t]).then_inc(w1_in[par], 16)

            def load_second(t, par):
                after(sp, y_done, t - 1)
                sp.dma_start(w2[:, par], w2_dram[t].rearrange("(c f) d -> f c d", f=P)
                             ).then_inc(w2_in[par], 16)

            def store(t, par):
                sp.wait_ge(y_copied, t + 1)
                sp.dma_start(ye_dram[bass.ds(t * CAP, CAP)].rearrange("(s p) d -> p s d", p=P), ye[:]
                             ).then_inc(stored, 16)

            pipelined(sp, E, ((0, load), (1, load_second), (3, store)))
            sp.wait_ge(stored, 16 * E)

        @block.tensor
        def _(pe):
            def turn_rows(t, par):
                pe.wait_ge(xe_in[par], 8 * (t - par) + 16)
                after(pe, t_copied, t - 1)
                for s in range(S):
                    last = nc.tensor.transpose(ps[TB[par]][:, s * P:(s + 1) * P], xe[:, par, s, :], ident[:])
                last.then_inc(t_done, 1)

            def first(t, par):
                pe.wait_ge(t_copied, t + 1)
                pe.wait_ge(w1_in[par], 8 * (t - par) + 16)
                for c in range(C):
                    after(pe, h_act if c % 2 == 0 else h_dve, (C // 2) * (t - 1) + c // 2 + 1)
                    nc.tensor.matmul(ps[HB[c]], w1[:, par, c * P:(c + 1) * P], xeT[:, par, :],
                                     start=True, stop=True).then_inc(h_done, 1)

            def second(t, par):
                pe.wait_ge(w2_in[par], 8 * (t - par) + 16)
                pe.wait_ge(h_act, (C // 2) * (t + 1))
                pe.wait_ge(h_dve, (C // 2) * (t + 1))
                after(pe, y_copied, t - 1)
                for s in range(S):
                    for c in range(C):
                        last = nc.tensor.matmul(ps[YB[par]][:, s * P:(s + 1) * P],
                                                hT[:, par, c, s * P:(s + 1) * P], w2[:, par, c, :],
                                                start=(c == 0), stop=(c == C - 1))
                last.then_inc(y_done, 1)

            pipelined(pe, E, ((0, turn_rows), (1, first), (2, second)))

        @block.scalar
        def _(act):
            def copy_rows(t, par):
                act.wait_ge(t_done, t + 1)
                after(act, h_done, C * (t - 1))
                nc.scalar.copy(xeT[:, par, :], ps[TB[par]]).then_inc(t_copied, 1)

            def even_relus(t, par):
                after(act, y_done, t - 1)
                for c in range(0, C, 2):
                    act.wait_ge(h_done, C * t + c + 1)
                    nc.scalar.activation(hT[:, par, c, :], ps[HB[c]], ACT.Relu).then_inc(h_act, 1)

            pipelined(act, E, ((0, copy_rows), (1, even_relus)))

        @block.vector
        def _(dve):
            def odd_relus(t, par):
                after(dve, y_done, t - 1)
                for c in range(1, C, 2):
                    dve.wait_ge(h_done, C * t + c + 1)
                    nc.vector.tensor_scalar(hT[:, par, c, :], ps[HB[c]], 0.0, None, ALU.max
                                            ).then_inc(h_dve, 1)

            def copy_out(t, par):
                after(dve, stored, 16 * t)
                dve.wait_ge(y_done, t + 1)
                nc.vector.tensor_copy(ye[:].rearrange("p s d -> p (s d)"), ps[YB[par]]
                                      ).then_inc(y_copied, 1)

            pipelined(dve, E, ((1, odd_relus), (2, copy_out)))




RH = 8
SEQ = NB


def relative_project_pass(nc, ps, w, ident, x_res, p_tok, slot, ye_dram, qT, x3_dram, pos_dram):
    G = 4
    TURNS = NB // G
    with ExitStack() as ctx:
        def sb(nm, shape, dt=F32):
            return ctx.enter_context(nc.sbuf_tensor("rp_" + nm, shape, dt))

        def sem(nm):
            return nc.alloc_semaphore("rp_" + nm)

        peT = sb("peT", [P, SEQ])
        wr = sb("wr", [P, RH * P])
        wqT = sb("wqT", [P, RH, P])
        v_wide = sb("v_wide", [P, RH, P])
        r = sb("r", [P, RH * SEQ])
        r_pad = sb("r_pad", [P, RH, 2 * SEQ])
        c_pad = sb("c_pad", [P, RH, 2 * SEQ])
        wq = sb("wq", [P, RH * P])
        chan = sb("chan", [P, 2 + RH])
        minus_half = sb("minus_half", [P, G])
        yg = sb("yg", [P, NB * P])
        res = sb("res", [P, G, P])
        stats = sb("stats", [P, G, 6])
        mv = sb("mv", [P, G, 2])
        ve = sb("ve", [P, G])
        rstd = sb("rstd", [P, G])
        x3 = sb("x3", [P, 2, G, P])
        stats2 = sb("stats2", [P, G, 6])
        mv2 = sb("mv2", [P, G, 2])
        ve2 = sb("ve2", [P, G])
        rstd2 = sb("rstd2", [P, G])
        hn = sb("hn", [P, G, P])
        hs = sb("hs", [P, 2, G * P])
        pos = sb("pos", [P, 2, G, RH * SEQ])

        weights_in = sem("weights_in")
        consts = sem("consts")
        gathered = [sem("gathered0"), sem("gathered1")]
        tables_in = sem("tables_in")
        chan_in = sem("chan_in")
        r_cleared = sem("r_cleared")
        r_made = sem("r_made")
        r_copied = sem("r_copied")
        pads_made = sem("pads_made")
        pads_copied = sem("pads_copied")
        res_link = sem("res_link")
        norm_link = sem("norm_link")
        var_done = sem("var_done")
        rstd_done = sem("rstd_done")
        x3_done = sem("x3_done")
        hn_done = sem("hn_done")
        t_done = sem("t_done")
        hs_done = sem("hs_done")
        h_kept = sem("h_kept")
        q_done = sem("q_done")
        q_kept = sem("q_kept")
        pos_done = sem("pos_done")
        pos_copied = sem("pos_copied")
        x3_stored = [sem("x3_stored0"), sem("x3_stored1")]
        pos_stored = [sem("pos_stored0"), sem("pos_stored1")]
        TB, QB, PB = 0, (1, 2, 3, 4), (5, 6)
        block = ctx.enter_context(nc.Block())

        def by_token(dram, t):
            return dram[:, bass.ds(G * t, G), :]

        @block.sync
        def _(sp):
            sp.dma_start(peT[:], w["r_peT"]).then_inc(tables_in, 16)
            sp.dma_start(chan[:], w["r_chan"]).then_inc(chan_in, 16)
            sp.dma_start(wr[:], w["r_wr"]).then_inc(tables_in, 16)
            sp.dma_start(wqT[:], w["r_qT"].rearrange("(h f) c -> f h c", f=P)).then_inc(weights_in, 16)
            sp.dma_start(wq[:], w["r_q"]).then_inc(weights_in, 16)

            def store_x3(t, par):
                sp.wait_ge(x3_done, t + 1)
                sp.dma_start(by_token(x3_dram, t), x3[:, par]).then_inc(x3_stored[par], 16)

            def store_pos(t, par):
                sp.wait_ge(pos_copied, 2 * t + 2)
                sp.dma_start(by_token(pos_dram, t), pos[:, par]).then_inc(pos_stored[par], 16)

            pipelined(sp, TURNS, ((0, store_x3), (2, store_pos)))
            for par in range(2):
                sp.wait_ge(x3_stored[par], 16 * TURNS // 2)
                sp.wait_ge(pos_stored[par], 16 * TURNS // 2)

        @block.gpsimd
        def _(pool):
            nc.gpsimd.memset(minus_half[:], -0.5).then_inc(consts, 1)
            pool.wait_ge(consts, 1)

            def gather(t, par):
                after(pool, gathered[par], 8 * G * (t - par))
                for b in range(G * t, G * t + G):
                    nc.gpsimd.indirect_dma_start(
                        out=yg[:, b * P:(b + 1) * P], out_offset=None, in_=ye_dram[:, :],
                        in_offset=bass.IndirectOffsetOnAxis(ap=slot[:, b:b + 1], axis=0),
                        bounds_check=TOKENS, oob_is_err=False).then_inc(gathered[par], 16)

            def rstds(t):
                pool.wait_ge(var_done, 2 * t + 1)
                nc.gpsimd.tensor_tensor(rstd[:], ve[:], minus_half[:], ALU.pow).then_inc(rstd_done, 1)
                pool.wait_ge(var_done, 2 * t + 2)
                nc.gpsimd.tensor_tensor(rstd2[:], ve2[:], minus_half[:], ALU.pow).then_inc(rstd_done, 1)

            gather(0, 0)
            gather(1, 1)
            for t in range(TURNS):
                rstds(t)
                if t + 2 < TURNS:
                    gather(t + 2, t % 2)

        @block.vector
        def _(dve):
            nc.vector.memset(r_pad[:], 0.0)
            nc.vector.memset(c_pad[:], 0.0)
            dve.wait_ge(chan_in, 16)
            nc.vector.tensor_copy(v_wide[:], chan[:, 2:2 + RH].unsqueeze(2).to_broadcast([P, RH, P])
                                  ).then_inc(r_cleared, 1)

            def residual(t, par):
                link = Chain(dve, res_link, t, 3)
                after(dve, hn_done, t)
                dve.wait_ge(gathered[par], 8 * G * (t - par) + 16 * G)
                if not isinstance(t, int):
                    dve.nop(nofuse=True)
                for j in range(G):
                    last = nc.vector.scalar_tensor_tensor(
                        out=res[:, j, :], in0=yg[:, bass.ds((G * t + j) * P, P)],
                        scalar=p_tok[:, bass.ds(G * t + j, 1)],
                        in1=x_res[:, bass.ds((G * t + j) * P, P)], op0=ALU.mult, op1=ALU.add)
                link(last)
                for j in range(G):
                    last = nc.vector.bn_stats(stats[:, j, :], res[:, j, :])
                link(last, alone=True)
                for j in range(G):
                    last = nc.vector.bn_aggr(mv[:, j, :], stats[:, j, :])
                link(last)
                nc.vector.tensor_scalar(ve[:], mv[:, :, 1], EPS, None, ALU.add).then_inc(var_done, 1)
                link.end()

            def residual_norm(t, par):
                link = Chain(dve, norm_link, t, 2)
                after(dve, x3_stored[par], 8 * (t - par))
                dve.wait_ge(rstd_done, 2 * t + 1)
                for j in range(G):
                    last = nc.vector.tensor_scalar(x3[:, par, j, :], res[:, j, :], mv[:, j, 0:1],
                                                   rstd[:, j:j + 1], ALU.subtract, ALU.mult)
                last.then_inc(x3_done, 1)
                dve.wait_ge(x3_done, t + 1)
                for j in range(G):
                    last = nc.vector.bn_stats(stats2[:, j, :], x3[:, par, j, :])
                link(last, alone=True)
                for j in range(G):
                    last = nc.vector.bn_aggr(mv2[:, j, :], stats2[:, j, :])
                link(last)
                nc.vector.tensor_scalar(ve2[:], mv2[:, :, 1], EPS, None, ALU.add).then_inc(var_done, 1)
                link.end()

            def second_norm(t, par):
                after(dve, t_done, t)
                dve.wait_ge(rstd_done, 2 * t + 2)
                for j in range(G):
                    last = nc.vector.tensor_scalar(hn[:, j, :], x3[:, par, j, :], mv2[:, j, 0:1],
                                                   rstd2[:, j:j + 1], ALU.subtract, ALU.mult)
                last.then_inc(hn_done, 1)

            def finish_pos(t, par, n):
                if isinstance(t, int) and t == 0 and n == 0:
                    dve.wait_ge(pads_copied, 2)
                if n == 0:
                    after(dve, pos_stored[par], 8 * (t - par))
                dve.wait_ge(pos_done, 2 * t + n + 1)
                if not isinstance(t, int):
                    dve.nop(nofuse=True)
                for j in (2 * n, 2 * n + 1):
                    last = nc.vector.tensor_tensor(
                        pos[:, par, j, :].rearrange("r (h n) -> r h n", h=RH),
                        ps[PB[n]][:, (j % 2) * RH * SEQ:(j % 2 + 1) * RH * SEQ]
                        .rearrange("r (h n) -> r h n", h=RH),
                        c_pad[:, :, bass.ds(SEQ - 1 - G * t - j, SEQ)], ALU.add)
                last.then_inc(pos_copied, 1)

            pipelined(dve, TURNS, ((0, residual), (0, residual_norm), (0, second_norm),
                                   (2, of(finish_pos, 0)), (2, of(finish_pos, 1))))

        @block.tensor
        def _(pe):
            pe.wait_ge(tables_in, 32)
            for h in range(RH):
                last = nc.tensor.matmul(ps[7][:, h * SEQ:(h + 1) * SEQ], wr[:, h * P:(h + 1) * P],
                                        peT[:], start=True, stop=True)
            last.then_inc(r_made, 1)
            pe.wait_ge(weights_in, 32)
            pe.wait_ge(r_cleared, 1)
            pe.wait_ge(r_copied, 1)
            for h in range(RH):
                cols = slice(h * SEQ, (h + 1) * SEQ)
                nc.tensor.matmul(ps[6][:, cols], wqT[:, h, :], r[:, cols], start=True, stop=True)
                last = nc.tensor.matmul(ps[5][:, cols], v_wide[:, h, :], r[:, cols],
                                        start=True, stop=True)
            last.then_inc(pads_made, 1)
            pe.wait_ge(pads_copied, 2)

            def transposes(t, par):
                after(pe, hs_done, t)
                pe.wait_ge(hn_done, t + 1)
                for j in range(G):
                    last = nc.tensor.transpose(ps[TB][:, j * P:(j + 1) * P], hn[:, j, :], ident[:])
                last.then_inc(t_done, 1)

            def queries(t, par):
                pe.wait_ge(hs_done, t + 1)
                for h in range(RH):
                    after(pe, q_kept, RH * t + h - 3)
                    nc.tensor.matmul(ps[QB[h % 4]], wq[:, h * P:(h + 1) * P], hs[:, par, :],
                                     start=True, stop=True).then_inc(q_done, 1)

            def positions(t, par, n):
                after(pe, pos_copied, 2 * t - 1 + n)
                if not isinstance(t, int):
                    pe.nop(nofuse=True)
                for j in (2 * n, 2 * n + 1):
                    bank = ps[PB[n]][:, (j % 2) * RH * SEQ:(j % 2 + 1) * RH * SEQ]
                    last = nc.tensor.matmul(bank.rearrange("r (h n) -> r h n", h=RH),
                                            hs[:, par, j * P:(j + 1) * P],
                                            r_pad[:, :, bass.ds(SEQ - 1 - G * t - j, SEQ)],
                                            start=True, stop=True)
                last.then_inc(pos_done, 1)

            pipelined(pe, TURNS, ((2, queries), (1, transposes), (2, of(positions, 0)),
                                  (2, of(positions, 1))))

        @block.scalar
        def _(act):
            act.wait_ge(chan_in, 16)
            act.wait_ge(r_made, 1)
            nc.scalar.copy(r[:], ps[7][:, 0:RH * SEQ]).then_inc(r_copied, 1)
            act.wait_ge(r_cleared, 1)
            act.wait_ge(pads_made, 1)
            for pad, bank in ((r_pad, 6), (c_pad, 5)):
                nc.scalar.copy(pad[:, :, 0:SEQ],
                               ps[bank][:, 0:RH * SEQ].rearrange("p (h n) -> p h n", h=RH)
                               ).then_inc(pads_copied, 1)


            def scale_h(t, par):
                after(act, q_done, RH * (t - 1))
                after(act, pos_done, 2 * t - 2)
                after(act, h_kept, t - 1)
                act.wait_ge(t_done, t + 1)
                nc.scalar.activation(hs[:, par, :], ps[TB], ACT.Identity,
                                     scale=chan[:, 0:1], bias=chan[:, 1:2]).then_inc(hs_done, 1)
                wait_alone(act, hs_done, t + 1)
                nc.scalar.copy(x_res[:, bass.ds(t * G * P, G * P)], hs[:, par, :]).then_inc(h_kept, 1)

            def keep_q(t, par):
                for h in range(RH):
                    wait_alone(act, q_done, RH * t + h + 1)
                    by_position = qT[:, h, :].rearrange("f (p i) -> f i p", i=NB)
                    nc.scalar.copy(by_position[:, bass.ds(G * t, G), :],
                                   ps[QB[h % 4]].rearrange("f (i p) -> f i p", i=G)).then_inc(q_kept, 1)

            pipelined(act, TURNS, ((2, keep_q), (1, scale_h)))
            act.wait_ge(q_kept, RH * TURNS)
            act.wait_ge(h_kept, TURNS)


def relative_attention_pass(nc, ps2s, ps, w, hT, qT, x3_dram, pos_dram, x4_dram):
    POS = 4
    TURNS = P // POS
    with ExitStack() as ctx:
        def sb(nm, shape, dt=F32):
            return ctx.enter_context(nc.sbuf_tensor("ra_" + nm, shape, dt))

        def sem(nm):
            return nc.alloc_semaphore("ra_" + nm)

        wvT = sb("wvT", [P, RH, P])
        wo = sb("wo", [P, RH, P])
        wvo = sb("wvo", [P, RH * P])
        u_bias = sb("u_bias", [P, RH])
        b_out = sb("b_out", [P, P])
        minus_half = sb("minus_half", [P, 1])
        hst = sb("hst", [P, 2, P])
        qu = sb("qu", [P, 2, RH, P])
        v = sb("v", [P, 2, RH * P])
        pos = sb("pos", [P, 2, RH * SEQ])
        s = sb("s", [P, 2, RH, SEQ])
        nmax = sb("nmax", [P, 2, RH])
        rsum = sb("rsum", [P, 2, RH])
        rinv = sb("rinv", [P, 2, RH])
        pTb = sb("pTb", [P, 2, RH, P])
        xr = sb("xr", [P, 2, P])
        res = sb("res", [P, P])
        stats = sb("stats", [P, 6])
        mv = sb("mv", [P, 2])
        ve = sb("ve", [P, 1])
        rstd = sb("rstd", [P, 1])
        x4 = sb("x4", [P, 2, P])

        weights_in = sem("weights_in")
        u_in = sem("u_in")
        b_in = sem("b_in")
        cleared = sem("cleared")
        consts = sem("consts")
        pos_in = [sem("pos_in0"), sem("pos_in1")]
        xr_in = [sem("xr_in0"), sem("xr_in1")]
        h_staged = sem("h_staged")
        qu_done = sem("qu_done")
        v_done = sem("v_done")
        v_copied = sem("v_copied")
        c_done = sem("c_done")
        s_done = sem("s_done")
        max_done = sem("max_done")
        sub_done = sem("sub_done")
        exp_done = sem("exp_done")
        rinv_done = sem("rinv_done")
        probs_done = sem("probs_done")
        pt_done = sem("pt_done")
        o_done = sem("o_done")
        fold_done = sem("fold_done")
        fold_copied = sem("fold_copied")
        bout_done = sem("bout_done")
        res_done = sem("res_done")
        var_done = sem("var_done")
        rstd_done = sem("rstd_done")
        x4_done = sem("x4_done")
        stored = [sem("stored0"), sem("stored1")]
        soft_link = sem("soft_link")
        norm_link = sem("norm_link")
        VB, PB = (0, 1), (6, 7)
        SCALE = float(P) ** -0.5
        block = ctx.enter_context(nc.Block())

        @block.sync
        def _(sp):
            sp.dma_start(u_bias[:], w["r_uT"]).then_inc(u_in, 16)
            sp.dma_start(wvT[:], w["r_vT"].rearrange("(h f) d -> f h d", f=P)).then_inc(weights_in, 16)
            sp.dma_start(wo[:], w["r_out"].rearrange("(h f) d -> f h d", f=P)).then_inc(weights_in, 16)
            sp.dma_start(b_out[:], w["r_bout"].to_broadcast([P, P])).then_inc(b_in, 16)

            def tile_rows(dram, t):
                return dram.rearrange("p i c -> (p i) c")[bass.ds(t * P, P), :]

            def load_pos(t, par):
                after(sp, s_done, t - 1)
                sp.dma_start(pos[:, par, :], tile_rows(pos_dram, t)).then_inc(pos_in[par], 16)

            def load_xr(t, par):
                after(sp, res_done, t - 1)
                sp.dma_start(xr[:, par, :], tile_rows(x3_dram, t)).then_inc(xr_in[par], 16)

            def store(t, par):
                sp.wait_ge(x4_done, t + 1)
                sp.dma_start(tile_rows(x4_dram, t), x4[:, par, :]).then_inc(stored[par], 16)

            pipelined(sp, TURNS, ((0, load_pos), (1, load_xr), (3, store)))
            for par in range(2):
                sp.wait_ge(stored[par], 16 * TURNS // 2)

        @block.gpsimd
        def _(pool):
            nc.gpsimd.memset(minus_half[:], -0.5).then_inc(consts, 1)
            pool.wait_ge(u_in, 16)
            pool.wait_ge(consts, 1)

            def stage(t, par):
                after(pool, c_done, t - 1)
                if not isinstance(t, int):
                    pool.nop(nofuse=True)
                nc.gpsimd.tensor_tensor(qu[:, par], qT[:, :, bass.ds(t * P, P)],
                                        u_bias[:].unsqueeze(2).to_broadcast([P, RH, P]),
                                        ALU.add).then_inc(qu_done, 1)

            def subtract_max(t, par):
                pool.wait_ge(max_done, t + 1)
                nc.gpsimd.tensor_tensor(s[:, par], s[:, par],
                                        nmax[:, par].unsqueeze(2).to_broadcast([P, RH, SEQ]),
                                        ALU.add).then_inc(sub_done, 1)

            def scale_probs(t, par):
                pool.wait_ge(rinv_done, t + 1)
                nc.gpsimd.tensor_tensor(s[:, par], s[:, par],
                                        rinv[:, par].unsqueeze(2).to_broadcast([P, RH, SEQ]),
                                        ALU.mult).then_inc(probs_done, 1)

            def add_bias(t, par):
                if isinstance(t, int) and t == 0:
                    pool.wait_ge(b_in, 16)
                pool.wait_ge(xr_in[par], 8 * (t - par) + 16)
                nc.gpsimd.tensor_tensor(xr[:, par, :], xr[:, par, :], b_out[:], ALU.add
                                        ).then_inc(bout_done, 1)

            def power(t, par):
                pool.wait_ge(var_done, t + 1)
                nc.gpsimd.tensor_tensor(rstd[:], ve[:], minus_half[:], ALU.pow).then_inc(rstd_done, 1)

            pipelined(pool, TURNS, ((0, stage), (1, subtract_max), (3, power), (1, scale_probs),
                                    (2, add_bias)))

        @block.tensor
        def _(pe):
            def fold():
                pe.wait_ge(weights_in, 32)
                for h in range(RH):
                    last = nc.tensor.matmul(ps[VB[h // 4]][:, (h % 4) * P:(h % 4 + 1) * P],
                                            wvT[:, h, :], wo[:, h, :], start=True, stop=True)
                last.then_inc(fold_done, 1)
                pe.wait_ge(fold_copied, 2)

            def scores(t, par):
                after(pe, s_done, t - 1)
                wait_alone(pe, qu_done, t + 1)
                for h in range(RH):
                    last = nc.tensor.matmul(ps2s[par][:, h * P:(h + 1) * P], qu[:, par, h, :],
                                            qT[:, h, bass.ds(t * P, P)], start=True, stop=True)
                last.then_inc(c_done, 1)

            def values(t, par):
                if isinstance(t, int) and t == 0:
                    fold()
                pe.wait_ge(h_staged, t + 1)
                for n in range(2):
                    after(pe, v_copied, 2 * t - 1 + n)
                    nc.tensor.matmul(ps[VB[n]], hst[:, par, :], wvo[:, n * BANK:(n + 1) * BANK],
                                     start=True, stop=True).then_inc(v_done, 1)

            def output(t, par):
                after(pe, res_done, t - 1)
                pe.wait_ge(v_copied, 2 * t + 2)
                pe.wait_ge(pt_done, t + 1)
                for h in range(RH):
                    last = nc.tensor.matmul(ps[PB[par]][:, 0:P], pTb[:, par, h, :],
                                            v[:, par, h * P:(h + 1) * P],
                                            start=(h == 0), stop=(h == RH - 1))
                last.then_inc(o_done, 1)

            pipelined(pe, TURNS, ((0, scores), (2, output), (0, values)))

        @block.scalar
        def _(act):
            def keep_fold():
                act.wait_ge(fold_done, 1)
                for n in range(2):
                    nc.scalar.copy(wvo[:, n * BANK:(n + 1) * BANK], ps[VB[n]]).then_inc(fold_copied, 1)

            def stage_h(t, par):
                after(act, v_done, 2 * t - 2)
                if not isinstance(t, int):
                    act.nop(nofuse=True)
                nc.scalar.copy(hst[:, par, :].rearrange("f (p i) -> f p i", p=POS),
                               hT.rearrange("f (i p) -> f p i", p=P)[:, bass.ds(t * POS, POS), :]
                               ).then_inc(h_staged, 1)

            def keep_v(t, par):
                if isinstance(t, int) and t == 0:
                    keep_fold()
                after(act, o_done, t - 1)
                for n in range(2):
                    act.wait_ge(v_done, 2 * t + n + 1)
                    nc.scalar.copy(v[:, par, n * BANK:(n + 1) * BANK], ps[VB[n]]).then_inc(v_copied, 1)

            def exponent(t, par):
                act.wait_ge(sub_done, t + 1)
                nc.scalar.activation(s[:, par], s[:, par], ACT.Exp, scale=SCALE).then_inc(exp_done, 1)

            pipelined(act, TURNS, ((0, stage_h), (1, keep_v), (1, exponent)))

        @block.vector
        def _(dve):
            nc.vector.memset(pTb[:], 0.0).then_inc(cleared, 1)
            dve.wait_ge(cleared, 1)

            def masked_max(t, par):
                after(dve, pt_done, t - 1)
                dve.wait_ge(pos_in[par], 8 * (t - par) + 16)
                dve.wait_ge(c_done, t + 1)
                blocks = ps2s[par].rearrange("r (h c) -> r h c", h=RH)
                for p in range(POS):
                    rows = slice(p * SEQ, (p + 1) * SEQ)
                    last = nc.vector.tensor_tensor(
                        s[rows, par], blocks[rows, :, rows],
                        pos[rows, par, :].rearrange("r (h j) -> r h j", h=RH), ALU.add)
                last.then_inc(s_done, 1)
                dve.wait_ge(s_done, t + 1)
                nc.vector.tensor_reduce(nmax[:, par], s[:, par], AX.X, ALU.max, negate=True).then_inc(max_done, 1)

            def probabilities(t, par):
                link = Chain(dve, soft_link, t, 1)
                dve.wait_ge(exp_done, t + 1)
                link(nc.vector.tensor_reduce(rsum[:, par], s[:, par], AX.X, ALU.add))
                nc.vector.reciprocal(rinv[:, par], rsum[:, par]).then_inc(rinv_done, 1)
                link.end()

            def turn_probs(t, par):
                after(dve, o_done, t - 1)
                dve.wait_ge(probs_done, t + 1)
                for p in range(POS):
                    rows = slice(p * SEQ, (p + 1) * SEQ)
                    last = nc.vector.transpose(pTb[rows, par, :, rows], s[rows, par])
                last.then_inc(pt_done, 1)

            def residual(t, par):
                link = Chain(dve, norm_link, t, 2)
                dve.wait_ge(o_done, t + 1)
                dve.wait_ge(bout_done, t + 1)
                after(dve, x4_done, t)
                nc.vector.tensor_tensor(res[:], ps[PB[par]][:, 0:P], xr[:, par, :], ALU.add
                                        ).then_inc(res_done, 1)
                dve.wait_ge(res_done, t + 1)
                link(nc.vector.bn_stats(stats[:], res[:]), alone=True)
                link(nc.vector.bn_aggr(mv[:], stats[:]))
                nc.vector.tensor_scalar(ve[:], mv[:, 1:2], EPS, None, ALU.add).then_inc(var_done, 1)
                link.end()

            def norm(t, par):
                after(dve, stored[par], 8 * (t - par))
                dve.wait_ge(rstd_done, t + 1)
                nc.vector.tensor_scalar(x4[:, par, :], res[:], mv[:, 0:1], rstd[:, 0:1],
                                        ALU.subtract, ALU.mult).then_inc(x4_done, 1)

            pipelined(dve, TURNS, ((0, masked_max), (1, turn_probs), (2, residual),
                                   (0, probabilities), (2, norm)))




def build(nc, a, out):
    def scratch(name, shape):
        return nc.dram_tensor(name, shape, F32, kind="Internal").ap()

    x1_dram = scratch("x1_scratch", (NB, P, P))
    x3_dram = scratch("x3_scratch", (P, NB, P))
    x4_dram = scratch("x4_scratch", (P, NB, P))
    xe_dram = scratch("xe_scratch", (TOKENS, P))
    ye_dram = scratch("ye_scratch", (TOKENS + 1, P))
    pos_dram = scratch("pos_scratch", (P, NB, RH * SEQ))
    with ExitStack() as ctx:
        banks = ctx.enter_context(nc.psum_tensor("banks", [P, 8 * BANK], F32))
        ps = [banks[:, i * BANK:(i + 1) * BANK] for i in range(8)]
        ident = ctx.enter_context(nc.sbuf_tensor("ident", [P, P], F32))
        x_res = ctx.enter_context(nc.sbuf_tensor("x_res", [P, NB * P], F32))
        p_tok = ctx.enter_context(nc.sbuf_tensor("p_tok", [P, NB], F32))
        slot = ctx.enter_context(nc.sbuf_tensor("slot", [P, NB], U32))
        ident_made = ctx.enter_context(nc.semaphore("ident_made"))
        with nc.Block() as block:
            @block.gpsimd
            def _(pool):
                make_identity(nc, pool, ident, ident_made)
                pool.wait_ge(ident_made, 2)

        def keep_x(t, par):
            return x_res[:, bass.ds(t * P, P)]

        with nc.cleanup_on_exit():
            mamba_pass(nc, banks, ps, {"x": a["x"], "xT": a["xT"]}, a, x1_dram)
            cross_attention_pass(nc, ps, "xa0", x1_dram, a["ctxT"], {n: a["x0_" + n] for n in "qkvo"},
                                 P ** -0.5, a["bias"], ident, keep_x,
                                 dispatch=(a["wr"], p_tok, slot, xe_dram, ye_dram))
        with nc.cleanup_on_exit():
            experts_pass(nc, ps, a["w1"], a["w2"], ident, xe_dram, ye_dram)
            with nc.sbuf_tensor("qT", [P, RH, TOKENS], F32) as qT:
                relative_project_pass(nc, ps, a, ident, x_res, p_tok, slot, ye_dram, qT, x3_dram,
                                      pos_dram)
                relative_attention_pass(nc, [banks[:, i * BANK:(i + 2) * BANK] for i in (2, 4)], ps, a,
                                        x_res[:], qT, x3_dram, pos_dram, x4_dram)
        with nc.cleanup_on_exit():
            cross_attention_pass(nc, ps, "xa1", x4_dram.rearrange("p i c -> i p c"), a["ctxT"],
                                 {n: a["x1_" + n] for n in "qkvo"}, DH ** -0.5, None, ident, None,
                                 routed=(a["gateT"], a["wexpT"], out))


def distance_table():
    pos = np.arange(SEQ, dtype=np.float32)[:, None]
    div = np.exp(np.arange(0, P, 2, dtype=np.float32) * np.float32(-math.log(10000.0) / P))
    ang = pos * div
    return np.stack([np.sin(ang), np.cos(ang)], axis=-1).reshape(SEQ, P)[::-1].T


def layout(inp):
    a = {k: np.asarray(v) for k, v in inp.items()}
    return {
        "x": a["x"], "xT": a["x"].reshape(TOKENS, P).T, "ctxT": a["ctx_1024"].reshape(TOKENS, P).T,
        "bias": a["fside_1x1xSxS2_0"].reshape(P, P),
        "W_inT": a["L0_attn_W_in"].T, "W_x": a["L0_attn_W_x"], "W_dtT": a["L0_attn_W_dt"].T,
        "W_outT": a["L0_attn_W_out"].T,
        "per_channel": np.concatenate(
            [a["L0_attn_conv_w"].reshape(2 * P, 4), a["L0_attn_conv_b"][:, None],
             a["L0_attn_b_dt"][:, None], a["L0_attn_D"][:, None]], axis=1),
        "x0_q": a["L0_xattn_Wq"].T, "x0_k": a["L0_xattn_Wk"].T, "x0_v": a["L0_xattn_Wv"].T,
        "x0_o": a["L0_xattn_Wp"].T,
        "wr": a["L0_ffn_Wr"], "w1": a["L0_ffn_W1"], "w2": a["L0_ffn_W2"],
        "r_q": a["L1_attn_Wq"], "r_qT": a["L1_attn_Wq"].T, "r_vT": a["L1_attn_Wv"].T, "r_wr": a["L1_attn_Wr"],
        "r_peT": distance_table(), "r_uT": a["L1_attn_u_bias"].T,
        "r_chan": np.concatenate([a["L1_attn_gamma"][:, None], a["L1_attn_beta"][:, None],
                                  a["L1_attn_v_bias"].T], axis=1),
        "r_bout": a["L1_attn_bout"].reshape(1, P), "r_out": a["L1_attn_Wout"],
        "x1_q": a["L1_xattn_w_q"], "x1_k": a["L1_xattn_w_k"], "x1_v": a["L1_xattn_w_v"],
        "x1_o": a["L1_xattn_w_o"],
        "gateT": a["L1_ffn_gate_w"].T,
        "wexpT": a["L1_ffn_expert_w"].transpose(2, 0, 1).reshape(P, E * P),
    }


def kernel(**inputs):
    import concourse.bacc as _bacc
    from concourse.bass_utils import run_bass_kernel_spmd as _run

    nc = _bacc.Bacc("TRN2", target_bir_lowering=False, num_devices=1)
    arrays, args = {}, {}

    def give(name, a):
        a = np.ascontiguousarray(a)
        arrays["in_" + name] = a
        args[name] = nc.dram_tensor("in_" + name, a.shape, mybir.dt.from_np(a.dtype),
                                    kind="ExternalInput").ap()

    for name, a in layout(inputs).items():
        give(name, a)
    out = nc.dram_tensor("out_0_dram", (NB, P, P), F32, kind="ExternalOutput").ap()
    build(nc, args, out)
    r = _run(nc, [arrays], core_ids=[0])
    return r.results[0]["out_0_dram"]
```
